# Optimizing a Trainium2 kernel written in Bass

```python
import numpy as np
import jax
import jax.numpy as jnp

def _softmax(x, axis=-1):
    return jax.nn.softmax(x, axis=axis)

def _gelu(x):
    return jax.nn.gelu(x, approximate=True)

def _silu(x):
    return jax.nn.silu(x)

def _sigmoid(x):
    return jax.nn.sigmoid(x)

def _layernorm(x, axis=-1, eps=1e-05):
    m = jnp.mean(x, axis=axis, keepdims=True)
    v = jnp.var(x, axis=axis, keepdims=True)
    return (x - m) / jnp.sqrt(v + eps)

def _scatter_add(tgt, idx, src, axis=0):
    return tgt.at[idx].add(src)

def _segment_sum(src, seg, n):
    return jax.ops.segment_sum(src, seg, n)
kernel_name = 'mk_perceiver_d2_seqx_r4_ff3694'

def setup_inputs(seed: int=0):
    np.random.seed(seed)
    _w = jnp.asarray

    def _rec_inputs():
        import jax
        import jax.numpy as jnp
        _rk = jax.random.key(seed)
        x = -0.0005207 + 1.001 * jax.random.normal(jax.random.fold_in(_rk, 1), (16, 64, 256), jnp.float32)
        _lenS = 64 - jax.random.randint(jax.random.fold_in(_rk, 7), (16,), 0, max(1, 64 // 4) + 1, jnp.int32)
        _lenS2 = 256 - jax.random.randint(jax.random.fold_in(_rk, 8), (16,), 0, max(1, 256 // 4) + 1, jnp.int32)
        _ctx_1024P = jax.random.normal(jax.random.fold_in(_rk, 11), (16, 16, 256), jnp.float32)
        _ctx_1024c = jax.random.dirichlet(jax.random.fold_in(_rk, 511), 0.3 * jnp.ones((16,), jnp.float32), (16, 256))
        _ctx_1024t = jnp.einsum('bsk,bkd->bsd', _ctx_1024c, _ctx_1024P)
        _ctx_1024t = _ctx_1024t * jax.lax.rsqrt(jnp.mean(jnp.square(_ctx_1024t)) + 1e-12) * 0.953939
        ctx_1024 = 4.13588e-05 + 0.999923 * (_ctx_1024t + 0.3 * jax.random.normal(jax.random.fold_in(_rk, 611), (16, 256, 256), jnp.float32))
        _validS = jnp.arange(64)[None, :] < _lenS[:, None]
        _validS2 = jnp.arange(256)[None, :] < _lenS2[:, None]
        _causal = jnp.tril(jnp.ones((64, 64), dtype=bool))
        mask_BxS2_bf1 = jnp.ones((16, 256), dtype=bool)
        mask_BxS2_bk0 = jnp.logical_not(jnp.broadcast_to(_validS2[:, :], (16, 256)))
        return (x, ctx_1024, mask_BxS2_bf1, mask_BxS2_bk0)
    x, ctx_1024, mask_BxS2_bf1, mask_BxS2_bk0 = _rec_inputs()

    def _L0_xattn_setup():
        import jax, jax.numpy as jnp
        import numpy as np
        HIDDEN = 256
        HEADS = 16
        HEAD_DIM = HIDDEN // HEADS
        key = jax.random.key(seed)
        ks = jax.random.split(key, 8)
        B, Q, KV = (4, 128, 512)
        s = 1.0 / np.sqrt(HIDDEN)
        return {'query': jax.random.normal(ks[0], (B, Q, HIDDEN), dtype=jnp.float32), 'key_value': jax.random.normal(ks[1], (B, KV, HIDDEN), dtype=jnp.float32), 'mask': jnp.ones((B, KV), dtype=bool), 'Wq': jax.random.normal(ks[2], (HIDDEN, HIDDEN), dtype=jnp.float32) * s, 'Wk': jax.random.normal(ks[3], (HIDDEN, HIDDEN), dtype=jnp.float32) * s, 'Wv': jax.random.normal(ks[4], (HIDDEN, HIDDEN), dtype=jnp.float32) * s, 'Wo': jax.random.normal(ks[5], (HIDDEN, HIDDEN), dtype=jnp.float32) * s, 'bo': jnp.zeros((HIDDEN,), dtype=jnp.float32)}
    _L0_xattn_all = _L0_xattn_setup()
    _L0_xattn_in = {k: v for k, v in _L0_xattn_all.items() if k in ('Wq', 'Wk', 'Wv', 'Wo', 'bo')}
    del _L0_xattn_all

    def _L0_attn_setup():
        import jax, jax.numpy as jnp
        import numpy as np
        HEADS, HEAD_SIZE, FREQS, MAX_PERIOD = (16, 64, 64, 2500)
        D_MODEL = 256
        NEG_INF = -1000000000.0

        def sinusoid_embedding(seq_len, frequencies, max_period):
            pos = np.arange(seq_len, dtype=np.float64)[:, None]
            idx = np.arange(frequencies)[None, :]
            inv_freq = max_period ** (-(idx // 2 * 2) / frequencies)
            angle = pos * inv_freq
            table = np.where(idx % 2 == 0, np.sin(angle), np.cos(angle))
            return table.astype(np.float32)

        def relative_causal(scores):
            L = scores.shape[-1]
            d = jnp.clip(jnp.arange(L)[:, None] - jnp.arange(L)[None, :], 0, L - 1)
            return jnp.take_along_axis(scores, d[None, None, :, :], axis=-1)
        key = jax.random.key(seed)
        ks = jax.random.split(key, 4)
        u = np.sqrt(3.0)
        inp = jax.random.normal(ks[0], (2, 512, D_MODEL), dtype=jnp.float32)
        qkv = jax.random.uniform(ks[1], (D_MODEL, 3, HEADS, HEAD_SIZE), jnp.float32, -u, u)
        q_bias = jnp.zeros((HEADS, HEAD_SIZE), jnp.float32)
        positional = jax.random.uniform(ks[2], (FREQS, HEADS, HEAD_SIZE), jnp.float32, -u, u)
        out_kernel = jax.random.uniform(ks[3], (HEADS * HEAD_SIZE, D_MODEL), jnp.float32, -u, u)
        out_bias = jnp.zeros((D_MODEL,), jnp.float32)
        return {'input': inp, 'qkv': qkv, 'q_bias': q_bias, 'positional': positional, 'out_kernel': out_kernel, 'out_bias': out_bias}
    _L0_attn_all = _L0_attn_setup()
    _L0_attn_in = {k: v for k, v in _L0_attn_all.items() if k in ('qkv', 'q_bias', 'positional', 'out_kernel', 'out_bias')}
    del _L0_attn_all

    def _L0_ffn_setup():
        import jax, jax.numpy as jnp
        import numpy as np
        LN_EPS = 1e-05

        def layernorm(x, g, b):
            mu = jnp.mean(x, axis=-1, keepdims=True)
            var = jnp.mean((x - mu) ** 2, axis=-1, keepdims=True)
            return (x - mu) * jax.lax.rsqrt(var + LN_EPS) * g + b

        def act_quant_fake(x):
            scale = 127.0 / jnp.clip(jnp.max(jnp.abs(x), axis=-1, keepdims=True), 1e-05)
            return jnp.clip(jnp.round(x * scale), -128.0, 127.0) / scale

        def weight_quant_fake(w):
            scale = 1.0 / jnp.clip(jnp.mean(jnp.abs(w)), 1e-05)
            return jnp.clip(jnp.round(w * scale), -1.0, 1.0) / scale

        def bitlinear(x, w, b):
            dqx = act_quant_fake(x)
            dqw = weight_quant_fake(w)
            return jnp.einsum('btd,hd->bth', dqx, dqw) + b
        key = jax.random.key(seed)
        ks = jax.random.split(key, 5)
        B, T, D, H = (8, 1024, 256, 1024)
        return {'x': jax.random.normal(ks[0], (B, T, D), dtype=jnp.float32), 'ln1_g': jnp.ones((D,), jnp.float32), 'ln1_b': jnp.zeros((D,), jnp.float32), 'w1': jax.random.normal(ks[1], (H, D), dtype=jnp.float32) * (1.0 / np.sqrt(D)), 'b1': jax.random.normal(ks[2], (H,), dtype=jnp.float32) * 0.02, 'ln2_g': jnp.ones((H,), jnp.float32), 'ln2_b': jnp.zeros((H,), jnp.float32), 'w2': jax.random.normal(ks[3], (D, H), dtype=jnp.float32) * (1.0 / np.sqrt(H)), 'b2': jax.random.normal(ks[4], (D,), jnp.float32) * 0.02}
    _L0_ffn_all = _L0_ffn_setup()
    _L0_ffn_in = {k: v for k, v in _L0_ffn_all.items() if k in ('ln1_g', 'ln1_b', 'w1', 'b1', 'ln2_g', 'ln2_b', 'w2', 'b2')}
    del _L0_ffn_all

    def _L1_xattn_setup():
        import jax, jax.numpy as jnp
        import numpy as np
        D_Q, D_KV, N_HEADS = (256, 256, 16)
        HEAD_DIM = D_Q // N_HEADS
        SCALE = HEAD_DIM ** (-0.5)
        key = jax.random.key(seed)
        ks = jax.random.split(key, 12)
        B, Sq, Skv = (4, 256, 512)
        q = jax.random.normal(ks[0], (B, Sq, D_Q), jnp.float32)
        kv = jax.random.normal(ks[1], (B, Skv, D_KV), jnp.float32)
        pad_mask = jax.random.randint(ks[2], (B, Skv), 0, 2) > 0
        s = 0.02
        Wq = jax.random.normal(ks[3], (D_Q, D_Q), jnp.float32) * s
        bq = jnp.zeros((D_Q,), jnp.float32)
        Wk = jax.random.normal(ks[4], (D_KV, D_Q), jnp.float32) * s
        bk = jnp.zeros((D_Q,), jnp.float32)
        Wv = jax.random.normal(ks[5], (D_KV, D_Q), jnp.float32) * s
        bv = jnp.zeros((D_Q,), jnp.float32)
        Wo = jax.random.normal(ks[6], (D_Q, D_Q), jnp.float32) * s
        bo = jnp.zeros((D_Q,), jnp.float32)
        return {'q': q, 'kv': kv, 'pad_mask': pad_mask, 'Wq': Wq, 'bq': bq, 'Wk': Wk, 'bk': bk, 'Wv': Wv, 'bv': bv, 'Wo': Wo, 'bo': bo}
    _L1_xattn_all = _L1_xattn_setup()
    _L1_xattn_in = {k: v for k, v in _L1_xattn_all.items() if k in ('Wq', 'bq', 'Wk', 'bk', 'Wv', 'bv', 'Wo', 'bo')}
    del _L1_xattn_all

    def _L1_attn_setup():
        import jax, jax.numpy as jnp
        import numpy as np
        B, S, H, NH = (4, 256, 256, 16)
        HD = H // NH
        CAUSAL_HEADS = 4
        META_HEADS = NH // 4
        CAUSAL_W = 0.7
        META_W = (0.9 - 0.8) / 0.2 * 0.3

        def _mha(xq, xkv, Win, bi, Wout, bout, nh):
            b, sq, h = xq.shape
            sk = xkv.shape[1]
            hd = h // nh
            q = (xq @ Win[:, :h] + bi[:h]).reshape(b, sq, nh, hd).transpose(0, 2, 1, 3)
            k = (xkv @ Win[:, h:2 * h] + bi[h:2 * h]).reshape(b, sk, nh, hd).transpose(0, 2, 1, 3)
            v = (xkv @ Win[:, 2 * h:] + bi[2 * h:]).reshape(b, sk, nh, hd).transpose(0, 2, 1, 3)
            scores = jnp.einsum('bhqd,bhkd->bhqk', q, k) / jnp.sqrt(jnp.asarray(hd, q.dtype))
            probs = jax.nn.softmax(scores, axis=-1)
            ctx = jnp.einsum('bhqk,bhkd->bhqd', probs, v)
            return ctx.transpose(0, 2, 1, 3).reshape(b, sq, h) @ Wout + bout

        def _forward(hidden_states, cons_vec, Wq, bq, Wk, bk, Wv, bv, cg_W, cg_b, am_W, am_b, ca_Win, ca_bin, ca_Wout, ca_bout, mc_Win, mc_bin, mc_Wout, mc_bout, Wo, bo):
            b, s, h = hidden_states.shape
            q = (hidden_states @ Wq + bq).reshape(b, s, NH, HD).transpose(0, 2, 1, 3)
            k = (hidden_states @ Wk + bk).reshape(b, s, NH, HD).transpose(0, 2, 1, 3)
            v = (hidden_states @ Wv + bv).reshape(b, s, NH, HD).transpose(0, 2, 1, 3)
            scores = jnp.einsum('bhqd,bhkd->bhqk', q, k) / jnp.sqrt(jnp.asarray(HD, q.dtype))
            mod = jax.nn.sigmoid(hidden_states @ cg_W + cg_b + (cons_vec @ am_W + am_b))
            scores = scores * mod.transpose(0, 2, 1)[..., None]
            probs = jax.nn.softmax(scores, axis=-1)
            ctx = jnp.einsum('bhqk,bhkd->bhqd', probs, v).transpose(0, 2, 1, 3).reshape(b, s, h)
            causal_ctx = _mha(hidden_states, hidden_states, ca_Win, ca_bin, ca_Wout, ca_bout, CAUSAL_HEADS)
            ctx = ctx * (1.0 - CAUSAL_W) + causal_ctx * CAUSAL_W
            meta_ctx = _mha(ctx, ctx, mc_Win, mc_bin, mc_Wout, mc_bout, META_HEADS)
            ctx = ctx * (1.0 - META_W) + meta_ctx * META_W
            return ctx @ Wo + bo
        key = jax.random.key(seed)
        ks = jax.random.split(key, 16)
        sc = 0.02
        d = {'hidden_states': jax.random.normal(ks[0], (B, S, H), jnp.float32), 'cons_vec': jax.random.uniform(ks[1], (16,), jnp.float32), 'Wq': jax.random.normal(ks[2], (H, H), jnp.float32) * sc, 'bq': jnp.zeros((H,), jnp.float32), 'Wk': jax.random.normal(ks[3], (H, H), jnp.float32) * sc, 'bk': jnp.zeros((H,), jnp.float32), 'Wv': jax.random.normal(ks[4], (H, H), jnp.float32) * sc, 'bv': jnp.zeros((H,), jnp.float32), 'cg_W': jax.random.normal(ks[5], (H, NH), jnp.float32) * sc, 'cg_b': jnp.zeros((NH,), jnp.float32), 'am_W': jax.random.normal(ks[6], (16, NH), jnp.float32) * sc, 'am_b': jnp.zeros((NH,), jnp.float32), 'ca_Win': jax.random.normal(ks[7], (H, 3 * H), jnp.float32) * sc, 'ca_bin': jnp.zeros((3 * H,), jnp.float32), 'ca_Wout': jax.random.normal(ks[8], (H, H), jnp.float32) * sc, 'ca_bout': jnp.zeros((H,), jnp.float32), 'mc_Win': jax.random.normal(ks[9], (H, 3 * H), jnp.float32) * sc, 'mc_bin': jnp.zeros((3 * H,), jnp.float32), 'mc_Wout': jax.random.normal(ks[10], (H, H), jnp.float32) * sc, 'mc_bout': jnp.zeros((H,), jnp.float32), 'Wo': jax.random.normal(ks[11], (H, H), jnp.float32) * sc, 'bo': jnp.zeros((H,), jnp.float32)}
        return d
    _L1_attn_all = _L1_attn_setup()
    _L1_attn_in = {k: v for k, v in _L1_attn_all.items() if k in ('cons_vec', 'Wq', 'bq', 'Wk', 'bk', 'Wv', 'bv', 'cg_W', 'cg_b', 'am_W', 'am_b', 'ca_Win', 'ca_bin', 'ca_Wout', 'ca_bout', 'mc_Win', 'mc_bin', 'mc_Wout', 'mc_bout', 'Wo', 'bo')}
    del _L1_attn_all

    def _L1_ffn_setup():
        import jax, jax.numpy as jnp
        import numpy as np
        D_MODEL = 256
        EXPERT_DIM = 128
        N_EXPERTS = 8
        TOP_K = 2

        def _sq_relu(h):
            return jnp.square(jax.nn.relu(h))
        key = jax.random.key(seed)
        ks = jax.random.split(key, 6)
        s = 0.02
        x = jax.random.normal(ks[0], (2, 512, D_MODEL), dtype=jnp.float32)
        Ws1 = jax.random.normal(ks[1], (D_MODEL, EXPERT_DIM), dtype=jnp.float32) * s
        Ws2 = jax.random.normal(ks[2], (EXPERT_DIM, D_MODEL), dtype=jnp.float32) * s
        W1 = jax.random.normal(ks[3], (N_EXPERTS, D_MODEL, EXPERT_DIM), dtype=jnp.float32) * s
        W2 = jax.random.normal(ks[4], (N_EXPERTS, EXPERT_DIM, D_MODEL), dtype=jnp.float32) * s
        Wr = jax.random.normal(ks[5], (D_MODEL, N_EXPERTS), dtype=jnp.float32) * s
        return {'x': x, 'Ws1': Ws1, 'Ws2': Ws2, 'W1': W1, 'W2': W2, 'Wr': Wr}
    _L1_ffn_all = _L1_ffn_setup()
    _L1_ffn_in = {k: v for k, v in _L1_ffn_all.items() if k in ('Ws1', 'Ws2', 'W1', 'W2', 'Wr')}
    del _L1_ffn_all
    return {'x': x, 'ctx_1024': ctx_1024, 'mask_BxS2_bf1': mask_BxS2_bf1, 'mask_BxS2_bk0': mask_BxS2_bk0, 'L0_xattn_Wq': _L0_xattn_in['Wq'], 'L0_xattn_Wk': _L0_xattn_in['Wk'], 'L0_xattn_Wv': _L0_xattn_in['Wv'], 'L0_xattn_Wo': _L0_xattn_in['Wo'], 'L0_xattn_bo': _L0_xattn_in['bo'], 'L0_attn_qkv': _L0_attn_in['qkv'], 'L0_attn_q_bias': _L0_attn_in['q_bias'], 'L0_attn_positional': _L0_attn_in['positional'], 'L0_attn_out_kernel': _L0_attn_in['out_kernel'], 'L0_attn_out_bias': _L0_attn_in['out_bias'], 'L0_ffn_ln1_g': _L0_ffn_in['ln1_g'], 'L0_ffn_ln1_b': _L0_ffn_in['ln1_b'], 'L0_ffn_w1': _L0_ffn_in['w1'], 'L0_ffn_b1': _L0_ffn_in['b1'], 'L0_ffn_ln2_g': _L0_ffn_in['ln2_g'], 'L0_ffn_ln2_b': _L0_ffn_in['ln2_b'], 'L0_ffn_w2': _L0_ffn_in['w2'], 'L0_ffn_b2': _L0_ffn_in['b2'], 'L1_xattn_Wq': _L1_xattn_in['Wq'], 'L1_xattn_bq': _L1_xattn_in['bq'], 'L1_xattn_Wk': _L1_xattn_in['Wk'], 'L1_xattn_bk': _L1_xattn_in['bk'], 'L1_xattn_Wv': _L1_xattn_in['Wv'], 'L1_xattn_bv': _L1_xattn_in['bv'], 'L1_xattn_Wo': _L1_xattn_in['Wo'], 'L1_xattn_bo': _L1_xattn_in['bo'], 'L1_attn_cons_vec': _L1_attn_in['cons_vec'], 'L1_attn_Wq': _L1_attn_in['Wq'], 'L1_attn_bq': _L1_attn_in['bq'], 'L1_attn_Wk': _L1_attn_in['Wk'], 'L1_attn_bk': _L1_attn_in['bk'], 'L1_attn_Wv': _L1_attn_in['Wv'], 'L1_attn_bv': _L1_attn_in['bv'], 'L1_attn_cg_W': _L1_attn_in['cg_W'], 'L1_attn_cg_b': _L1_attn_in['cg_b'], 'L1_attn_am_W': _L1_attn_in['am_W'], 'L1_attn_am_b': _L1_attn_in['am_b'], 'L1_attn_ca_Win': _L1_attn_in['ca_Win'], 'L1_attn_ca_bin': _L1_attn_in['ca_bin'], 'L1_attn_ca_Wout': _L1_attn_in['ca_Wout'], 'L1_attn_ca_bout': _L1_attn_in['ca_bout'], 'L1_attn_mc_Win': _L1_attn_in['mc_Win'], 'L1_attn_mc_bin': _L1_attn_in['mc_bin'], 'L1_attn_mc_Wout': _L1_attn_in['mc_Wout'], 'L1_attn_mc_bout': _L1_attn_in['mc_bout'], 'L1_attn_Wo': _L1_attn_in['Wo'], 'L1_attn_bo': _L1_attn_in['bo'], 'L1_ffn_Ws1': _L1_ffn_in['Ws1'], 'L1_ffn_Ws2': _L1_ffn_in['Ws2'], 'L1_ffn_W1': _L1_ffn_in['W1'], 'L1_ffn_W2': _L1_ffn_in['W2'], 'L1_ffn_Wr': _L1_ffn_in['Wr']}

def reference(x, ctx_1024, mask_BxS2_bf1, mask_BxS2_bk0, L0_xattn_Wq, L0_xattn_Wk, L0_xattn_Wv, L0_xattn_Wo, L0_xattn_bo, L0_attn_qkv, L0_attn_q_bias, L0_attn_positional, L0_attn_out_kernel, L0_attn_out_bias, L0_ffn_ln1_g, L0_ffn_ln1_b, L0_ffn_w1, L0_ffn_b1, L0_ffn_ln2_g, L0_ffn_ln2_b, L0_ffn_w2, L0_ffn_b2, L1_xattn_Wq, L1_xattn_bq, L1_xattn_Wk, L1_xattn_bk, L1_xattn_Wv, L1_xattn_bv, L1_xattn_Wo, L1_xattn_bo, L1_attn_cons_vec, L1_attn_Wq, L1_attn_bq, L1_attn_Wk, L1_attn_bk, L1_attn_Wv, L1_attn_bv, L1_attn_cg_W, L1_attn_cg_b, L1_attn_am_W, L1_attn_am_b, L1_attn_ca_Win, L1_attn_ca_bin, L1_attn_ca_Wout, L1_attn_ca_bout, L1_attn_mc_Win, L1_attn_mc_bin, L1_attn_mc_Wout, L1_attn_mc_bout, L1_attn_Wo, L1_attn_bo, L1_ffn_Ws1, L1_ffn_Ws2, L1_ffn_W1, L1_ffn_W2, L1_ffn_Wr):
    import jax
    import jax.numpy as jnp

    def _L0_xattn_ref(query, key_value, mask, Wq, Wk, Wv, Wo, bo):
        import jax, jax.numpy as jnp
        import numpy as np
        HIDDEN = 256
        HEADS = 16
        HEAD_DIM = HIDDEN // HEADS
        B, Q, _ = query.shape
        KV = key_value.shape[1]
        q = (query @ Wq.T).reshape(B, Q, HEADS, HEAD_DIM)
        k = (key_value @ Wk.T).reshape(B, KV, HEADS, HEAD_DIM)
        v = (key_value @ Wv.T).reshape(B, KV, HEADS, HEAD_DIM)
        scale = 1.0 / np.sqrt(HEAD_DIM).astype(np.float32)
        attn = jnp.einsum('bqhd,bkhd->bhqk', q, k) * scale
        attn = jnp.where(mask[:, None, None, :], attn, -jnp.inf)
        attn = jax.nn.softmax(attn, axis=-1)
        out = jnp.einsum('bhqk,bkhd->bqhd', attn, v).reshape(B, Q, HIDDEN)
        return out @ Wo.T + bo

    def _L0_attn_ref(input, qkv, q_bias, positional, out_kernel, out_bias):
        import jax, jax.numpy as jnp
        import numpy as np
        HEADS, HEAD_SIZE, FREQS, MAX_PERIOD = (16, 64, 64, 2500)
        D_MODEL = 256
        NEG_INF = -1000000000.0

        def sinusoid_embedding(seq_len, frequencies, max_period):
            pos = np.arange(seq_len, dtype=np.float64)[:, None]
            idx = np.arange(frequencies)[None, :]
            inv_freq = max_period ** (-(idx // 2 * 2) / frequencies)
            angle = pos * inv_freq
            table = np.where(idx % 2 == 0, np.sin(angle), np.cos(angle))
            return table.astype(np.float32)

        def relative_causal(scores):
            L = scores.shape[-1]
            d = jnp.clip(jnp.arange(L)[:, None] - jnp.arange(L)[None, :], 0, L - 1)
            return jnp.take_along_axis(scores, d[None, None, :, :], axis=-1)
        b, s, x = input.shape
        n, h = (HEADS, HEAD_SIZE)
        w = qkv * (3.0 * x * h * n) ** (-0.25)
        q, k, v = jnp.einsum('bsx,xAnh->Abnsh', input, w)
        q = q + q_bias[:, None, :]
        a = jnp.einsum('bnqh,bnkh->bnqk', q, k) * h ** (-0.5)
        sins = jnp.asarray(np.sqrt(2.0) * sinusoid_embedding(s, FREQS, MAX_PERIOD))
        emb = jnp.einsum('sf,fnh->nsh', sins, positional * FREQS ** (-0.5))
        pos_scores = jnp.einsum('bnqh,nvh->bnqv', q, emb) * h ** (-0.5)
        a = a + relative_causal(pos_scores)
        mask = jnp.tril(jnp.ones((s, s), dtype=bool))
        a = jax.nn.softmax(jnp.where(mask, a, NEG_INF), axis=-1)
        o = jnp.einsum('bnqk,bnkh->bqnh', a, v).reshape(b, s, n * h)
        fan_in, fan_out = out_kernel.shape
        out = o @ (out_kernel * (fan_in * fan_out) ** (-0.25)) + out_bias
        return out

    def _L0_ffn_ref(x, ln1_g, ln1_b, w1, b1, ln2_g, ln2_b, w2, b2):
        import jax, jax.numpy as jnp
        import numpy as np
        LN_EPS = 1e-05

        def layernorm(x, g, b):
            mu = jnp.mean(x, axis=-1, keepdims=True)
            var = jnp.mean((x - mu) ** 2, axis=-1, keepdims=True)
            return (x - mu) * jax.lax.rsqrt(var + LN_EPS) * g + b

        def act_quant_fake(x):
            scale = 127.0 / jnp.clip(jnp.max(jnp.abs(x), axis=-1, keepdims=True), 1e-05)
            return jnp.clip(jnp.round(x * scale), -128.0, 127.0) / scale

        def weight_quant_fake(w):
            scale = 1.0 / jnp.clip(jnp.mean(jnp.abs(w)), 1e-05)
            return jnp.clip(jnp.round(w * scale), -1.0, 1.0) / scale

        def bitlinear(x, w, b):
            dqx = act_quant_fake(x)
            dqw = weight_quant_fake(w)
            return jnp.einsum('btd,hd->bth', dqx, dqw) + b
        h = layernorm(x, ln1_g, ln1_b)
        h = bitlinear(h, w1, b1)
        h = jax.nn.gelu(h, approximate=False)
        h = layernorm(h, ln2_g, ln2_b)
        h = bitlinear(h, w2, b2)
        return h

    def _L1_xattn_ref(q, kv, pad_mask, Wq, bq, Wk, bk, Wv, bv, Wo, bo):
        import jax, jax.numpy as jnp
        import numpy as np
        D_Q, D_KV, N_HEADS = (256, 256, 16)
        HEAD_DIM = D_Q // N_HEADS
        SCALE = HEAD_DIM ** (-0.5)
        B, Sq, _ = q.shape
        Skv = kv.shape[1]
        H, D = (N_HEADS, HEAD_DIM)
        q_h = (q @ Wq + bq).reshape(B, Sq, H, D).transpose(0, 2, 1, 3)
        k_h = (kv @ Wk + bk).reshape(B, Skv, H, D).transpose(0, 2, 1, 3)
        v_h = (kv @ Wv + bv).reshape(B, Skv, H, D).transpose(0, 2, 1, 3)
        scores = jnp.einsum('bhqd,bhkd->bhqk', q_h, k_h) * SCALE
        scores = jnp.where(pad_mask[:, None, None, :], jnp.float32(-1000000000.0), scores)
        attn = jax.nn.softmax(scores, axis=-1)
        out = jnp.einsum('bhqk,bhkd->bhqd', attn, v_h)
        out = out.transpose(0, 2, 1, 3).reshape(B, Sq, H * D)
        return out @ Wo + bo

    def _L1_attn_ref(hidden_states, cons_vec, Wq, bq, Wk, bk, Wv, bv, cg_W, cg_b, am_W, am_b, ca_Win, ca_bin, ca_Wout, ca_bout, mc_Win, mc_bin, mc_Wout, mc_bout, Wo, bo):
        import jax, jax.numpy as jnp
        import numpy as np
        B, S, H, NH = (4, 256, 256, 16)
        HD = H // NH
        CAUSAL_HEADS = 4
        META_HEADS = NH // 4
        CAUSAL_W = 0.7
        META_W = (0.9 - 0.8) / 0.2 * 0.3

        def _mha(xq, xkv, Win, bi, Wout, bout, nh):
            b, sq, h = xq.shape
            sk = xkv.shape[1]
            hd = h // nh
            q = (xq @ Win[:, :h] + bi[:h]).reshape(b, sq, nh, hd).transpose(0, 2, 1, 3)
            k = (xkv @ Win[:, h:2 * h] + bi[h:2 * h]).reshape(b, sk, nh, hd).transpose(0, 2, 1, 3)
            v = (xkv @ Win[:, 2 * h:] + bi[2 * h:]).reshape(b, sk, nh, hd).transpose(0, 2, 1, 3)
            scores = jnp.einsum('bhqd,bhkd->bhqk', q, k) / jnp.sqrt(jnp.asarray(hd, q.dtype))
            probs = jax.nn.softmax(scores, axis=-1)
            ctx = jnp.einsum('bhqk,bhkd->bhqd', probs, v)
            return ctx.transpose(0, 2, 1, 3).reshape(b, sq, h) @ Wout + bout

        def _forward(hidden_states, cons_vec, Wq, bq, Wk, bk, Wv, bv, cg_W, cg_b, am_W, am_b, ca_Win, ca_bin, ca_Wout, ca_bout, mc_Win, mc_bin, mc_Wout, mc_bout, Wo, bo):
            b, s, h = hidden_states.shape
            q = (hidden_states @ Wq + bq).reshape(b, s, NH, HD).transpose(0, 2, 1, 3)
            k = (hidden_states @ Wk + bk).reshape(b, s, NH, HD).transpose(0, 2, 1, 3)
            v = (hidden_states @ Wv + bv).reshape(b, s, NH, HD).transpose(0, 2, 1, 3)
            scores = jnp.einsum('bhqd,bhkd->bhqk', q, k) / jnp.sqrt(jnp.asarray(HD, q.dtype))
            mod = jax.nn.sigmoid(hidden_states @ cg_W + cg_b + (cons_vec @ am_W + am_b))
            scores = scores * mod.transpose(0, 2, 1)[..., None]
            probs = jax.nn.softmax(scores, axis=-1)
            ctx = jnp.einsum('bhqk,bhkd->bhqd', probs, v).transpose(0, 2, 1, 3).reshape(b, s, h)
            causal_ctx = _mha(hidden_states, hidden_states, ca_Win, ca_bin, ca_Wout, ca_bout, CAUSAL_HEADS)
            ctx = ctx * (1.0 - CAUSAL_W) + causal_ctx * CAUSAL_W
            meta_ctx = _mha(ctx, ctx, mc_Win, mc_bin, mc_Wout, mc_bout, META_HEADS)
            ctx = ctx * (1.0 - META_W) + meta_ctx * META_W
            return ctx @ Wo + bo
        return _forward(hidden_states, cons_vec, Wq, bq, Wk, bk, Wv, bv, cg_W, cg_b, am_W, am_b, ca_Win, ca_bin, ca_Wout, ca_bout, mc_Win, mc_bin, mc_Wout, mc_bout, Wo, bo)

    def _L1_ffn_ref(x, Ws1, Ws2, W1, W2, Wr):
        import jax, jax.numpy as jnp
        import numpy as np
        D_MODEL = 256
        EXPERT_DIM = 128
        N_EXPERTS = 8
        TOP_K = 2

        def _sq_relu(h):
            return jnp.square(jax.nn.relu(h))
        shape = x.shape
        xf = x.reshape(-1, D_MODEL)
        out_shared = _sq_relu(xf @ Ws1) @ Ws2
        logits = xf @ Wr
        top_vals, top_idx = jax.lax.top_k(logits, TOP_K)
        rw = jax.nn.softmax(top_vals.astype(jnp.float32), axis=-1).astype(x.dtype)
        onehot = jax.nn.one_hot(top_idx, N_EXPERTS, dtype=x.dtype)
        prob = jnp.einsum('tk,tke->te', rw, onehot)
        prob = jnp.trunc(prob)
        h = _sq_relu(jnp.einsum('td,edf->tef', xf, W1))
        y = jnp.einsum('tef,efd->ted', h, W2)
        out_routed = jnp.einsum('ted,te->td', y, prob)
        return (out_shared + out_routed).reshape(shape)
    x = x + _L0_xattn_ref(_layernorm(x, axis=-1), ctx_1024, mask_BxS2_bf1, L0_xattn_Wq, L0_xattn_Wk, L0_xattn_Wv, L0_xattn_Wo, L0_xattn_bo)
    x = x + _L0_attn_ref(_layernorm(x, axis=-1), L0_attn_qkv, L0_attn_q_bias, L0_attn_positional, L0_attn_out_kernel, L0_attn_out_bias)
    x = x + _L0_ffn_ref(_layernorm(x, axis=-1), L0_ffn_ln1_g, L0_ffn_ln1_b, L0_ffn_w1, L0_ffn_b1, L0_ffn_ln2_g, L0_ffn_ln2_b, L0_ffn_w2, L0_ffn_b2)
    x = x + _L1_xattn_ref(_layernorm(x, axis=-1), ctx_1024, mask_BxS2_bk0, L1_xattn_Wq, L1_xattn_bq, L1_xattn_Wk, L1_xattn_bk, L1_xattn_Wv, L1_xattn_bv, L1_xattn_Wo, L1_xattn_bo)
    x = x + _L1_attn_ref(_layernorm(x, axis=-1), L1_attn_cons_vec, L1_attn_Wq, L1_attn_bq, L1_attn_Wk, L1_attn_bk, L1_attn_Wv, L1_attn_bv, L1_attn_cg_W, L1_attn_cg_b, L1_attn_am_W, L1_attn_am_b, L1_attn_ca_Win, L1_attn_ca_bin, L1_attn_ca_Wout, L1_attn_ca_bout, L1_attn_mc_Win, L1_attn_mc_bin, L1_attn_mc_Wout, L1_attn_mc_bout, L1_attn_Wo, L1_attn_bo)
    x = x + _L1_ffn_ref(_layernorm(x, axis=-1), L1_ffn_Ws1, L1_ffn_Ws2, L1_ffn_W1, L1_ffn_W2, L1_ffn_Wr)
    return x

_drawn_inputs = setup_inputs


def setup_inputs(seed=0):
    import zlib

    import numpy as np

    out = dict(_drawn_inputs(seed))
    spreads = {'L0_xattn_bo': (0.0, 0.1),
     'L0_attn_q_bias': (0.0, 0.46),
     'L0_attn_out_bias': (0.0, 0.1),
     'L0_ffn_ln1_g': (1.0, 0.2),
     'L0_ffn_ln1_b': (0.0, 0.1),
     'L0_ffn_ln2_g': (1.0, 0.2),
     'L0_ffn_ln2_b': (0.0, 0.1),
     'L1_xattn_bq': (0.0, 0.8),
     'L1_xattn_bk': (0.0, 2.0),
     'L1_xattn_bv': (0.0, 0.341),
     'L1_xattn_bo': (0.0, 0.1),
     'L1_attn_bq': (0.0, 0.8),
     'L1_attn_bk': (0.0, 2.0),
     'L1_attn_bv': (0.0, 0.8),
     'L1_attn_cg_b': (0.0, 0.8),
     'L1_attn_am_b': (0.0, 0.8),
     'L1_attn_ca_bin': (0.0, 0.8),
     'L1_attn_ca_bout': (0.0, 0.651),
     'L1_attn_mc_bin': (0.0, 0.8),
     'L1_attn_mc_bout': (0.0, 2.0),
     'L1_attn_bo': (0.0, 0.367)}
    factors = {'L0_ffn_b1': 2.82,
     'L0_ffn_b2': 4.062,
     'L1_xattn_Wq': 8.0,
     'L1_xattn_Wk': 8.0,
     'L1_attn_cons_vec': 8.0,
     'L1_attn_Wq': 8.0,
     'L1_attn_Wk': 8.0,
     'L1_attn_Wv': 5.933,
     'L1_attn_cg_W': 8.0,
     'L1_attn_am_W': 8.0,
     'L1_attn_ca_Win': 7.85,
     'L1_attn_ca_Wout': 7.043,
     'L1_attn_mc_Win': 8.0,
     'L1_attn_mc_Wout': 8.0,
     'L1_attn_Wo': 2.806,
     'L1_ffn_Ws1': 3.005,
     'L1_ffn_Ws2': 2.782}
    for name, (base, spread) in spreads.items():
        noise = np.random.default_rng([zlib.crc32(name.encode()), seed]).standard_normal(out[name].shape)
        drawn = base * np.exp(spread * noise) if base else spread * noise
        out[name] = jnp.asarray(drawn.astype(out[name].dtype))
    for name, factor in factors.items():
        out[name] = (out[name] * factor).astype(out[name].dtype)
    return out
```

```python
from contextlib import ExitStack

import concourse.bass as bass
from concourse import mybir

F32 = mybir.dt.float32
BF16 = mybir.dt.bfloat16
U8 = mybir.dt.uint8
ALU = mybir.AluOpType
ACT = mybir.ActivationFunctionType
AX = mybir.AxisListType

P = 128
B, S, D = 16, 64, 256
T = B * S
TT = T // P
DC = D // P
NKV = 256
KT = NKV // P
BANK = 512
NH = T // BANK
HID = 1024
HC = HID // P
EXPERTS = 8
EPS = 1e-5
ROUND = 12582912.0
L0_MASKED = -3.0e38
PADDED = -1.0e9
CAUSAL_W = 0.7
META_W = (0.9 - 0.8) / 0.2 * 0.3


def bc(ap, axis, n):
    shape = list(ap.shape)
    return ap.unsqueeze(axis).broadcast_to(shape[:axis] + [n] + shape[axis:])


def wait_free(eng, sem, value):
    if not (isinstance(value, int) and value <= 0):
        eng.wait_ge(sem, value)


class Shared:

    def __init__(self, nc, ctx):
        self.nc, self.ctx = nc, ctx
        self.sems = {}
        sb = self.sb
        self.x_tok = sb("x_tok", [P, TT, D])
        self.xn_tok = sb("xn_tok", [P, TT, D])
        self.xn_feat = sb("xn_feat", [P, DC, T])
        self.q_feat = sb("q_feat", [P, DC, T])
        self.o_feat = sb("o_feat", [P, DC, T])
        self.stats = sb("stats", [P, TT, 2, 6])
        self.mean_var = sb("mean_var", [P, TT, 2])
        self.ln_var = sb("ln_var", [P, TT])
        self.rstd = sb("rstd", [P, TT])
        self.newton = sb("newton", [P, TT])
        self.identity = sb("identity", [P, P])
        self.identity_bf = sb("identity_bf", [P, P], BF16)
        self.ones = sb("ones", [P, P])
        self.ones_bf = sb("ones_bf", [1, P], BF16)
        self.head_rows = sb("head_rows", [P, 8])
        self.pad_bias = sb("pad_bias", [P, B, NKV], BF16)
        self.keep = sb("keep", [P, B, NKV], BF16)
        self.half_rows = sb("half_rows", [P, 2])
        self.psum = ctx.enter_context(nc.psum_tensor("psum", [P, 8, BANK], F32))

    def sb(self, name, shape, dt=F32, scope=None):
        return (scope or self.ctx).enter_context(self.nc.sbuf_tensor(name, shape, dt))

    def sem(self, name):
        if name not in self.sems:
            self.sems[name] = self.ctx.enter_context(self.nc.semaphore(name))
        return self.sems[name]


class Stage:

    def tensor(self, pe):
        pass

    def scalar(self, act):
        pass

    def vector(self, dve):
        pass

    def gpsimd(self, pool):
        pass

    def sync(self, sp):
        pass


def load_stage(c, dram):
    s = Stage()
    x_in, const_in, ident_bf = c.sem("x_in"), c.sem("const_in"), c.sem("ident_bf")

    def sync(sp):
        sp.dma_start(c.x_tok[:], dram["x"].rearrange("(t p) d -> p t d", p=P)).then_inc(x_in, 16)
        sp.dma_start(c.identity[:], dram["identity"]).then_inc(const_in, 16)
        sp.dma_start(c.head_rows[:], dram["head_rows"]).then_inc(const_in, 16)
        sp.dma_start(c.half_rows[:], dram["half_rows"]).then_inc(const_in, 16)

    def gpsimd(pool):
        pool.memset(c.ones_bf[:], 1.0).then_inc(ident_bf, 1)
        pool.memset(c.ones[:], 1.0).then_inc(ident_bf, 1)
        pool.wait_ge(const_in, 48)
        pool.tensor_copy(c.identity_bf[:], c.identity[:]).then_inc(ident_bf, 1)

    def tensor(pe):
        pe.wait_ge(const_in, 48)
        pe.wait_ge(ident_bf, 3)

    def vector(dve):
        dve.wait_ge(const_in, 48)
        dve.wait_ge(x_in, 16)

    s.sync, s.gpsimd, s.tensor, s.vector = sync, gpsimd, tensor, vector
    return s


def rstd_scalar(c, act, aggr, aggr_value, use):
    rstd_ln, rstd_exp = c.sem("rstd_ln"), c.sem("rstd_exp")
    act.wait_ge(aggr, aggr_value)
    act.activation(c.ln_var[:], c.newton[:], ACT.Ln).then_inc(rstd_ln, 1)
    act.wait_ge(rstd_ln, use + 1)
    act.activation(c.rstd[:], c.ln_var[:], ACT.Exp, scale=-0.5).then_inc(rstd_exp, 1)


def rstd_vector(c, dve, use):
    rstd_exp, refined = c.sem("rstd_exp"), c.sem("rstd_refined")
    y, t, v = c.rstd, c.ln_var, c.newton
    dve.wait_ge(rstd_exp, use + 1)
    dve.tensor_tensor(t[:], y[:], y[:], ALU.mult).then_inc(refined, 1)
    dve.wait_ge(refined, 4 * use + 1)
    dve.tensor_tensor(t[:], t[:], v[:], ALU.mult).then_inc(refined, 1)
    dve.wait_ge(refined, 4 * use + 2)
    dve.tensor_scalar(t[:], t[:], -0.5, 1.5, ALU.mult, ALU.add).then_inc(refined, 1)
    dve.wait_ge(refined, 4 * use + 3)
    dve.tensor_tensor(y[:], y[:], t[:], ALU.mult).then_inc(refined, 1)
    dve.wait_ge(refined, 4 * use + 4)


def statistics(c, dve, source, pieces, use, scope_sems):
    stats_done, aggr_done, var_eps = scope_sems
    for t in range(TT):
        for h in range(pieces):
            ins = dve.bn_stats(c.stats[:, t, h, :], source(t, h))
        ins.then_inc(stats_done, 1)
    for t in range(TT):
        dve.wait_ge(stats_done, TT * use + t + 1)
        dve.bn_aggr(c.mean_var[:, t, :], c.stats[:, t, 0:pieces, :]).then_inc(aggr_done, 1)
    dve.wait_ge(aggr_done, TT * (use + 1))
    dve.tensor_scalar(c.newton[:], c.mean_var[:, :, 1], EPS, None, ALU.add).then_inc(var_eps, 1)


def norm_stage(c, use, stat_use):
    s = Stage()
    sems = c.sem("stats_done"), c.sem("aggr_done"), c.sem("var_eps")
    x_ready, xn_ready, turned = c.sem("x_ready"), c.sem("xn_ready"), c.sem("norm_turned")
    feat_act, feat_dve = c.sem("feat_act"), c.sem("feat_dve")
    tiles = TT // 2

    def feat(k):
        return c.xn_feat[:, :, 2 * P * k:2 * P * (k + 1)]

    def bank(k):
        return c.psum[:, k, :].rearrange("p (c n) -> p c n", c=DC)

    def vector(dve):
        if use:
            dve.wait_ge(x_ready, TT * use)
        statistics(c, dve, lambda t, h: c.x_tok[:, t, :], 1, stat_use, sems)
        rstd_vector(c, dve, stat_use)
        for t in range(TT):
            dve.tensor_scalar(c.xn_tok[:, t, :], c.x_tok[:, t, :], c.mean_var[:, t, 0:1],
                              c.rstd[:, t:t + 1], ALU.subtract, ALU.mult).then_inc(xn_ready, 1)
        for k in range(1, tiles, 2):
            dve.wait_ge(turned, tiles * use + k + 1)
            dve.tensor_copy(feat(k), bank(k)).then_inc(feat_dve, 1)

    def scalar(act):
        rstd_scalar(c, act, sems[2], stat_use + 1, stat_use)
        for k in range(0, tiles, 2):
            act.wait_ge(turned, tiles * use + k + 1)
            act.activation(feat(k), bank(k), ACT.Copy).then_inc(feat_act, 1)

    def tensor(pe):
        for k in range(tiles):
            for h in range(2):
                pe.wait_ge(xn_ready, TT * use + 2 * k + h + 1)
                for m in range(DC):
                    ins = pe.transpose(bank(k)[:, m, h * P:(h + 1) * P],
                                       c.xn_tok[:, 2 * k + h, m * P:(m + 1) * P], c.identity[:])
            ins.then_inc(turned, 1)

    s.vector, s.scalar, s.tensor = vector, scalar, tensor
    return s


def wait_feat(c, eng, use):
    eng.wait_ge(c.sem("feat_act"), 2 * (use + 1))
    eng.wait_ge(c.sem("feat_dve"), 2 * (use + 1))


def out_projection(c, use, out_use, feat, chunks, weight, weights, feat_ready, bias):
    s = Stage()
    x_ready, xn_ready, out_done = c.sem("x_ready"), c.sem("xn_ready"), c.sem("out_done")
    bias_added = c.sem("bias_added")
    ring = 4

    def gpsimd(pool):
        weights.wait(pool)
        pool.wait_ge(xn_ready, TT * (use + 1))
        pool.tensor_tensor(c.x_tok[:], c.x_tok[:], bc(bias[:], 1, TT), ALU.add).then_inc(bias_added, 1)

    def tensor(pe):
        weights.wait(pe)
        for sem, value in feat_ready:
            pe.wait_ge(sem, value)
        for t in range(TT):
            if t >= ring:
                pe.wait_ge(x_ready, TT * use + t - ring + 1)
            for k in range(chunks):
                ins = pe.matmul(c.psum[:, t % ring, 0:D], feat[:, k, t * P:(t + 1) * P],
                                weight[:, k, :], start=(k == 0), stop=(k == chunks - 1))
            ins.then_inc(out_done, 1)

    def vector(dve):
        dve.wait_ge(bias_added, out_use + 1)
        for t in range(TT):
            dve.wait_ge(out_done, TT * out_use + t + 1)
            dve.tensor_tensor(c.x_tok[:, t, :], c.psum[:, t % ring, 0:D], c.x_tok[:, t, :],
                              ALU.add).then_inc(x_ready, 1)

    s.gpsimd, s.tensor, s.vector = gpsimd, tensor, vector
    return s


class Loads:

    def __init__(self, c, name, count):
        self.sem, self.total = c.sem(name), 16 * count

    def dma(self, sp, out, in_):
        sp.dma_start(out, in_).then_inc(self.sem, 16)

    def wait(self, eng):
        eng.wait_ge(self.sem, self.total)


def allocate_cross_weights(c, layer):
    wq, wk, wv, wo = (c.sb(f"{layer}x_{n}", [P, DC, D]) for n in ("wq", "wk", "wv", "wo"))
    bo = c.sb(f"{layer}x_bo", [P, D])
    cols = c.sb(f"{layer}x_cols", [P, 3, DC])
    return wq, wk, wv, wo, bo, cols


def cross_attention(c, dram, use, norm_use, out_use, layer, biased):
    s = Stage()
    scope = ExitStack()
    steps = DC * B
    pairs = 4
    wq, wk, wv, wo, bo, cols = c.cross_weights[layer]
    mask = c.sb(f"{layer}x_mask", [P, B, NKV], U8, scope)
    ctx_t = [c.sb(f"{layer}ctx{i}", [P, DC, NKV], F32, scope) for i in range(2)]
    k_feat = [c.sb(f"{layer}k{i}", [P, DC, NKV], F32, scope) for i in range(2)]
    v_tok = [c.sb(f"{layer}v{i}", [P, KT, D], F32, scope) for i in range(2)]
    q_diag = [c.sb(f"{layer}qd{i}", [P, DC, 8, S], F32, scope) for i in range(2)]
    probs = [c.sb(f"{layer}p{i}", [P, pairs, NKV], F32, scope) for i in range(2)]
    pad_row = [c.sb(f"{layer}pr{i}", [1, NKV], BF16, scope) for i in range(2)]
    probs_t = c.sb(f"{layer}pt", [P, KT, BANK], F32, scope)
    neg_max = c.sb(f"{layer}nm", [P, 2, pairs], F32, scope)
    row_sum = c.sb(f"{layer}rs", [P, 2, pairs], F32, scope)
    row_inv = c.sb(f"{layer}ri", [P, 2, pairs], F32, scope)
    o_half = c.sb(f"{layer}oh", [P, DC, S], F32, scope)
    scope.close()

    weights = Loads(c, f"{layer}x_weights", 6 if biased else 5)
    mask_in = c.sem(f"{layer}x_mask_in")
    ctx_in = [c.sem("ctx_in0"), c.sem("ctx_in1")]
    q_done, q_moved = c.sem("xq_done"), c.sem("xq_moved")
    mask_ready = c.sem("x_mask_ready")
    kv_done, kv_moved = c.sem("x_kv_done"), c.sem("x_kv_moved")
    diag_ready, scores_done, max_done = c.sem("x_diag_ready"), c.sem("x_scores_done"), c.sem("x_max_done")
    exp_done, inv_ready, probs_ready = c.sem("x_exp_done"), c.sem("x_inv_ready"), c.sem("x_probs_ready")
    turned, pt_act, pt_dve = c.sem("x_turned"), c.sem("x_pt_act"), c.sem("x_pt_dve")
    pv_done, half_ready, o_moved = c.sem("x_pv_done"), c.sem("x_half_ready"), c.sem("x_o_moved")
    x_ready = c.sem("x_ready")
    n0, b0 = steps * use, B * use
    KV_BANK, O_BANK, TURN_BANK = 4, 5, 6

    def sync(sp):
        for a, name in ((wq, "Wq"), (wk, "Wk"), (wv, "Wv"), (wo, "Wo")):
            weights.dma(sp, a[:], dram[f"{layer}_xattn_{name}"].rearrange("(k p) n -> p k n", p=P))
        weights.dma(sp, bo[:], bc(dram[f"{layer}_xattn_bo"], 0, P))
        if biased:
            weights.dma(sp, cols[:], dram["L1_xattn_cols"])
        if use:
            sp.wait_ge(x_ready, TT * norm_use)
        sp.dma_start(mask[:], bc(dram[f"{layer}_mask"], 0, P)).then_inc(mask_in, 16)

        def load(b, half):
            sp.dma_start(ctx_t[half][:], dram["ctx"][b]).then_inc(ctx_in[half], 16)

        load(0, 0)
        load(1, 1)
        with sp.Fori(1, B // 2) as i:
            for half in range(2):
                sp.wait_ge(kv_done, 2 * b0 + 2 * (2 * i + half) - 2)
                load(2 * i + half, half)

    def tensor(pe):
        weights.wait(pe)
        wait_feat(c, pe, norm_use)
        for m in range(DC):
            for n in range(NH):
                for k in range(DC):
                    ins = pe.matmul(c.psum[:, KV_BANK + 2 * m + n, :], wq[:, k, m * P:(m + 1) * P],
                                    c.xn_feat[:, k, n * BANK:(n + 1) * BANK],
                                    start=(k == 0), stop=(k == DC - 1))
                ins.then_inc(q_done, 1)
        pe.wait_ge(q_moved, 4 * (use + 1))
        pe.wait_ge(mask_ready, 2 * use + 1)

        def project_k(b, half, pair):
            pe.wait_ge(ctx_in[half], 16 * (B // 2 * use + pair + 1))
            wait_free(pe, kv_moved, 2 * b0 + 2 * b)
            for m in range(DC):
                for k in range(DC):
                    ins = pe.matmul(c.psum[:, KV_BANK, m * NKV:(m + 1) * NKV], wk[:, k, m * P:(m + 1) * P],
                                    ctx_t[half][:, k, :], start=(k == 0), stop=(k == DC - 1))
            ins.then_inc(kv_done, 1)

        def project_v(b, half):
            pe.wait_ge(kv_moved, 2 * b0 + 2 * b + 1)
            for t in range(KT):
                for k in range(DC):
                    ins = pe.matmul(c.psum[:, KV_BANK, t * D:(t + 1) * D], ctx_t[half][:, k, t * P:(t + 1) * P],
                                    wv[:, k, :], start=(k == 0), stop=(k == DC - 1))
            ins.then_inc(kv_done, 1)

        def scores(n, b, half, chunk):
            slot = 2 * chunk
            if chunk == 0:
                pe.wait_ge(kv_moved, 2 * b0 + 2 * b + 1)
                pe.wait_ge(diag_ready, 3 * b0 + 3 * b + 3)
            wait_free(pe, exp_done, n0 + n - 1)
            for i in range(pairs):
                bank = c.psum[:, slot + i // 2, :]
                if i % 2 == 0:
                    pe.matmul(bank.rearrange("p (a k) -> p a k", a=2), c.ones_bf[:],
                              bc(pad_row[half][:], 1, 2), start=True, stop=False,
                              skip_group_check=True)
                ins = pe.matmul(bank[:, (i % 2) * NKV:(i % 2 + 1) * NKV],
                                q_diag[half][:, chunk, 2 * i:2 * i + 2, :].rearrange("p j q -> p (j q)"),
                                k_feat[half][:, chunk, :], start=False, stop=True, skip_group_check=True)
            ins.then_inc(scores_done, 1)

        def turn(n, slot):
            pe.wait_ge(probs_ready, n0 + n + 1)
            for t in range(KT):
                wait_free(pe, (pt_act, pt_dve)[t], n0 + n)
                for i in range(pairs):
                    ins = pe.transpose(c.psum[:, TURN_BANK + t, i * P:(i + 1) * P],
                                       probs[slot][:, i, t * P:(t + 1) * P], c.identity[:])
                ins.then_inc(turned, 1)

        def values(n, b, half, chunk):
            pe.wait_ge(pt_act, n0 + n + 1)
            pe.wait_ge(pt_dve, n0 + n + 1)
            if chunk == 0:
                pe.wait_ge(kv_moved, 2 * b0 + 2 * b + 2)
                wait_free(pe, o_moved, b0 + b)
            for i in range(pairs):
                for t in range(KT):
                    ins = pe.matmul(c.psum[32 * i:32 * i + 32, O_BANK, chunk * P:(chunk + 1) * P],
                                    v_tok[half][:, t, chunk * P + 32 * i:chunk * P + 32 * i + 32],
                                    probs_t[:, t, i * P:(i + 1) * P], start=(t == 0), stop=(t == KT - 1))
            ins.then_inc(pv_done, 1)

        def body(i, last=False):
            for j in range(4):
                n, b, half, chunk = 4 * i + j, 2 * i + j // 2, j // 2, j % 2
                if not (last and j == 3):
                    b1 = 2 * i + (j + 1) // 2
                    scores(n + 1, b1, (j + 1) // 2 % 2, (j + 1) % 2)
                turn(n, j % 2)
                if not (last and j >= 2):
                    if chunk == 0:
                        project_k(b + 1, 1 - half, i + (j + 2) // 4)
                    else:
                        project_v(b + 1, 1 - half)
                values(n, b, half, chunk)

        project_k(0, 0, 0)
        project_v(0, 0)
        scores(0, 0, 0, 0)
        body(0)
        with pe.Fori(1, B // 2 - 1) as i:
            body(i)
        body(B // 2 - 1, last=True)

    def scalar(act):
        weights.wait(act)
        for m in range(DC):
            for n in range(NH):
                act.wait_ge(q_done, 4 * use + 2 * m + n + 1)
                out, src = c.q_feat[:, m, n * BANK:(n + 1) * BANK], c.psum[:, KV_BANK + 2 * m + n, :]
                if biased:
                    act.activation(out, src, ACT.Identity, bias=cols[:, 0, m:m + 1]).then_inc(q_moved, 1)
                else:
                    act.activation(out, src, ACT.Copy).then_inc(q_moved, 1)

        def exps(n, slot):
            act.wait_ge(max_done, n0 + n + 1)
            for i in range(pairs):
                ins = act.activation(probs[slot][:, i, :], c.psum[:, 2 * slot + i // 2, (i % 2) * NKV:(i % 2 + 1) * NKV],
                                     ACT.Exp, bias=neg_max[:, slot, i:i + 1],
                                     accum_out=row_sum[:, slot, i:i + 1])
            ins.then_inc(exp_done, 1)

        def move_turned(n):
            act.wait_ge(turned, 2 * (n0 + n) + 1)
            act.activation(probs_t[:, 0, :], c.psum[:, TURN_BANK, :], ACT.Copy).then_inc(pt_act, 1)

        def body(i, last=False):
            for j in range(4):
                move_turned(4 * i + j)
                if not (last and j == 3):
                    exps(4 * i + j + 1, (j + 1) % 2)

        exps(0, 0)
        body(0)
        with act.Fori(1, B // 2 - 1) as i:
            body(i)
        body(B // 2 - 1, last=True)

    def vector(dve):
        weights.wait(dve)
        dve.wait_ge(mask_in, 16)
        if biased:
            dve.tensor_scalar(c.keep[:], mask[:], -1.0, 1.0, ALU.mult, ALU.add)\
               .then_inc(mask_ready, 1)
            dve.tensor_scalar(c.pad_bias[:], mask[:], PADDED, None, ALU.mult).then_inc(mask_ready, 1)
        else:
            dve.tensor_scalar(c.pad_bias[:], mask[:], 1.0, -L0_MASKED, ALU.subtract, ALU.mult)\
               .then_inc(mask_ready, 1)
        dve.wait_ge(mask_ready, 2 * use + 1)

        def max_rows(n, slot):
            dve.wait_ge(scores_done, n0 + n + 1)
            dve.tensor_reduce(neg_max[:, slot, :],
                              c.psum[:, 2 * slot:2 * slot + 2, :].rearrange("p a (h k) -> p (a h) k", h=2),
                              AX.X, ALU.max, negate=True).then_inc(max_done, 1)

        def move_k(b, half):
            dve.wait_ge(kv_done, 2 * (b0 + b) + 1)
            src = c.psum[:, KV_BANK, :].rearrange("p (m k) -> p m k", m=DC)
            if biased:
                for m in range(DC):
                    ins = dve.scalar_tensor_tensor(k_feat[half][:, m, :], src[:, m, :], cols[:, 1, m:m + 1],
                                                   c.keep[:, b, :], ALU.add, ALU.mult)
            else:
                ins = dve.tensor_copy(k_feat[half][:], src)
            ins.then_inc(kv_moved, 1)

        def move_v(b, half):
            dve.wait_ge(kv_done, 2 * (b0 + b) + 2)
            dve.tensor_copy(v_tok[half][:], c.psum[:, KV_BANK, :].rearrange("p (t d) -> p t d", t=KT))\
               .then_inc(kv_moved, 1)

        def move_turned(n):
            dve.wait_ge(turned, 2 * (n0 + n) + 2)
            dve.tensor_copy(probs_t[:, 1, :], c.psum[:, TURN_BANK + 1, :]).then_inc(pt_dve, 1)

        def normalize(n, slot):
            dve.wait_ge(exp_done, n0 + n + 1)
            dve.reciprocal(row_inv[:, slot, :], row_sum[:, slot, :]).then_inc(inv_ready, 1)
            dve.wait_ge(inv_ready, n0 + n + 1)
            for i in range(pairs):
                ins = dve.tensor_scalar(probs[slot][:, i, :], probs[slot][:, i, :], row_inv[:, slot, i:i + 1],
                                        None, ALU.mult)
            ins.then_inc(probs_ready, 1)

        def move_o(b):
            dve.wait_ge(pv_done, n0 + 2 * b + 2)
            src = c.psum[:, O_BANK, 0:DC * P].rearrange("p (m h q) -> p m h q", m=DC, h=2)
            for m in range(DC):
                bias = (cols[:, 2, m:m + 1], ALU.add) if biased else (None, ALU.bypass)
                ins = dve.tensor_scalar(o_half[:, m, :], src[:, m, 1, :], c.half_rows[:, 1:2], bias[0],
                                        ALU.mult, bias[1])
            ins.then_inc(half_ready, 1)
            dve.wait_ge(half_ready, b0 + b + 1)
            dve.scalar_tensor_tensor(c.o_feat[:, :, bass.ds(S * b, S)], src[:, :, 0, :], c.half_rows[:, 0:1],
                                     o_half[:], ALU.mult, ALU.add).then_inc(o_moved, 1)

        def body(i, last=False):
            for j in range(4):
                n, b, half = 4 * i + j, 2 * i + j // 2, j // 2
                if not (last and j == 3):
                    max_rows(n + 1, (j + 1) % 2)
                move_turned(n)
                if not (last and j >= 2):
                    if j % 2 == 0:
                        move_k(b + 1, 1 - half)
                    else:
                        move_v(b + 1, 1 - half)
                if not (last and j == 3):
                    normalize(n + 1, (j + 1) % 2)
                if j % 2 == 1:
                    move_o(b)

        move_k(0, 0)
        move_v(0, 0)
        max_rows(0, 0)
        normalize(0, 0)
        body(0)
        with dve.Fori(1, B // 2 - 1) as i:
            body(i)
        body(B // 2 - 1, last=True)

    def gpsimd(pool):
        pool.wait_ge(q_moved, 4 * (use + 1))
        pool.wait_ge(mask_ready, 2 * use + 1)

        def diagonal(b, half):
            pool.tensor_copy(pad_row[half][:], c.pad_bias[0:1, b, :]).then_inc(diag_ready, 1)
            for m in range(DC):
                pool.tensor_tensor(q_diag[half][:, m, :, :], bc(c.q_feat[:, m, bass.ds(S * b, S)], 1, 8),
                                   bc(c.head_rows[:], 2, S), ALU.mult).then_inc(diag_ready, 1)

        diagonal(0, 0)
        diagonal(1, 1)
        with pool.Fori(1, B // 2) as i:
            for half in range(2):
                b = 2 * i + half
                pool.wait_ge(scores_done, n0 + 2 * b - 2)
                diagonal(b, half)

    s.sync, s.tensor, s.scalar, s.vector, s.gpsimd = sync, tensor, scalar, vector, gpsimd
    out = out_projection(c, norm_use, out_use, c.o_feat, DC, wo, weights, [(o_moved, B * (use + 1))], bo)
    return [s, out]


def wide_attention(c, name, use, groups, weights_dram, xin, xin_ready, out, scale, positions,
                   scratch_free, first_units):
    s = Stage()
    scope = ExitStack()
    g0, r0 = first_units
    heads = 2
    unit_act = 6
    unit_dve = 4 if positions else 0
    w_tile = [c.sb(f"{name}_w{i}", [P, 3 * DC * P + 3], F32, scope) for i in range(2)]
    w = [t[:, 0:3 * DC * P].rearrange("p (a k n) -> p a k n", a=3, k=DC) for t in w_tile]
    bias = [t[:, 3 * DC * P:3 * DC * P + 3] for t in w_tile]
    w_pos = [c.sb(f"{name}_wp{i}", [P, P], F32, scope) for i in range(2)] if positions else None
    q_g = [c.sb(f"{name}_q{i}", [P, T], F32, scope) for i in range(2)]
    k_g = [c.sb(f"{name}_k{i}", [P, T], F32, scope) for i in range(2)]
    v_g = [c.sb(f"{name}_v{i}", [P, TT, P], F32, scope) for i in range(2)]
    r_g = [c.sb(f"{name}_r{i}", [P, heads, T], F32, scope) for i in range(2)] if positions else None
    x_paired = c.sb(f"{name}_xp", [P, DC, 4, 2, P], F32, scope)
    paired = c.sem("w_paired")
    probs = [c.sb(f"{name}_p{i}", [P, TT, S], F32, scope) for i in range(heads)]
    probs_t = [c.sb(f"{name}_pt{i}", [P, BANK], F32, scope) for i in range(heads)]
    neg_max = c.sb(f"{name}_nm", [P, heads, TT], F32, scope)
    row_sum = c.sb(f"{name}_rs", [P, heads, TT], F32, scope)
    scope.close()

    w_in = [c.sem("w_in0"), c.sem("w_in1")]
    act_done, dve_done = c.sem("w_act_units"), c.sem("w_dve_units")
    act_moved, dve_moved = c.sem("w_act_moved"), c.sem("w_dve_moved")
    scores_done, max_done, shifted = c.sem("w_scores_done"), c.sem("w_max_done"), c.sem("w_shifted")
    exp_done, sum_done, inv_done = c.sem("w_exp_done"), c.sem("w_sum_done"), c.sem("w_inv_done")
    probs_ready, turned = c.sem("w_probs_ready"), c.sem("w_turned")
    pt_moved = [c.sem("w_pt_moved0"), c.sem("w_pt_moved1")]
    pv_done, o_moved = c.sem("w_pv_done"), c.sem("w_o_moved")
    SCORE_BANK, UNIT_BANK, TURN_BANK, O_BANK = 0, 2, 4, 6

    def sync(sp):
        for sem, value in scratch_free:
            sp.wait_ge(sem, value)

        def load(g, slot):
            sp.dma_start(w_tile[slot][:], weights_dram[0][g]).then_inc(w_in[slot], 16)
            if positions:
                sp.dma_start(w_pos[slot][:], weights_dram[1][g]).then_inc(w_in[slot], 16)

        load(0, 0)
        load(1, 1)
        if groups > 2:
            with sp.Fori(1, groups // 2) as i:
                for slot in range(2):
                    sp.wait_ge(o_moved, 2 * (g0 + 2 * i + slot - 1))
                    load(2 * i + slot, slot)

    loads = 2 if positions else 1

    def loaded(pair):
        return c.wide_loads + 16 * loads * (pair + 1)

    base_loads = c.wide_loads

    def gpsimd(pool):
        for sem, value in xin_ready:
            pool.wait_ge(sem, value)
        for k in range(DC):
            src = xin[:, k, :].rearrange("p (q e o s) -> p o q e s", q=4, e=2, o=2)
            dst = x_paired[:, k].rearrange("p q o (e s) -> p o q e s", e=2)
            for parity in range(2):
                pool.tensor_copy(dst[:, parity], src[:, parity]).then_inc(paired, 1)

    def tensor(pe):
        for sem, value in xin_ready:
            pe.wait_ge(sem, value)

        def project(g, slot, pair, units):
            for u in units:
                if u == 0:
                    pe.wait_ge(w_in[slot], base_loads + 16 * loads * (pair + 1))
                bank = c.psum[:, UNIT_BANK + u % 2, :]
                if u < 2:
                    if positions:
                        wait_free(pe, dve_moved, unit_dve * (r0 + g) - 1 + u)
                    else:
                        wait_free(pe, act_moved, unit_act * (g0 + g) - 1 + u)
                elif u < unit_act + 2:
                    pe.wait_ge(act_moved, unit_act * (g0 + g) + u - 1)
                else:
                    pe.wait_ge(dve_moved, unit_dve * (r0 + g) + u - unit_act - 1)
                if u < 4:
                    a, n = divmod(u, 2)
                    for k in range(DC):
                        ins = pe.matmul(bank, w[slot][:, a, k, :], xin[:, k, n * BANK:(n + 1) * BANK],
                                        start=(k == 0), stop=(k == DC - 1))
                elif u < 6:
                    pe.wait_ge(paired, 4 * (use + 1))
                    for t in range(4):
                        quad, parity = divmod(4 * (u - 4) + t, 2)
                        for k in range(DC):
                            ins = pe.matmul(bank[:, t * P:(t + 1) * P], x_paired[:, k, quad, parity, :],
                                            w[slot][:, 2, k, :],
                                            start=(k == 0), stop=(k == DC - 1))
                else:
                    h, n = divmod(u - 6, 2)
                    rows = slice(h * S, (h + 1) * S)
                    ins = pe.matmul(bank, w_pos[slot][rows, :], q_g[slot][rows, n * BANK:(n + 1) * BANK],
                                    start=True, stop=True)
                ins.then_inc(act_done if u < 6 else dve_done, 1)

        def scores(g, slot):
            for h in range(heads):
                pe.wait_ge(act_moved, unit_act * (g0 + g + 1))
                if positions:
                    pe.wait_ge(dve_moved, unit_dve * (r0 + g + 1))
                wait_free(pe, shifted, heads * (g0 + g))
                bank = c.psum[:, SCORE_BANK + h, :]
                rows = slice(h * S, (h + 1) * S)
                if positions:
                    pe.matmul(bank.rearrange("p (t k) -> p t k", t=TT), c.identity_bf[:],
                              bc(positions.causal[:], 1, TT), start=True, stop=False, skip_group_check=True)
                    for t in range(TT):
                        pe.matmul(bank[:, t * S:(t + 1) * S], r_g[slot][:, h, t * P:(t + 1) * P],
                                  positions.key[:], start=False, stop=False, skip_group_check=True)
                for t in range(TT):
                    for half in range(2):
                        at = t * P + half * S
                        ins = pe.matmul(bank[half * S:(half + 1) * S, t * S:(t + 1) * S],
                                        q_g[slot][rows, at:at + S], k_g[slot][rows, at:at + S],
                                        start=not positions, stop=True, skip_group_check=bool(positions))
                ins.then_inc(scores_done, 1)

        def turn(g):
            for h in range(heads):
                pe.wait_ge(probs_ready, heads * (g0 + g) + h + 1)
                wait_free(pe, pt_moved[h], g0 + g)
                for quad in range(4):
                    ins = pe.transpose(c.psum[:, TURN_BANK + h, quad * P:(quad + 1) * P],
                                       probs[h][:, 2 * quad:2 * quad + 2, :].rearrange("p t k -> p (t k)"),
                                       c.identity[:])
                ins.then_inc(turned, 1)

        def turned_moved(g):
            for h in range(heads):
                pe.wait_ge(pt_moved[h], g0 + g + 1)
            wait_free(pe, o_moved, 2 * (g0 + g))

        def values(g, slot):
            for e in range(2):
                keys = slice(e * S, (e + 1) * S)
                for h in range(heads):
                    for quad in range(4):
                        for parity in range(2):
                            at = (2 * quad + parity) * S
                            ins = pe.matmul(c.psum[h * S:(h + 1) * S, O_BANK + e, at:at + S],
                                            v_g[slot][keys, 2 * quad + parity, h * S:(h + 1) * S],
                                            probs_t[h][keys, at:at + S], start=True, stop=True)
                ins.then_inc(pv_done, 1)

        def body(pair, last=False):
            for slot in range(2):
                g = 2 * pair + slot
                scores(g, slot)
                if not (last and slot == 1):
                    project(g + 1, 1 - slot, pair + slot, range(all_units - 1))
                turn(g)
                turned_moved(g)
                if not (last and slot == 1):
                    project(g + 1, 1 - slot, pair + slot, [all_units - 1])
                values(g, slot)

        all_units = unit_act + unit_dve
        project(0, 0, 0, range(all_units))
        if groups > 2:
            body(0)
            with pe.Fori(1, groups // 2 - 1) as i:
                body(i)
        body(groups // 2 - 1, last=True)

    def scalar(act):
        for sem, value in scratch_free:
            act.wait_ge(sem, value)

        early = unit_act if positions else unit_act - 1

        def move_units(g, slot, units):
            for u in units:
                act.wait_ge(act_done, unit_act * (g0 + g) + u + 1)
                bank, n = c.psum[:, UNIT_BANK + u % 2, :], u % 2
                if u < 4:
                    dst = (q_g, k_g)[u // 2][slot][:, n * BANK:(n + 1) * BANK]
                    act.activation(dst, bank, ACT.Identity, scale=scale,
                                   bias=bias[slot][:, u // 2:u // 2 + 1]).then_inc(act_moved, 1)
                else:
                    act.activation(v_g[slot][:, 4 * n:4 * n + 4, :], bank.rearrange("p (t d) -> p t d", t=4),
                                   ACT.Copy, scale=scale).then_inc(act_moved, 1)

        def exps(g):
            for h in range(heads):
                act.wait_ge(shifted, heads * (g0 + g) + h + 1)
                act.activation(probs[h][:], probs[h][:], ACT.Exp, scale=0.125).then_inc(exp_done, 1)

        def move_turned(g):
            for h in range(heads):
                act.wait_ge(turned, heads * (g0 + g) + h + 1)
                act.activation(probs_t[h][:], c.psum[:, TURN_BANK + h, :], ACT.Copy).then_inc(pt_moved[h], 1)

        def body(pair, last=False):
            for slot in range(2):
                g = 2 * pair + slot
                more = not (last and slot == 1)
                exps(g)
                if more:
                    move_units(g + 1, 1 - slot, range(early))
                move_turned(g)
                if more:
                    move_units(g + 1, 1 - slot, range(early, unit_act))

        move_units(0, 0, range(unit_act))
        if groups > 2:
            body(0)
            with act.Fori(1, groups // 2 - 1) as i:
                body(i)
        body(groups // 2 - 1, last=True)

    def vector(dve):
        for sem, value in scratch_free:
            dve.wait_ge(sem, value)

        def move_units(g, slot):
            for u in range(unit_dve):
                h, n = divmod(u, 2)
                dve.wait_ge(dve_done, unit_dve * (r0 + g) + u + 1)
                dve.tensor_tensor(r_g[slot][:, h, n * BANK:(n + 1) * BANK].rearrange("p (b q) -> p b q", q=S),
                                  c.psum[:, UNIT_BANK + u % 2, :].rearrange("p (b q) -> p b q", q=S),
                                  bc(positions.query[:], 1, BANK // S), ALU.mult).then_inc(dve_moved, 1)

        def softmax_head(g, h):
            src = c.psum[:, SCORE_BANK + h, :].rearrange("p (t k) -> p t k", t=TT)
            n = heads * (g0 + g) + h + 1
            dve.wait_ge(scores_done, n)
            dve.tensor_reduce(neg_max[:, h, :], src, AX.X, ALU.max, negate=True).then_inc(max_done, 1)
            dve.wait_ge(max_done, n)
            dve.tensor_tensor(probs[h][:], src, bc(neg_max[:, h, :], 2, S), ALU.add).then_inc(shifted, 1)

        def softmax_tail(g, h):
            n = heads * (g0 + g) + h + 1
            dve.wait_ge(exp_done, n)
            dve.tensor_reduce(row_sum[:, h, :], probs[h][:], AX.X, ALU.add).then_inc(sum_done, 1)
            dve.wait_ge(sum_done, n)
            dve.reciprocal(row_sum[:, h, :], row_sum[:, h, :]).then_inc(inv_done, 1)
            dve.wait_ge(inv_done, n)
            dve.tensor_tensor(probs[h][:], probs[h][:], bc(row_sum[:, h, :], 2, S), ALU.mult)\
               .then_inc(probs_ready, 1)

        def move_o(g, slot):
            for e in range(2):
                dve.wait_ge(pv_done, 2 * (g0 + g) + e + 1)
                dst = out[:, g, :].rearrange("p (q e n) -> p e q n", e=2, n=P)[:, e]
                src = c.psum[:, O_BANK + e, :].rearrange("p (q n) -> p q n", n=P)
                dve.tensor_scalar(dst, src, 1.0, bias[slot][:, 2:3], ALU.mult, ALU.add).then_inc(o_moved, 1)

        def body(pair, last=False):
            for slot in range(2):
                g = 2 * pair + slot
                softmax_head(g, 0)
                softmax_head(g, 1)
                softmax_tail(g, 0)
                softmax_tail(g, 1)
                if not (last and slot == 1):
                    move_units(g + 1, 1 - slot)
                move_o(g, slot)

        move_units(0, 0)
        if groups > 2:
            body(0)
            with dve.Fori(1, groups // 2 - 1) as i:
                body(i)
        body(groups // 2 - 1, last=True)

    c.wide_loads += 16 * loads * (groups // 2)
    s.gpsimd = gpsimd
    s.sync, s.tensor, s.scalar, s.vector = sync, tensor, scalar, vector
    return s, (o_moved, 2 * (g0 + groups))


class Positions:
    pass


def first_self_attention(c, dram, norm_use, out_use):
    groups, heads_out = 8, 8
    fan = 1024
    qkv_scale = (3.0 * D * 64 * 16) ** -0.25
    out_scale = (float(fan) * D) ** -0.25
    prep = Stage()
    weights = Loads(c, "a0_weights", 5)
    prepared = c.sem("a0_prepared")
    x_ready = c.sem("x_ready")
    scope = ExitStack()
    pos = Positions()
    wo = c.sb("a0_wo", [P, heads_out, D], F32, scope)
    bo = c.sb("a0_bo", [P, D], F32, scope)
    o8 = c.sb("a0_o", [P, groups, T], F32, scope)
    pos.query = c.sb("a0_query", [P, S], F32, scope)
    pos.key = c.sb("a0_key", [P, S], F32, scope)
    pos.causal = c.sb("a0_causal", [P, S], BF16, scope)
    causal32 = c.sb("a0_causal32", [P, S], F32, scope)

    def sync(sp):
        sp.wait_ge(x_ready, TT * norm_use)
        weights.dma(sp, pos.query[:], dram["pos_query"])
        weights.dma(sp, pos.key[:], dram["pos_key"])
        weights.dma(sp, causal32[:], dram["causal"])
        weights.dma(sp, bo[:], bc(dram["L0_attn_out_bias"], 0, P))
        weights.dma(sp, wo[:], dram["L0_attn_out_kernel"].rearrange("(k p) n -> p k n", p=P))

    def gpsimd(pool):
        weights.wait(pool)
        pool.tensor_copy(pos.causal[:], causal32[:]).then_inc(prepared, 1)
        pool.tensor_scalar(wo[:], wo[:], out_scale, None, ALU.mult).then_inc(prepared, 1)

    def vector(dve):
        weights.wait(dve)

    prep.sync, prep.gpsimd, prep.vector = sync, gpsimd, vector
    ready = [(c.sem("feat_act"), 2 * (norm_use + 1)), (c.sem("feat_dve"), 2 * (norm_use + 1)),
             (prepared, 2), (weights.sem, weights.total)]
    core, done = nested(c, scope, lambda: wide_attention(
        c, "a0", 0, groups, (dram["L0_attn_w"], dram["L0_attn_pos"]), c.xn_feat, ready, o8,
        qkv_scale, pos,
        [(x_ready, TT * norm_use)], (0, 0)))
    out = out_projection(c, norm_use, out_use, o8, groups, wo, weights, [done, (prepared, 2)], bo)
    return [prep, core, out]


def nested(c, scope, make):
    result = make()
    scope.close()
    return result


def narrow_attention(c, q_scaled, k_all, v_w, v_cols, inputs_ready, norm_use, diag_base, scratch_scope):
    s = Stage()
    pairs = 8
    xb = [c.sb(f"n_x{i}", [P, DC, 2, S], F32, scratch_scope) for i in range(2)]
    q_diag = [c.sb(f"n_qd{i}", [P, DC, 8, S], F32, scratch_scope) for i in range(2)]
    v2 = [c.sb(f"n_v{i}", [P, D], F32, scratch_scope) for i in range(2)]
    probs = [c.sb(f"n_p{i}", [P, pairs, S], F32, scratch_scope) for i in range(2)]
    probs_t = c.sb("n_pt", [P, BANK], F32, scratch_scope)
    neg_max = c.sb("n_nm", [P, 2, pairs], F32, scratch_scope)
    row_sum = c.sb("n_rs", [P, 2, pairs], F32, scratch_scope)
    o_half = c.sb("n_oh", [P, DC, S], F32, scratch_scope)
    copies, scores_done, max_done = c.sem("n_copies"), c.sem("n_scores_done"), c.sem("n_max_done")
    shifted, exp_done, sum_done = c.sem("n_shifted"), c.sem("n_exp_done"), c.sem("n_sum_done")
    inv_done, probs_ready, turned = c.sem("n_inv_done"), c.sem("n_probs_ready"), c.sem("n_turned")
    pt_moved, v_done, v_moved = c.sem("n_pt_moved"), c.sem("n_v_done"), c.sem("n_v_moved")
    pv_done, half_ready, o_moved = c.sem("n_pv_done"), c.sem("n_half_ready"), c.sem("n_o_moved")
    V_BANK, TURN_BANK, O_BANK = 4, 5, 6

    def gpsimd(pool):
        for sem, value in inputs_ready:
            pool.wait_ge(sem, value)

        def copy_in(b, half):
            pool.tensor_copy(xb[half][:], bc(c.xn_feat[:, :, bass.ds(S * b, S)], 2, 2)).then_inc(copies, 1)
            for m in range(DC):
                pool.tensor_tensor(q_diag[half][:, m, :, :], bc(q_scaled[:, m, bass.ds(S * b, S)], 1, 8),
                                   bc(c.head_rows[:], 2, S), ALU.mult).then_inc(copies, 1)

        copy_in(0, 0)
        copy_in(1, 1)
        with pool.Fori(1, B // 2) as i:
            for half in range(2):
                b = 2 * i + half
                pool.wait_ge(scores_done, b - 1)
                pool.wait_ge(v_done, b - 1)
                copy_in(b, half)

    def tensor(pe):
        for sem, value in inputs_ready:
            pe.wait_ge(sem, value)

        def scores(b, half):
            pe.wait_ge(copies, 3 * b + 3)
            wait_free(pe, shifted, b - 1)
            for i in range(pairs):
                m, j = divmod(i, 4)
                ins = pe.matmul(c.psum[:, half, i * S:(i + 1) * S],
                                q_diag[half][:, m, 2 * j:2 * j + 2, :].rearrange("p j q -> p (j q)"),
                                k_all[:, m, bass.ds(S * b, S)], start=True, stop=True)
            ins.then_inc(scores_done, 1)

        def project_v(b, half, before_last=lambda: None):
            wait_free(pe, v_moved, b)
            for k in range(DC):
                if k == DC - 1:
                    before_last()
                ins = pe.matmul(c.psum[:, V_BANK, 0:D], xb[half][:, k, :, :].rearrange("p a s -> p (a s)"),
                                v_w[:, k, :], start=(k == 0), stop=(k == DC - 1))
            ins.then_inc(v_done, 1)

        def turn(b, half):
            pe.wait_ge(probs_ready, b + 1)
            wait_free(pe, pt_moved, b)
            for u in range(pairs // 2):
                ins = pe.transpose(c.psum[:, TURN_BANK, u * P:(u + 1) * P],
                                   probs[half][:, 2 * u:2 * u + 2, :].rearrange("p t k -> p (t k)"),
                                   c.identity[:])
            ins.then_inc(turned, 1)

        def values_ready(b):
            pe.wait_ge(pt_moved, b + 1)
            pe.wait_ge(v_moved, b + 1)
            wait_free(pe, o_moved, b)

        def values(b, half):
            for i in range(pairs):
                m, j = divmod(i, 4)
                u, rows = i // 2, slice((i % 2) * S, (i % 2 + 1) * S)
                ins = pe.matmul(c.psum[32 * j:32 * j + 32, O_BANK, m * P:(m + 1) * P],
                                v2[half][rows, 32 * i:32 * i + 32], probs_t[rows, u * P:(u + 1) * P],
                                start=True, stop=True)
            ins.then_inc(pv_done, 1)

        def body(i, last=False):
            for half in range(2):
                b = 2 * i + half
                more = not (last and half == 1)
                if more:
                    scores(b + 1, 1 - half)
                turn(b, half)
                if more:
                    project_v(b + 1, 1 - half, before_last=lambda: values_ready(b))
                else:
                    values_ready(b)
                values(b, half)

        scores(0, 0)
        project_v(0, 0)
        body(0)
        with pe.Fori(1, B // 2 - 1) as i:
            body(i)
        body(B // 2 - 1, last=True)

    def scalar(act):
        for sem, value in inputs_ready:
            act.wait_ge(sem, value)

        def exps(b, half):
            act.wait_ge(shifted, b + 1)
            act.activation(probs[half][:], probs[half][:], ACT.Exp).then_inc(exp_done, 1)

        def move_v(b, half):
            act.wait_ge(v_done, b + 1)
            act.activation(v2[half][:], c.psum[:, V_BANK, 0:D], ACT.Copy).then_inc(v_moved, 1)

        def move_turned(b):
            act.wait_ge(turned, b + 1)
            act.activation(probs_t[:], c.psum[:, TURN_BANK, :], ACT.Copy).then_inc(pt_moved, 1)

        def body(i, last=False):
            for half in range(2):
                b = 2 * i + half
                move_turned(b)
                if not (last and half == 1):
                    exps(b + 1, 1 - half)
                    move_v(b + 1, 1 - half)

        exps(0, 0)
        move_v(0, 0)
        body(0)
        with act.Fori(1, B // 2 - 1) as i:
            body(i)
        body(B // 2 - 1, last=True)

    def vector(dve):
        for sem, value in inputs_ready:
            dve.wait_ge(sem, value)

        def softmax(b, half):
            src = c.psum[:, half, :].rearrange("p (t k) -> p t k", t=pairs)
            dve.wait_ge(scores_done, b + 1)
            dve.tensor_reduce(neg_max[:, half, :], src, AX.X, ALU.max, negate=True).then_inc(max_done, 1)
            dve.wait_ge(max_done, b + 1)
            dve.tensor_tensor(probs[half][:], src, bc(neg_max[:, half, :], 2, S), ALU.add).then_inc(shifted, 1)

        def normalize(b, half):
            dve.wait_ge(exp_done, b + 1)
            dve.tensor_reduce(row_sum[:, half, :], probs[half][:], AX.X, ALU.add).then_inc(sum_done, 1)
            dve.wait_ge(sum_done, b + 1)
            dve.reciprocal(row_sum[:, half, :], row_sum[:, half, :]).then_inc(inv_done, 1)
            dve.wait_ge(inv_done, b + 1)
            dve.tensor_tensor(probs[half][:], probs[half][:], bc(row_sum[:, half, :], 2, S), ALU.mult)\
               .then_inc(probs_ready, 1)

        def move_o(b):
            dve.wait_ge(pv_done, b + 1)
            src = c.psum[:, O_BANK, 0:DC * P].rearrange("p (m h q) -> p m h q", m=DC, h=2)
            for m in range(DC):
                ins = dve.tensor_scalar(o_half[:, m, :], src[:, m, 1, :], c.half_rows[:, 1:2],
                                        v_cols[:, m:m + 1], ALU.mult, ALU.add)
            ins.then_inc(half_ready, 1)
            dve.wait_ge(half_ready, b + 1)
            dve.scalar_tensor_tensor(c.o_feat[:, :, bass.ds(S * b, S)], src[:, :, 0, :], c.half_rows[:, 0:1],
                                     o_half[:], ALU.mult, ALU.add).then_inc(o_moved, 1)

        def body(i, last=False):
            for half in range(2):
                b = 2 * i + half
                if not (last and half == 1):
                    softmax(b + 1, 1 - half)
                    normalize(b + 1, 1 - half)
                move_o(b)

        softmax(0, 0)
        normalize(0, 0)
        body(0)
        with dve.Fori(1, B // 2 - 1) as i:
            body(i)
        body(B // 2 - 1, last=True)

    s.gpsimd, s.tensor, s.scalar, s.vector = gpsimd, tensor, scalar, vector
    return s, (o_moved, B)


def feature_projection(c, name, weight, xin, ready, move, move_act):
    s = Stage()
    done = c.sem(f"{name}_done")

    def tensor(pe):
        for sem, value in ready:
            pe.wait_ge(sem, value)
        for u in range(DC * NH):
            m, n = divmod(u, NH)
            for k in range(DC):
                ins = pe.matmul(c.psum[:, u, :], weight[:, k, m * P:(m + 1) * P],
                                xin[:, k, n * BANK:(n + 1) * BANK], start=(k == 0), stop=(k == DC - 1))
            ins.then_inc(done, 1)

    def scalar(act):
        for u in range(DC * NH):
            act.wait_ge(done, u + 1)
            move_act(act, u, c.psum[:, u, :])

    def vector(dve):
        for u in range(DC * NH):
            move(dve, u)

    s.tensor, s.scalar, s.vector = tensor, scalar, vector
    return s


def second_self_attention(c, dram, norm_use, out_use):
    weights = Loads(c, "a1_weights", 12)
    x_ready, prepared = c.sem("x_ready"), c.sem("a1_prepared")
    scope = ExitStack()
    names = ["Wq", "Wk", "Wv", "Wo", "gate", "ca_Wout", "mc_Wout"]
    w = {n: c.sb(f"a1_{n}", [P, DC, D], F32, scope) for n in names}
    cols = c.sb("a1_cols", [P, 6, DC], F32, scope)
    am_w = c.sb("a1_am_w", [16, D], F32, scope)
    cons = c.sb("a1_cons", [16, 1], F32, scope)
    bo = c.sb("a1_bo", [P, D], F32, scope)
    gate = c.sb("a1_gate_value", [P, DC, T], F32, scope)
    k_all = c.sb("a1_k", [P, DC, T], F32, scope)
    mixed = c.sb("a1_mixed", [P, DC, T], F32, scope)
    inner = c.sb("a1_inner", [P, DC, T], F32, scope)
    o_wide = c.sb("a1_o_wide", [P, DC, T], F32, scope)
    neg_gate = c.sb("a1_neg_gate", [P, DC], F32, scope)
    gate_bias_done = c.sem("a1_gate_bias")
    stages = []

    prep = Stage()

    def sync(sp):
        sp.wait_ge(x_ready, TT * norm_use)
        weights.dma(sp, cols[:], dram["a1_cols"])
        weights.dma(sp, am_w[:], dram["am_w"])
        weights.dma(sp, cons[:], dram["L1_attn_cons_vec"].rearrange("(n a) -> n a", a=1))
        weights.dma(sp, bo[:], bc(dram["L1_attn_bo"], 0, P))
        for n in names:
            src = "a1_gate" if n == "gate" else f"L1_attn_{n}"
            weights.dma(sp, w[n][:], dram[src].rearrange("(k p) n -> p k n", p=P))
        weights.dma(sp, neg_gate[:], dram["am_b_cols"])

    def tensor(pe):
        weights.wait(pe)
        for m in range(DC):
            ins = pe.matmul(c.psum[:, 7, m:m + 1], am_w[:, m * P:(m + 1) * P], cons[:],
                            start=True, stop=True)
        ins.then_inc(gate_bias_done, 1)

    def gpsimd(pool):
        weights.wait(pool)
        pool.tensor_scalar(cols[:, 4, :], cols[:, 4, :], CAUSAL_W, None, ALU.mult).then_inc(prepared, 1)
        pool.tensor_scalar(cols[:, 5, :], cols[:, 5, :], META_W, None, ALU.mult).then_inc(prepared, 1)

    def vector(dve):
        weights.wait(dve)
        dve.wait_ge(gate_bias_done, 1)
        dve.tensor_tensor(cols[:, 3, :], c.psum[:, 7, 0:DC], cols[:, 3, :], ALU.add).then_inc(prepared, 1)
        dve.wait_ge(prepared, 3)
        dve.tensor_tensor(neg_gate[:], cols[:, 3, :], neg_gate[:], ALU.add).then_inc(prepared, 1)
        dve.wait_ge(prepared, 4)
        dve.tensor_scalar(neg_gate[:], neg_gate[:], -1.0, None, ALU.mult).then_inc(prepared, 1)

    def scalar(act):
        act.wait_ge(prepared, 5)

    prep.sync, prep.tensor, prep.gpsimd, prep.vector, prep.scalar = sync, tensor, gpsimd, vector, scalar
    stages.append(prep)

    feat = [(c.sem("feat_act"), 2 * (norm_use + 1)), (c.sem("feat_dve"), 2 * (norm_use + 1)),
            (weights.sem, weights.total)]
    proj = Stage()
    p_done, p_moved = c.sem("a1_p_done"), c.sem("a1_p_moved")
    plus_one, gate_done, q_gated = c.sem("a1_plus_one"), c.sem("a1_gate_done"), c.sem("a1_q_gated")
    jobs = [("gate", gate), ("Wq", c.q_feat), ("Wk", k_all)]
    units = DC * NH

    def tensor(pe):
        for sem, value in feat:
            pe.wait_ge(sem, value)
        for a, (n, _) in enumerate(jobs):
            for u in range(units):
                m, h = divmod(u, NH)
                v = a * units + u
                if v >= 4:
                    pe.wait_ge(p_moved, v - 3)
                for k in range(DC):
                    ins = pe.matmul(c.psum[:, v % 4, :], w[n][:, k, m * P:(m + 1) * P],
                                    c.xn_feat[:, k, h * BANK:(h + 1) * BANK],
                                    start=(k == 0), stop=(k == DC - 1))
                ins.then_inc(p_done, 1)

    def scalar(act):
        for a, (n, dst) in enumerate(jobs):
            for u in range(units):
                m, h = divmod(u, NH)
                v = a * units + u
                act.wait_ge(p_done, v + 1)
                out = dst[:, m, h * BANK:(h + 1) * BANK]
                if n == "gate":
                    act.activation(out, c.psum[:, v % 4, :], ACT.Exp, scale=-1.0,
                                   bias=neg_gate[:, m:m + 1]).then_inc(p_moved, 1)
                else:
                    act.activation(out, c.psum[:, v % 4, :], ACT.Identity,
                                   bias=cols[:, a - 1, m:m + 1]).then_inc(p_moved, 1)

    def vector(dve):
        for m in range(DC):
            dve.wait_ge(p_moved, NH * (m + 1))
            dve.tensor_scalar(gate[:, m, :], gate[:, m, :], 1.0, None, ALU.add).then_inc(plus_one, 1)
            dve.wait_ge(plus_one, m + 1)
            dve.reciprocal(gate[:, m, :], gate[:, m, :]).then_inc(gate_done, 1)
        for m in range(DC):
            dve.wait_ge(gate_done, m + 1)
            dve.wait_ge(p_moved, units + NH * (m + 1))
            dve.tensor_tensor(c.q_feat[:, m, :], c.q_feat[:, m, :], gate[:, m, :], ALU.mult)\
               .then_inc(q_gated, 1)

    proj.tensor, proj.scalar, proj.vector = tensor, scalar, vector
    stages.append(proj)

    narrow_scope = ExitStack()
    core, main_done = narrow_attention(
        c, c.q_feat, k_all, w["Wv"], cols[:, 2, :], feat + [(q_gated, DC), (p_moved, 3 * units), (prepared, 5)],
        norm_use, None, narrow_scope)
    narrow_scope.close()
    stages.append(core)

    ca, ca_done = wide_attention(
        c, "ca", 1, DC, (dram["ca_w"],), c.xn_feat, feat + [main_done], o_wide, 1.0,
        None, [main_done], (8, 8))
    stages.append(ca)

    ca_moved, mixed_done = c.sem("ca_out_moved"), c.sem("mixed_done")

    def take(sem, dst, column, factor):
        def move_act(act, u, bank):
            m, n = divmod(u, NH)
            act.activation(dst[:, m, n * BANK:(n + 1) * BANK], bank, ACT.Identity, scale=factor,
                           bias=cols[:, column, m:m + 1]).then_inc(sem, 1)
        return move_act

    def mix(dst, old, added, sem, factor, done):
        def move(dve, u):
            m, n = divmod(u, NH)
            at = slice(n * BANK, (n + 1) * BANK)
            dve.wait_ge(sem, u + 1)
            dve.scalar_tensor_tensor(dst[:, m, at], old[:, m, at], 1.0 - factor, added[:, m, at],
                                     ALU.mult, ALU.add).then_inc(done, 1)
        return move

    stages.append(feature_projection(c, "ca_out", w["ca_Wout"], o_wide, [ca_done],
                                     mix(mixed, c.o_feat, inner, ca_moved, CAUSAL_W, mixed_done),
                                     take(ca_moved, inner, 4, CAUSAL_W)))
    mc, mc_done = wide_attention(
        c, "mc", 2, DC, (dram["mc_w"],), mixed, [(mixed_done, 4)], o_wide, 1.0,
        None, [(mixed_done, 4)], (10, 8))
    stages.append(mc)
    mc_moved, final_done = c.sem("mc_out_moved"), c.sem("final_done")
    stages.append(feature_projection(c, "mc_out", w["mc_Wout"], o_wide, [mc_done],
                                     mix(k_all, mixed, inner, mc_moved, META_W, final_done),
                                     take(mc_moved, inner, 5, META_W)))
    scope.close()
    stages.append(out_projection(c, norm_use, out_use, k_all, DC, w["Wo"], weights, [(final_done, 4)], bo))
    return stages


def quantized_ffn(c, dram, norm_use, stat_use):
    s = Stage()
    scope = ExitStack()
    loads = Loads(c, "f_loads", 8)
    raw = [c.sb("f_raw1", [P, DC, HID], F32, scope), c.sb("f_raw2", [P, HC, D], F32, scope)]
    ternary = [c.sb("f_w1", [P, DC, HID], BF16, scope), c.sb("f_w2", [P, HC, D], BF16, scope)]
    g1, b1n = c.sb("f_g1", [P, D], F32, scope), c.sb("f_b1n", [P, D], F32, scope)
    g2, b2n = c.sb("f_g2", [P, HID], F32, scope), c.sb("f_b2n", [P, HID], F32, scope)
    bias1, bias2 = c.sb("f_bias1", [P, HID], F32, scope), c.sb("f_bias2", [P, D], F32, scope)
    asum = c.sb("f_asum", [P, 2], F32, scope)
    w_mean, w_inv = c.sb("f_wmean", [P, 2], F32, scope), c.sb("f_winv", [P, 2], F32, scope)
    top = c.sb("f_top", [P, 2, TT], F32, scope)
    q_scale, back = c.sb("f_qscale", [P, 2, TT], F32, scope), c.sb("f_back", [P, 2, TT], F32, scope)
    x1 = c.sb("f_x1", [P, TT, D], F32, scope)
    x1_feat = c.sb("f_x1_feat", [P, DC, T], BF16, scope)
    hid = c.sb("f_hid", [P, TT, HID], F32, scope)
    hid_feat = [c.sb(f"f_hid_feat{i}", [P, HC, P], BF16, scope) for i in range(2)]
    scope.close()
    x_ready, xn_ready = c.sem("x_ready"), c.sem("xn_ready")
    sems = c.sem("stats_done"), c.sem("aggr_done"), c.sem("var_eps")
    step = c.sem("f_step")
    asum_done, total_done = c.sem("f_asum_done"), c.sem("f_total_done")
    q1_ready, q1_turned, q1_moved = c.sem("f_q1_ready"), c.sem("f_q1_turned"), c.sem("f_q1_moved")
    up_done, up_moved, gelu_done = c.sem("f_up_done"), c.sem("f_up_moved"), c.sem("f_gelu_done")
    q2_ready, q2_turned, q2_moved = c.sem("f_q2_ready"), c.sem("f_q2_turned"), c.sem("f_q2_moved")
    down_done, f_bias_added = c.sem("f_down_done"), c.sem("f_bias_added")

    def sync(sp):
        sp.wait_ge(x_ready, TT * norm_use)
        loads.dma(sp, raw[0][:], dram["w1_t"].rearrange("(k p) n -> p k n", p=P))
        loads.dma(sp, raw[1][:], dram["w2_t"].rearrange("(k p) n -> p k n", p=P))
        for dst, name in ((g1, "ln1_g"), (b1n, "ln1_b"), (g2, "ln2_g"), (b2n, "ln2_b"), (bias1, "b1"),
                          (bias2, "b2")):
            loads.dma(sp, dst[:], bc(dram[f"L0_ffn_{name}"], 0, P))

    def gpsimd(pool):
        loads.wait(pool)
        pool.wait_ge(xn_ready, TT * (norm_use + 1))
        pool.tensor_tensor(c.x_tok[:], c.x_tok[:], bc(bias2[:], 1, TT), ALU.add).then_inc(f_bias_added, 1)

    def vector(dve):
        count = [0]

        def after(ins):
            count[0] += 1
            ins.then_inc(step, 1)
            dve.wait_ge(step, count[0])

        loads.wait(dve)
        for a in range(2):
            dve.tensor_reduce(asum[:, a:a + 1], raw[a][:], AX.XY, ALU.add, apply_absolute_value=True)\
               .then_inc(asum_done, 1)
        dve.wait_ge(total_done, 1)
        after(dve.tensor_scalar(w_mean[:], c.psum[:, 7, 0:2], 1.0 / (D * HID), 1e-5, ALU.mult, ALU.max))
        after(dve.reciprocal(w_inv[:], w_mean[:]))
        for a in range(2):
            after(dve.tensor_scalar(raw[a][:], raw[a][:], w_inv[:, a:a + 1], ROUND, ALU.mult, ALU.add))
            after(dve.tensor_scalar(raw[a][:], raw[a][:], ROUND, 1.0, ALU.subtract, ALU.min))
            after(dve.tensor_scalar(ternary[a][:], raw[a][:], -1.0, None, ALU.max))

        def scales(a):
            after(dve.tensor_scalar(top[:, a, :], top[:, a, :], 1e-5, None, ALU.max))
            after(dve.reciprocal(q_scale[:, a, :], top[:, a, :]))
            after(dve.tensor_scalar(q_scale[:, a, :], q_scale[:, a, :], 127.0, None, ALU.mult))
            after(dve.tensor_scalar(back[:, a, :], top[:, a, :], w_mean[:, a:a + 1], 1.0 / 127.0,
                                    ALU.mult, ALU.mult))

        dve.wait_ge(xn_ready, TT * (norm_use + 1))
        statistics(c, dve, lambda t, h: c.xn_tok[:, t, :], 1, stat_use, sems)
        rstd_vector(c, dve, stat_use)
        for t in range(TT):
            ins = dve.scalar_tensor_tensor(x1[:, t, :], c.xn_tok[:, t, :], c.mean_var[:, t, 0:1], g1[:],
                                           ALU.subtract, ALU.mult)
        after(ins)
        for t in range(TT):
            ins = dve.scalar_tensor_tensor(x1[:, t, :], x1[:, t, :], c.rstd[:, t:t + 1], b1n[:],
                                           ALU.mult, ALU.add)
        after(ins)
        after(dve.tensor_reduce(top[:, 0, :], x1[:], AX.X, ALU.max, apply_absolute_value=True))
        scales(0)
        for t in range(TT):
            ins = dve.tensor_scalar(x1[:, t, :], x1[:, t, :], q_scale[:, 0, t:t + 1], ROUND, ALU.mult, ALU.add)
        after(ins)
        for t in range(TT):
            dve.tensor_scalar(x1[:, t, :], x1[:, t, :], ROUND, 127.0, ALU.subtract, ALU.min)\
               .then_inc(q1_ready, 1)
        for t in range(TT):
            dve.wait_ge(up_done, t + 1)
            src = c.psum[:, 4 + 2 * (t % 2):6 + 2 * (t % 2), :]
            dve.scalar_tensor_tensor(hid[:, t, :].rearrange("p (a n) -> p a n", a=2), src, back[:, 0, t:t + 1],
                                     bias1[:].rearrange("p (a n) -> p a n", a=2), ALU.mult, ALU.add)\
               .then_inc(up_moved, 1)
        dve.wait_ge(gelu_done, TT)
        statistics(c, dve, lambda t, h: hid[:, t, h * BANK:(h + 1) * BANK], 2, stat_use + 1, sems)
        rstd_vector(c, dve, stat_use + 1)
        for t in range(TT):
            ins = dve.scalar_tensor_tensor(hid[:, t, :], hid[:, t, :], c.mean_var[:, t, 0:1], g2[:],
                                           ALU.subtract, ALU.mult)
        after(ins)
        for t in range(TT):
            ins = dve.scalar_tensor_tensor(hid[:, t, :], hid[:, t, :], c.rstd[:, t:t + 1], b2n[:],
                                           ALU.mult, ALU.add)
        after(ins)
        after(dve.tensor_reduce(top[:, 1, :], hid[:], AX.X, ALU.max, apply_absolute_value=True))
        scales(1)
        for t in range(TT):
            after(dve.tensor_scalar(hid[:, t, :], hid[:, t, :], q_scale[:, 1, t:t + 1], ROUND, ALU.mult, ALU.add))
            dve.tensor_scalar(hid[:, t, :], hid[:, t, :], ROUND, 127.0, ALU.subtract, ALU.min)\
               .then_inc(q2_ready, 1)
        dve.wait_ge(f_bias_added, 1)
        for t in range(TT):
            dve.wait_ge(down_done, t + 1)
            dve.scalar_tensor_tensor(c.x_tok[:, t, :], c.psum[:, 4 + t % 4, 0:D], back[:, 1, t:t + 1],
                                     c.x_tok[:, t, :], ALU.mult, ALU.add).then_inc(x_ready, 1)

    def scalar(act):
        rstd_scalar(c, act, sems[2], stat_use + 1, stat_use)
        for k in range(TT // 2):
            act.wait_ge(q1_turned, k + 1)
            act.activation(x1_feat[:, :, 2 * P * k:2 * P * (k + 1)],
                           c.psum[:, k, :].rearrange("p (c n) -> p c n", c=DC), ACT.Copy).then_inc(q1_moved, 1)
        for t in range(TT):
            act.wait_ge(up_moved, t + 1)
            act.activation(hid[:, t, :], hid[:, t, :], ACT.Gelu).then_inc(gelu_done, 1)
        rstd_scalar(c, act, sems[2], stat_use + 2, stat_use + 1)
        for t in range(TT):
            for a in range(2):
                act.wait_ge(q2_turned, 2 * t + a + 1)
                if t >= 2:
                    act.wait_ge(down_done, t - 1)
                act.activation(hid_feat[t % 2][:, 4 * a:4 * a + 4, :],
                               c.psum[:, 2 * (t % 2) + a, :].rearrange("p (k n) -> p k n", k=4), ACT.Copy)\
                   .then_inc(q2_moved, 1)

    def tensor(pe):
        pe.wait_ge(asum_done, 2)
        pe.matmul(c.psum[:, 7, 0:2], c.ones[:], asum[:], start=True, stop=True).then_inc(total_done, 1)
        wait_feat(c, pe, norm_use)
        for t in range(TT):
            pe.wait_ge(q1_ready, t + 1)
            bank = c.psum[:, t // 2, :].rearrange("p (c n) -> p c n", c=DC)
            for m in range(DC):
                ins = pe.transpose(bank[:, m, (t % 2) * P:(t % 2 + 1) * P], x1[:, t, m * P:(m + 1) * P],
                                   c.identity[:])
            if t % 2:
                ins.then_inc(q1_turned, 1)
        for t in range(TT):
            pe.wait_ge(q1_moved, t // 2 + 1)
            if t >= 2:
                pe.wait_ge(up_moved, t - 1)
            for n in range(2):
                for k in range(DC):
                    ins = pe.matmul(c.psum[:, 4 + 2 * (t % 2) + n, :], x1_feat[:, k, t * P:(t + 1) * P],
                                    ternary[0][:, k, n * BANK:(n + 1) * BANK],
                                    start=(k == 0), stop=(k == DC - 1))
            ins.then_inc(up_done, 1)
        pe.wait_ge(up_moved, TT)

        def turn(t):
            pe.wait_ge(q2_ready, t + 1)
            if t >= 2:
                pe.wait_ge(q2_moved, 2 * (t - 1))
            for a in range(2):
                for k in range(4):
                    ins = pe.transpose(c.psum[:, 2 * (t % 2) + a, k * P:(k + 1) * P],
                                       hid[:, t, (4 * a + k) * P:(4 * a + k + 1) * P], c.identity[:])
                ins.then_inc(q2_turned, 1)

        turn(0)
        for t in range(TT):
            if t + 1 < TT:
                turn(t + 1)
            pe.wait_ge(q2_moved, 2 * (t + 1))
            if t >= 4:
                pe.wait_ge(x_ready, TT * norm_use + t - 3)
            for k in range(HC):
                ins = pe.matmul(c.psum[:, 4 + t % 4, 0:D], hid_feat[t % 2][:, k, :], ternary[1][:, k, :],
                                start=(k == 0), stop=(k == HC - 1))
            ins.then_inc(down_done, 1)

    s.sync, s.gpsimd, s.vector, s.scalar, s.tensor = sync, gpsimd, vector, scalar, tensor
    return [s]


def expert_ffn(c, dram, norm_use):
    s = Stage()
    scope = ExitStack()
    sh_in, wr_in = c.sem("m_sh_in"), c.sem("m_wr_in")
    e_in = [c.sem("m_e_in0"), c.sem("m_e_in1")]
    F = P
    up_sh = c.sb("m_up_sh", [P, DC, F], F32, scope)
    down_sh = c.sb("m_down_sh", [P, D], F32, scope)
    up = [c.sb(f"m_up{i}", [P, DC, F], F32, scope) for i in range(2)]
    down = [c.sb(f"m_down{i}", [P, D], F32, scope) for i in range(2)]
    wr = c.sb("m_wr", [P, DC, EXPERTS], F32, scope)
    logits = c.sb("m_logits", [P, TT, EXPERTS], F32, scope)
    best = c.sb("m_best", [P, TT, 8], F32, scope)
    chance = c.sb("m_chance", [P, TT], F32, scope)
    prob = c.sb("m_prob", [P, TT, EXPERTS], F32, scope)
    act_h = [c.sb(f"m_h{i}", [P, T], F32, scope) for i in range(2)]
    scope.close()
    x_ready = c.sem("x_ready")
    step = c.sem("m_step")
    logits_done, gap_ready, gap_exp = c.sem("m_logits_done"), c.sem("m_gap_ready"), c.sem("m_gap_exp")
    up_done, relu_done, h_ready = c.sem("m_up_done"), c.sem("m_relu_done"), c.sem("m_h_ready")
    down_done, added = c.sem("m_down_done"), c.sem("m_added")
    prob_ready = c.sem("m_prob_ready")
    UP_BANK, DOWN_BANK = 0, 4

    def sync(sp):
        sp.wait_ge(x_ready, TT * norm_use)
        sp.dma_start(wr[:], dram["L1_ffn_Wr"].rearrange("(k p) n -> p k n", p=P)).then_inc(wr_in, 16)
        sp.dma_start(up_sh[:], dram["L1_ffn_Ws1"].rearrange("(k p) n -> p k n", p=P)).then_inc(sh_in, 16)
        sp.dma_start(down_sh[:], dram["L1_ffn_Ws2"]).then_inc(sh_in, 16)

        def load(e, slot):
            sp.dma_start(up[slot][:], dram["L1_ffn_W1"][e].rearrange("(k p) n -> p k n", p=P)).then_inc(e_in[slot], 16)
            sp.dma_start(down[slot][:], dram["L1_ffn_W2"][e]).then_inc(e_in[slot], 16)

        load(0, 0)
        load(1, 1)
        with sp.Fori(1, EXPERTS // 2) as i:
            for slot in range(2):
                sp.wait_ge(down_done, TT * (2 * i + slot))
                load(2 * i + slot, slot)

    def tensor(pe):
        wait_feat(c, pe, norm_use)
        pe.wait_ge(wr_in, 16)
        pe.wait_ge(sh_in, 32)
        for t in range(TT):
            for k in range(DC):
                ins = pe.matmul(c.psum[:, 7, t * EXPERTS:(t + 1) * EXPERTS], c.xn_feat[:, k, t * P:(t + 1) * P],
                                wr[:, k, :], start=(k == 0), stop=(k == DC - 1))
        ins.then_inc(logits_done, 1)

        def hidden(wi, h, weight):
            wait_free(pe, h_ready, NH * (wi - 1))
            for n in range(NH):
                for k in range(DC):
                    ins = pe.matmul(c.psum[:, UP_BANK + 2 * h + n, :], weight[:, k, :],
                                    c.xn_feat[:, k, n * BANK:(n + 1) * BANK], start=(k == 0), stop=(k == DC - 1))
                ins.then_inc(up_done, 1)

        def outputs(wi, h, weight):
            for t in range(TT):
                pe.wait_ge(h_ready, NH * wi + t // 4 + 1)
                if isinstance(wi, int) and wi == 0 and t == 3:
                    pe.wait_ge(prob_ready, 1)
                elif isinstance(wi, int) and wi == EXPERTS and t >= 4:
                    pe.wait_ge(x_ready, TT * norm_use + t - 3)
                else:
                    wait_free(pe, added, TT * wi + t - 3)
                ins = pe.matmul(c.psum[:, DOWN_BANK + t % 4, 0:D], act_h[h][:, t * P:(t + 1) * P], weight[:],
                                start=True, stop=True)
                ins.then_inc(down_done, 1)

        def expert(e, slot, pair, last):
            if not last:
                pe.wait_ge(e_in[1 - slot], 32 * (pair + slot + 1))
                hidden(e + 2, slot, up[1 - slot])
            outputs(e + 1, 1 - slot, down[slot])

        hidden(0, 0, up_sh)
        pe.wait_ge(e_in[0], 32)
        hidden(1, 1, up[0])
        outputs(0, 0, down_sh)
        with pe.Fori(0, EXPERTS // 2 - 1) as i:
            for slot in range(2):
                expert(2 * i + slot, slot, i, False)
        for slot in range(2):
            expert(EXPERTS - 2 + slot, slot, EXPERTS // 2 - 1, slot == 1)

    def scalar(act):
        act.wait_ge(gap_ready, 1)
        act.activation(chance[:], chance[:], ACT.Exp).then_inc(gap_exp, 1)

        def relu(wi, h):
            for n in range(NH):
                act.wait_ge(up_done, NH * wi + n + 1)
                if not isinstance(wi, int) or wi >= 2:
                    act.wait_ge(down_done, TT * (wi - 1))
                act.activation(act_h[h][:, n * BANK:(n + 1) * BANK], c.psum[:, UP_BANK + 2 * h + n, :],
                               ACT.Relu).then_inc(relu_done, 1)
                act.wait_ge(relu_done, NH * wi + n + 1)
                act.activation(act_h[h][:, n * BANK:(n + 1) * BANK], act_h[h][:, n * BANK:(n + 1) * BANK],
                               ACT.Square).then_inc(h_ready, 1)

        relu(0, 0)
        relu(1, 1)
        with act.Fori(1, EXPERTS // 2) as i:
            for slot in range(2):
                relu(2 * i + slot, slot)
        relu(EXPERTS, 0)

    def vector(dve):
        count = [0]

        def after(ins):
            count[0] += 1
            ins.then_inc(step, 1)
            dve.wait_ge(step, count[0])

        dve.wait_ge(logits_done, 1)
        after(dve.tensor_copy(logits[:], c.psum[:, 7, 0:TT * EXPERTS].rearrange("p (t e) -> p t e", t=TT)))
        for t in range(TT):
            ins = dve.max(best[:, t, :], logits[:, t, :])
        after(ins)
        dve.tensor_tensor(chance[:], best[:, :, 1], best[:, :, 0], ALU.subtract).then_inc(gap_ready, 1)
        dve.wait_ge(gap_exp, 1)
        after(dve.tensor_scalar(chance[:], chance[:], 1.0, None, ALU.add))
        after(dve.reciprocal(chance[:], chance[:]))
        after(dve.tensor_scalar(chance[:], chance[:], 1.0, None, ALU.is_ge))
        after(dve.tensor_tensor(prob[:], logits[:], bc(best[:, :, 0], 2, EXPERTS), ALU.is_equal))
        dve.tensor_tensor(prob[:], prob[:], bc(chance[:], 2, EXPERTS), ALU.mult).then_inc(prob_ready, 1)
        dve.wait_ge(prob_ready, 1)

        def add(wi, weight, last=False):
            for t in range(TT):
                dve.wait_ge(down_done, TT * wi + t + 1)
                if not isinstance(wi, int) or wi:
                    dve.wait_ge(added, TT * (wi - 1) + t + 1)
                ins = dve.scalar_tensor_tensor(c.x_tok[:, t, :], c.psum[:, DOWN_BANK + t % 4, 0:D], weight(t),
                                               c.x_tok[:, t, :], ALU.mult, ALU.add)
                ins.then_inc(x_ready if last else added, 1)

        add(0, lambda t: c.ones[:, 0:1])
        with dve.Fori(1, EXPERTS) as wi:
            add(wi, lambda t: prob[:, t, bass.ds(wi - 1, 1)])
        add(EXPERTS, lambda t: prob[:, t, EXPERTS - 1:EXPERTS], last=True)

    s.sync, s.tensor, s.scalar, s.vector = sync, tensor, scalar, vector
    return [s]


def store_stage(c, dram, uses):
    s = Stage()
    x_ready, stored = c.sem("x_ready"), c.sem("stored")

    def sync(sp):
        for t in range(0, TT, 2):
            sp.wait_ge(x_ready, TT * uses + t + 2)
            sp.dma_start(dram["out"].rearrange("(t p) d -> p t d", p=P)[:, t:t + 2, :], c.x_tok[:, t:t + 2, :])\
              .then_inc(stored, 16)
        sp.wait_ge(stored, 16 * (TT // 2))

    s.sync = sync
    return s


def perceiver(nc, dram, upto=6):
    ctx = ExitStack()
    with ctx:
        c = Shared(nc, ctx)
        c.wide_loads = 0
        c.cross_weights = {layer: allocate_cross_weights(c, layer) for layer in ("L0", "L1")}
        stages = [load_stage(c, dram)]
        parts = [
            lambda: [norm_stage(c, 0, 0), *cross_attention(c, dram, 0, 0, 0, "L0", False)],
            lambda: [norm_stage(c, 1, 1), *first_self_attention(c, dram, 1, 1)],
            lambda: [norm_stage(c, 2, 2), *quantized_ffn(c, dram, 2, 3)],
            lambda: [norm_stage(c, 3, 5), *cross_attention(c, dram, 1, 3, 2, "L1", True)],
            lambda: [norm_stage(c, 4, 6), *second_self_attention(c, dram, 4, 3)],
            lambda: [norm_stage(c, 5, 7), *expert_ffn(c, dram, 5)],
        ]
        for part in parts[:upto]:
            stages += part()
        stages.append(store_stage(c, dram, upto - 1))
        block = ctx.enter_context(nc.Block())

        @block.sync
        def _(sp):
            for s in stages:
                s.sync(sp)

        @block.gpsimd
        def _(pool):
            for s in stages:
                s.gpsimd(pool)

        @block.tensor
        def _(pe):
            for s in stages:
                s.tensor(pe)

        @block.scalar
        def _(act):
            for s in stages:
                s.scalar(act)

        @block.vector
        def _(dve):
            for s in stages:
                s.vector(dve)


UPTO = 6


def kernel(**inputs):
    import numpy as np
    import concourse.bacc as bacc
    from concourse.bass_utils import run_bass_kernel_spmd as run

    a = {name: np.asarray(v) for name, v in inputs.items()}
    lay = {"x": a["x"].reshape(T, D)}

    def columns(v):
        return v.reshape(-1, P).T

    lay["ctx"] = a["ctx_1024"].reshape(B, NKV, DC, P).transpose(0, 3, 2, 1)
    lay["L0_mask"] = a["mask_BxS2_bf1"]
    lay["L1_mask"] = a["mask_BxS2_bk0"]
    for n in ("Wq", "Wk", "Wv", "Wo"):
        lay[f"L0_xattn_{n}"] = a[f"L0_xattn_{n}"].T
        lay[f"L1_xattn_{n}"] = a[f"L1_xattn_{n}"]
        lay[f"L1_attn_{n}"] = a[f"L1_attn_{n}"]
    lay["L0_xattn_bo"], lay["L1_xattn_bo"] = a["L0_xattn_bo"], a["L1_xattn_bo"]
    lay["L1_xattn_cols"] = np.stack([columns(a[f"L1_xattn_{n}"]) for n in ("bq", "bk", "bv")], axis=1)
    def grouped(w, biases):
        groups = w.shape[2]
        tiles = w.reshape(DC, P, 3, groups, P).transpose(3, 1, 2, 0, 4).reshape(groups, P, 3 * DC * P)
        cols = np.stack([v.reshape(groups, P) for v in biases], axis=2)
        return np.concatenate([tiles, cols], axis=2)

    no_bias = np.zeros(HID, np.float32)
    lay["L0_attn_w"] = grouped(a["L0_attn_qkv"].reshape(D, 3, 8, P),
                               [a["L0_attn_q_bias"].reshape(-1), no_bias, no_bias])
    pos = a["L0_attn_positional"].transpose(1, 2, 0)
    swapped = pos.reshape(16, 64, 32, 2)[..., ::-1].reshape(16, 64, 64)
    lay["L0_attn_pos"] = np.concatenate([pos, swapped], axis=2).reshape(8, P, P)
    lay["L0_attn_out_kernel"], lay["L0_attn_out_bias"] = a["L0_attn_out_kernel"], a["L0_attn_out_bias"]
    lay["w1_t"], lay["w2_t"] = a["L0_ffn_w1"].T, a["L0_ffn_w2"].T
    for n in ("ln1_g", "ln1_b", "ln2_g", "ln2_b", "b1", "b2"):
        lay[f"L0_ffn_{n}"] = a[f"L0_ffn_{n}"]
    lay["a1_gate"] = np.repeat(a["L1_attn_cg_W"], 16, axis=1)
    lay["am_w"] = np.repeat(a["L1_attn_am_W"], 16, axis=1)
    lay["am_b_cols"] = columns(np.repeat(a["L1_attn_am_b"], 16))
    lay["a1_cols"] = np.stack([columns(v) for v in (
        a["L1_attn_bq"], a["L1_attn_bk"], a["L1_attn_bv"], np.repeat(a["L1_attn_cg_b"], 16),
        a["L1_attn_ca_bout"], a["L1_attn_mc_bout"])], axis=1)
    lay["L1_attn_cons_vec"], lay["L1_attn_bo"] = a["L1_attn_cons_vec"], a["L1_attn_bo"]
    for n in ("ca", "mc"):
        lay[f"L1_attn_{n}_Wout"] = a[f"L1_attn_{n}_Wout"]
        lay[f"{n}_w"] = grouped(a[f"L1_attn_{n}_Win"].reshape(D, 3, DC, P), a[f"L1_attn_{n}_bin"].reshape(3, D))
    for n in ("Ws1", "Ws2", "W1", "W2", "Wr"):
        lay[f"L1_ffn_{n}"] = a[f"L1_ffn_{n}"]

    lay["identity"] = np.eye(P, dtype=np.float32)
    row = np.arange(P)
    lay["head_rows"] = np.where(row[:, None] // 16 == np.arange(8)[None], 0.25, 0).astype(np.float32)
    lay["half_rows"] = np.where(row[:, None] // 16 % 2 == np.arange(2)[None], 1, 0).astype(np.float32)
    place = np.arange(S)
    lay["causal"] = np.where(place[None, :] > (row % S)[:, None], -1.0e9, 0).astype(np.float32)
    freq = np.arange(S)
    angle = np.outer(2500.0 ** (-(freq // 2 * 2) / 64), place.astype(np.float64))
    sin, cos, even = np.sin(angle), np.cos(angle), (freq % 2 == 0)[:, None]
    key = np.where(even, sin, cos)
    query = np.concatenate([np.where(even, -cos, cos), sin]) * np.sqrt(2.0) / 8
    lay["pos_key"] = np.concatenate([key, key]).astype(np.float32)
    lay["pos_query"] = query.astype(np.float32)

    nc = bacc.Bacc("TRN2", target_bir_lowering=False, num_devices=1)
    arrays, dram = {}, {}
    for name, v in lay.items():
        v = np.ascontiguousarray(v)
        arrays[f"in_{name}"] = v
        dram[name] = nc.dram_tensor(f"in_{name}", v.shape, mybir.dt.from_np(v.dtype), kind="ExternalInput").ap()
    dram["out"] = nc.dram_tensor("out", (T, D), F32, kind="ExternalOutput").ap()
    perceiver(nc, dram, UPTO)
    r = run(nc, [arrays], core_ids=[0])
    return r.results[0]["out"].reshape(B, S, D)
```

```python
from contextlib import ExitStack

import concourse.bass as bass
from concourse import mybir

F32 = mybir.dt.float32
BF16 = mybir.dt.bfloat16
U8 = mybir.dt.uint8
I32 = mybir.dt.int32
ALU = mybir.AluOpType
ACT = mybir.ActivationFunctionType
AX = mybir.AxisListType

P = 128
B, S, D = 16, 64, 256
T = B * S
TT = T // P
DC = D // P
NKV = 256
KT = NKV // P
BANK = 512
NH = T // BANK
HID = 1024
HC = HID // P
EXPERTS = 8
EPS = 1e-5
RSQRT_GUESS = float(0x5f3759df)
ROUND = 12582912.0
MASKED = -3.0e38
CAUSAL_W = 0.7
META_W = (0.9 - 0.8) / 0.2 * 0.3


def bc(ap, axis, n):
    shape = list(ap.shape)
    return ap.unsqueeze(axis).broadcast_to(shape[:axis] + [n] + shape[axis:])


def wait_free(eng, sem, value):
    if not (isinstance(value, int) and value <= 0):
        eng.wait_ge(sem, value)


class Shared:

    def __init__(self, nc, ctx):
        self.nc, self.ctx = nc, ctx
        self.sems = {}
        sb = self.sb
        self.x_tok = sb("x_tok", [P, TT, D])
        self.xn_tok = sb("xn_tok", [P, TT, D])
        self.xn_feat = sb("xn_feat", [P, DC, T])
        self.q_feat = sb("q_feat", [P, DC, T])
        self.o_feat = sb("o_feat", [P, DC, T])
        self.stats = sb("stats", [P, TT, 2, 6])
        self.mean_var = sb("mean_var", [P, TT, 2])
        self.var_eps = sb("var_eps", [P, TT])
        self.rstd = sb("rstd", [P, TT])
        self.newton = sb("newton", [P, TT])
        self.identity = sb("identity", [P, P])
        self.identity_bf = sb("identity_bf", [P, P], BF16)
        self.ones = sb("ones", [P, P])
        self.ones_bf = sb("ones_bf", [1, P], BF16)
        self.head_rows = sb("head_rows", [P, 8])
        self.half_rows = sb("half_rows", [P, 2])
        self.psum = ctx.enter_context(nc.psum_tensor("psum", [P, 8, BANK], F32))

    def sb(self, name, shape, dt=F32, scope=None):
        return (scope or self.ctx).enter_context(self.nc.sbuf_tensor(name, shape, dt))

    def sem(self, name):
        if name not in self.sems:
            self.sems[name] = self.ctx.enter_context(self.nc.semaphore(name))
        return self.sems[name]


class Stage:

    def tensor(self, pe):
        pass

    def scalar(self, act):
        pass

    def vector(self, dve):
        pass

    def gpsimd(self, pool):
        pass

    def sync(self, sp):
        pass


def load_stage(c, dram):
    s = Stage()
    x_in = [c.sem("x_in0"), c.sem("x_in1")]
    const_in, ident_bf = c.sem("const_in"), c.sem("ident_bf")

    def sync(sp):
        for half in range(2):
            at = slice(TT // 2 * half, TT // 2 * (half + 1))
            sp.dma_start(c.x_tok[:, at, :], dram["x"].rearrange("(t p) d -> p t d", p=P)[:, at, :])\
              .then_inc(x_in[half], 16)
        sp.dma_start(c.identity[:], dram["identity"]).then_inc(const_in, 16)
        sp.dma_start(c.head_rows[:], dram["head_rows"]).then_inc(const_in, 16)
        sp.dma_start(c.half_rows[:], dram["half_rows"]).then_inc(const_in, 16)

    def gpsimd(pool):
        pool.memset(c.ones_bf[:], 1.0).then_inc(ident_bf, 1)
        pool.memset(c.ones[:], 1.0).then_inc(ident_bf, 1)
        pool.wait_ge(const_in, 48)
        pool.tensor_copy(c.identity_bf[:], c.identity[:]).then_inc(ident_bf, 1)

    def tensor(pe):
        pe.wait_ge(const_in, 48)
        pe.wait_ge(ident_bf, 3)

    def vector(dve):
        dve.wait_ge(const_in, 48)
        for t in range(TT):
            if t % (TT // 2) == 0:
                dve.wait_ge(x_in[2 * t // TT], 16)
            c.norms[0].follow(dve, t)

    s.sync, s.gpsimd, s.tensor, s.vector = sync, gpsimd, tensor, vector
    return s


class RowStatistics:
    STEPS = 11

    def __init__(self, c, use):
        self.c, self.use = c, use
        self.stats_done, self.aggr_done = c.sem("stats_done"), c.sem("aggr_done")
        self.chain = c.sem("rstd_chain")

    def tile(self, dve, t, pieces):
        for h, piece in enumerate(pieces):
            ins = dve.bn_stats(self.c.stats[:, t, h, :], piece)
        ins.then_inc(self.stats_done, 1)

    def finish(self, dve, pieces=1):
        c, use = self.c, self.use
        dve.wait_ge(self.stats_done, TT * (use + 1))
        for t in range(TT):
            ins = dve.bn_aggr(c.mean_var[:, t, :], c.stats[:, t, 0:pieces, :])
        ins.then_inc(self.aggr_done, 1)
        dve.wait_ge(self.aggr_done, use + 1)
        v, y, t = c.var_eps[:], c.rstd[:], c.newton[:]
        count = [self.STEPS * use]

        def after(ins):
            count[0] += 1
            ins.then_inc(self.chain, 1)
            dve.wait_ge(self.chain, count[0])

        after(dve.tensor_scalar(v, c.mean_var[:, :, 1], EPS, None, ALU.add))
        after(dve.tensor_scalar(y.bitcast(I32), v.bitcast(I32), -0.5, RSQRT_GUESS, ALU.mult, ALU.add))
        for _ in range(3):
            after(dve.tensor_tensor(t, y, y, ALU.mult))
            after(dve.scalar_tensor_tensor(t, t, -0.5, v, ALU.mult, ALU.mult))
            after(dve.scalar_tensor_tensor(y, t, 1.5, y, ALU.add, ALU.mult))


class Norm:

    def __init__(self, c, use, stat_use, turn_bank=4):
        self.c, self.use, self.turn_bank = c, use, turn_bank
        self.rows = RowStatistics(c, stat_use)

    def follow(self, dve, t):
        if t:
            self._tile(dve, t - 1)
        if t == TT - 1:
            self._tile(dve, t)
            self._normalize(dve)

    def _tile(self, dve, t):
        if self.use:
            dve.wait_ge(self.c.sem("x_ready"), TT * (self.use - 1) + t + 1)
        self.rows.tile(dve, t, [self.c.x_tok[:, t, :]])

    def _normalize(self, dve):
        c = self.c
        self.rows.finish(dve)
        for t in range(TT):
            dve.tensor_scalar(c.xn_tok[:, t, :], c.x_tok[:, t, :], c.mean_var[:, t, 0:1],
                              c.rstd[:, t:t + 1], ALU.subtract, ALU.mult).then_inc(c.sem("xn_ready"), 1)

    def stage(self):
        c, use = self.c, self.use
        s = Stage()
        xn_ready, turned = c.sem("xn_ready"), c.sem("norm_turned")
        feat_act, feat_dve = c.sem("feat_act"), c.sem("feat_dve")
        tiles = TT // 2

        def feat(k):
            return c.xn_feat[:, :, 2 * P * k:2 * P * (k + 1)]

        def bank(k):
            return c.psum[:, self.turn_bank + k, :].rearrange("p (c n) -> p c n", c=DC)

        def vector(dve):
            for k in range(1, tiles, 2):
                dve.wait_ge(turned, tiles * use + k + 1)
                dve.tensor_copy(feat(k), bank(k)).then_inc(feat_dve, 1)

        def scalar(act):
            for k in range(0, tiles, 2):
                act.wait_ge(turned, tiles * use + k + 1)
                act.activation(feat(k), bank(k), ACT.Copy).then_inc(feat_act, 1)

        def tensor(pe):
            for k in range(tiles):
                for h in range(2):
                    pe.wait_ge(xn_ready, TT * use + 2 * k + h + 1)
                    for m in range(DC):
                        ins = pe.transpose(bank(k)[:, m, h * P:(h + 1) * P],
                                           c.xn_tok[:, 2 * k + h, m * P:(m + 1) * P], c.identity[:])
                ins.then_inc(turned, 1)

        s.vector, s.scalar, s.tensor = vector, scalar, tensor
        return s


def wait_feat(c, eng, use):
    eng.wait_ge(c.sem("feat_act"), 2 * (use + 1))
    eng.wait_ge(c.sem("feat_dve"), 2 * (use + 1))


def out_projection(c, use, out_use, feat, chunks, weight, weights, feat_ready, bias):
    s = Stage()
    x_ready, xn_ready, out_done = c.sem("x_ready"), c.sem("xn_ready"), c.sem("out_done")
    bias_added = c.sem("bias_added")
    following = c.norms.get(use + 1)
    ring = 4

    def gpsimd(pool):
        weights.wait(pool)
        pool.wait_ge(xn_ready, TT * (use + 1))
        pool.tensor_tensor(c.x_tok[:], c.x_tok[:], bc(bias[:], 1, TT), ALU.add).then_inc(bias_added, 1)

    def tensor(pe):
        weights.wait(pe)
        for sem, value in feat_ready:
            pe.wait_ge(sem, value)
        for t in range(TT):
            if t >= ring:
                pe.wait_ge(x_ready, TT * use + t - ring + 1)
            for k in range(chunks):
                ins = pe.matmul(c.psum[:, t % ring, 0:D], feat[:, k, t * P:(t + 1) * P],
                                weight[:, k, :], start=(k == 0), stop=(k == chunks - 1))
            ins.then_inc(out_done, 1)

    def vector(dve):
        dve.wait_ge(bias_added, out_use + 1)
        for t in range(TT):
            dve.wait_ge(out_done, TT * out_use + t + 1)
            dve.tensor_tensor(c.x_tok[:, t, :], c.psum[:, t % ring, 0:D], c.x_tok[:, t, :],
                              ALU.add).then_inc(x_ready, 1)
            if following:
                following.follow(dve, t)

    s.gpsimd, s.tensor, s.vector = gpsimd, tensor, vector
    return s


class Loads:

    def __init__(self, c, name, count):
        self.sem, self.total = c.sem(name), 16 * count

    def dma(self, sp, out, in_):
        sp.dma_start(out, in_).then_inc(self.sem, 16)

    def wait(self, eng):
        eng.wait_ge(self.sem, self.total)


def allocate_cross_weights(c, layer):
    wq, wk, wv, wo = (c.sb(f"{layer}x_{n}", [P, DC, D]) for n in ("wq", "wk", "wv", "wo"))
    bo = c.sb(f"{layer}x_bo", [P, D])
    cols = c.sb(f"{layer}x_cols", [P, 3, DC])
    return wq, wk, wv, wo, bo, cols


def load_cross_weights(c, dram, sp, layer, weights):
    wq, wk, wv, wo, bo, cols = c.cross_weights[layer]
    for a, name in ((wk, "Wk"), (wq, "Wq"), (wv, "Wv"), (wo, "Wo")):
        weights.dma(sp, a[:], dram[f"{layer}_xattn_{name}"].rearrange("(k p) n -> p k n", p=P))
    weights.dma(sp, bo[:], bc(dram[f"{layer}_xattn_bo"], 0, P))
    if layer == "L1":
        weights.dma(sp, cols[:], dram["L1_xattn_cols"])


class ContextKeys:
    RING = 4

    def __init__(self, c, dram):
        self.c, self.dram = c, dram
        self.scope = ExitStack()
        self.k_feat = c.sb("keys", [P, B, DC, NKV], F32, self.scope)
        self.weights = Loads(c, "L1x_weights", 6)
        self.ctx_in = [c.sem(f"keys_ctx_in{j}") for j in range(self.RING)]
        self.done, self.moved = c.sem("keys_done"), c.sem("keys_moved")

    def allocate_context(self, scope):
        self.ctx_t = [self.c.sb(f"keys_ctx{j}", [P, DC, NKV], F32, scope) for j in range(self.RING)]

    def load_weights(self, sp):
        load_cross_weights(self.c, self.dram, sp, "L1", self.weights)

    def load(self, sp, b):
        if b >= self.RING:
            sp.wait_ge(self.done, b - self.RING + 1)
        sp.dma_start(self.ctx_t[b % self.RING][:], self.dram["ctx"][b]).then_inc(self.ctx_in[b % self.RING], 16)

    def project(self, pe, b):
        wk = self.c.cross_weights["L1"][1]
        if b == 0:
            self.weights.wait(pe)
        pe.wait_ge(self.ctx_in[b % self.RING], 16 * (b // self.RING + 1))
        if b >= self.RING:
            pe.wait_ge(self.moved, b - self.RING + 1)
        for m in range(DC):
            for k in range(DC):
                ins = pe.matmul(self.c.psum[:, b % self.RING, m * NKV:(m + 1) * NKV],
                                wk[:, k, m * P:(m + 1) * P], self.ctx_t[b % self.RING][:, k, :],
                                start=(k == 0), stop=(k == DC - 1))
        ins.then_inc(self.done, 1)

    def move(self, act, b):
        cols = self.c.cross_weights["L1"][5]
        if b == 0:
            self.weights.wait(act)
        act.wait_ge(self.done, b + 1)
        for m in range(DC):
            ins = act.activation(self.k_feat[:, b, m, :], self.c.psum[:, b % self.RING, m * NKV:(m + 1) * NKV],
                                 ACT.Identity, bias=cols[:, 1, m:m + 1])
        ins.then_inc(self.moved, 1)


def cross_attention(c, dram, use, norm_use, out_use, layer, biased, keys=None):
    s = Stage()
    scope = ExitStack()
    steps = DC * B
    pairs = 4
    wq, wk, wv, wo, bo, cols = c.cross_weights[layer]
    mask = c.sb(f"{layer}x_mask", [1, B, NKV], U8, scope)
    pad_bias = c.sb(f"{layer}x_pad_bias", [1, B, NKV], BF16, scope)
    ctx_t = [c.sb(f"{layer}ctx{i}", [P, DC, NKV], F32, scope) for i in range(2)]
    k_feat = None if keys else [c.sb(f"{layer}k{i}", [P, DC, NKV], F32, scope) for i in range(2)]
    v_tok = [c.sb(f"{layer}v{i}", [P, KT, D], F32, scope) for i in range(2)]
    q_diag = [c.sb(f"{layer}qd{i}", [P, DC, 8, S], F32, scope) for i in range(2)]
    probs = [c.sb(f"{layer}p{i}", [P, pairs, NKV], F32, scope) for i in range(2)]
    pad_row = [c.sb(f"{layer}pr{i}", [1, NKV], BF16, scope) for i in range(2)]
    probs_t = c.sb(f"{layer}pt", [P, KT, BANK], F32, scope)
    neg_max = c.sb(f"{layer}nm", [P, 2, pairs], F32, scope)
    row_sum = c.sb(f"{layer}rs", [P, 2, pairs], F32, scope)
    row_inv = c.sb(f"{layer}ri", [P, 2, pairs], F32, scope)
    o_half = c.sb(f"{layer}oh", [P, DC, S], F32, scope)
    scope.close()
    if keys:
        keys.scope.close()

    weights = keys.weights if keys else Loads(c, f"{layer}x_weights", 5)
    mask_is_pad = layer == "L1"
    mask_in, mask_ready = c.sem(f"{layer}x_mask_in"), c.sem("x_mask_ready")
    ctx_in = [c.sem("ctx_in0"), c.sem("ctx_in1")]
    q_done, q_moved = c.sem("xq_done"), c.sem("xq_moved")
    kv_done, kv_moved = c.sem("x_kv_done"), c.sem("x_kv_moved")
    diag_ready, scores_done, max_done = c.sem("x_diag_ready"), c.sem("x_scores_done"), c.sem("x_max_done")
    exp_done, inv_ready, probs_ready = c.sem("x_exp_done"), c.sem("x_inv_ready"), c.sem("x_probs_ready")
    turned, pt_act, pt_dve = c.sem("x_turned"), c.sem("x_pt_act"), c.sem("x_pt_dve")
    pv_done, half_ready, o_moved = c.sem("x_pv_done"), c.sem("x_half_ready"), c.sem("x_o_moved")
    x_ready = c.sem("x_ready")
    n0, b0 = steps * use, B * use
    kv0, per = 2 * b0, 1 if keys else 2
    KV_BANK, O_BANK, TURN_BANK = 4, 5, 6

    def sync(sp):
        if not keys:
            load_cross_weights(c, dram, sp, layer, weights)
        if use:
            sp.wait_ge(x_ready, TT * norm_use)
        sp.dma_start(mask[:], dram[f"{layer}_mask"].unsqueeze(0)).then_inc(mask_in, 16)

        def load(b, half):
            sp.dma_start(ctx_t[half][:], dram["ctx"][b]).then_inc(ctx_in[half], 16)

        load(0, 0)
        load(1, 1)
        with sp.Fori(1, B // 2) as i:
            for half in range(2):
                sp.wait_ge(kv_done, kv0 + per * (2 * i + half - 1))
                load(2 * i + half, half)

    def tensor(pe):
        weights.wait(pe)
        wait_feat(c, pe, norm_use)
        for m in range(DC):
            for n in range(NH):
                for k in range(DC):
                    ins = pe.matmul(c.psum[:, KV_BANK + 2 * m + n, :], wq[:, k, m * P:(m + 1) * P],
                                    c.xn_feat[:, k, n * BANK:(n + 1) * BANK],
                                    start=(k == 0), stop=(k == DC - 1))
                ins.then_inc(q_done, 1)
        pe.wait_ge(q_moved, 4 * (use + 1))

        if keys:
            pe.wait_ge(keys.moved, B)

        def project_k(b, half, pair):
            pe.wait_ge(ctx_in[half], 16 * (B // 2 * use + pair + 1))
            if keys:
                return
            wait_free(pe, kv_moved, kv0 + per * b)
            for m in range(DC):
                for k in range(DC):
                    ins = pe.matmul(c.psum[:, KV_BANK, m * NKV:(m + 1) * NKV], wk[:, k, m * P:(m + 1) * P],
                                    ctx_t[half][:, k, :], start=(k == 0), stop=(k == DC - 1))
            ins.then_inc(kv_done, 1)

        def project_v(b, half):
            wait_free(pe, kv_moved, kv0 + per * (b + 1) - 1)
            for t in range(KT):
                for k in range(DC):
                    ins = pe.matmul(c.psum[:, KV_BANK, t * D:(t + 1) * D], ctx_t[half][:, k, t * P:(t + 1) * P],
                                    wv[:, k, :], start=(k == 0), stop=(k == DC - 1))
            ins.then_inc(kv_done, 1)

        def scores(n, b, half, chunk):
            slot = 2 * chunk
            if chunk == 0:
                if not keys:
                    pe.wait_ge(kv_moved, kv0 + per * b + 1)
                pe.wait_ge(diag_ready, 3 * b0 + 3 * b + 3)
            wait_free(pe, exp_done, n0 + n - 1)
            for i in range(pairs):
                bank = c.psum[:, slot + i // 2, :]
                if i % 2 == 0:
                    pe.matmul(bank.rearrange("p (a k) -> p a k", a=2), c.ones_bf[:],
                              bc(pad_row[half][:], 1, 2), start=True, stop=False,
                              skip_group_check=True)
                ins = pe.matmul(bank[:, (i % 2) * NKV:(i % 2 + 1) * NKV],
                                q_diag[half][:, chunk, 2 * i:2 * i + 2, :].rearrange("p j q -> p (j q)"),
                                keys.k_feat[:, b, chunk, :] if keys else k_feat[half][:, chunk, :], start=False, stop=True, skip_group_check=True)
            ins.then_inc(scores_done, 1)

        def turn(n, slot):
            pe.wait_ge(probs_ready, n0 + n + 1)
            for t in range(KT):
                wait_free(pe, (pt_act, pt_dve)[t], n0 + n)
                for i in range(pairs):
                    ins = pe.transpose(c.psum[:, TURN_BANK + t, i * P:(i + 1) * P],
                                       probs[slot][:, i, t * P:(t + 1) * P], c.identity[:])
                ins.then_inc(turned, 1)

        def values(n, b, half, chunk):
            pe.wait_ge(pt_act, n0 + n + 1)
            pe.wait_ge(pt_dve, n0 + n + 1)
            if chunk == 0:
                pe.wait_ge(kv_moved, kv0 + per * (b + 1))
                wait_free(pe, o_moved, b0 + b)
            for i in range(pairs):
                for t in range(KT):
                    ins = pe.matmul(c.psum[32 * i:32 * i + 32, O_BANK, chunk * P:(chunk + 1) * P],
                                    v_tok[half][:, t, chunk * P + 32 * i:chunk * P + 32 * i + 32],
                                    probs_t[:, t, i * P:(i + 1) * P], start=(t == 0), stop=(t == KT - 1))
            ins.then_inc(pv_done, 1)

        def body(i, first=False, last=False):
            for j in range(4):
                n, b, half, chunk = 4 * i + j, 2 * i + j // 2, j // 2, j % 2
                before = not (first and j == 0)
                if before:
                    turn(n - 1, (j - 1) % 2)
                if not (last and j == 3):
                    scores(n + 1, 2 * i + (j + 1) // 2, (j + 1) // 2 % 2, (j + 1) % 2)
                if not (last and j >= 2):
                    if chunk == 0:
                        project_k(b + 1, 1 - half, i + (j + 2) // 4)
                    else:
                        project_v(b + 1, 1 - half)
                if before:
                    values(n - 1, 2 * i + (j - 1) // 2, (j - 1) // 2 % 2, (j - 1) % 2)

        project_k(0, 0, 0)
        project_v(0, 0)
        scores(0, 0, 0, 0)
        body(0, first=True)
        with pe.Fori(1, B // 2 - 1) as i:
            body(i)
        body(B // 2 - 1, last=True)
        turn(steps - 1, 1)
        values(steps - 1, B - 1, 1, 1)

    def scalar(act):
        weights.wait(act)
        for m in range(DC):
            for n in range(NH):
                act.wait_ge(q_done, 4 * use + 2 * m + n + 1)
                out, src = c.q_feat[:, m, n * BANK:(n + 1) * BANK], c.psum[:, KV_BANK + 2 * m + n, :]
                if biased:
                    act.activation(out, src, ACT.Identity, bias=cols[:, 0, m:m + 1]).then_inc(q_moved, 1)
                else:
                    act.activation(out, src, ACT.Copy).then_inc(q_moved, 1)

        def exps(n, slot):
            act.wait_ge(max_done, n0 + n + 1)
            if not isinstance(n, int) or n >= 2:
                act.wait_ge(turned, 2 * (n0 + n - 1))
            for i in range(pairs):
                ins = act.activation(probs[slot][:, i, :], c.psum[:, 2 * slot + i // 2, (i % 2) * NKV:(i % 2 + 1) * NKV],
                                     ACT.Exp, bias=neg_max[:, slot, i:i + 1],
                                     accum_out=row_sum[:, slot, i:i + 1])
            ins.then_inc(exp_done, 1)

        def move_turned(n):
            act.wait_ge(turned, 2 * (n0 + n) + 1)
            act.activation(probs_t[:, 0, :], c.psum[:, TURN_BANK, :], ACT.Copy).then_inc(pt_act, 1)

        def body(i, first=False):
            for j in range(4):
                exps(4 * i + j, j % 2)
                if not (first and j == 0):
                    move_turned(4 * i + j - 1)

        body(0, first=True)
        with act.Fori(1, B // 2) as i:
            body(i)
        move_turned(steps - 1)

    def vector(dve):
        dve.wait_ge(mask_in, 16)
        if mask_is_pad:
            dve.tensor_scalar(pad_bias[:], mask[:], MASKED, None, ALU.mult).then_inc(mask_ready, 1)
        else:
            dve.tensor_scalar(pad_bias[:], mask[:], 1.0, -MASKED, ALU.subtract, ALU.mult).then_inc(mask_ready, 1)
        weights.wait(dve)

        def max_rows(n, slot):
            dve.wait_ge(scores_done, n0 + n + 1)
            dve.tensor_reduce(neg_max[:, slot, :],
                              c.psum[:, 2 * slot:2 * slot + 2, :].rearrange("p a (h k) -> p (a h) k", h=2),
                              AX.X, ALU.max, negate=True).then_inc(max_done, 1)

        def move_k(b, half):
            if keys:
                return
            dve.wait_ge(kv_done, kv0 + per * b + 1)
            dve.tensor_copy(k_feat[half][:], c.psum[:, KV_BANK, :].rearrange("p (m k) -> p m k", m=DC))\
               .then_inc(kv_moved, 1)

        def move_v(b, half):
            dve.wait_ge(kv_done, kv0 + per * (b + 1))
            dve.tensor_copy(v_tok[half][:], c.psum[:, KV_BANK, :].rearrange("p (t d) -> p t d", t=KT))\
               .then_inc(kv_moved, 1)

        def move_turned(n):
            dve.wait_ge(turned, 2 * (n0 + n) + 2)
            dve.tensor_copy(probs_t[:, 1, :], c.psum[:, TURN_BANK + 1, :]).then_inc(pt_dve, 1)

        def normalize(n, slot):
            dve.wait_ge(exp_done, n0 + n + 1)
            dve.reciprocal(row_inv[:, slot, :], row_sum[:, slot, :]).then_inc(inv_ready, 1)
            dve.wait_ge(inv_ready, n0 + n + 1)
            for i in range(pairs):
                ins = dve.tensor_scalar(probs[slot][:, i, :], probs[slot][:, i, :], row_inv[:, slot, i:i + 1],
                                        None, ALU.mult)
            ins.then_inc(probs_ready, 1)

        def move_o(b):
            dve.wait_ge(pv_done, n0 + 2 * b + 2)
            src = c.psum[:, O_BANK, 0:DC * P].rearrange("p (m h q) -> p m h q", m=DC, h=2)
            for m in range(DC):
                bias = (cols[:, 2, m:m + 1], ALU.add) if biased else (None, ALU.bypass)
                ins = dve.tensor_scalar(o_half[:, m, :], src[:, m, 1, :], c.half_rows[:, 1:2], bias[0],
                                        ALU.mult, bias[1])
            ins.then_inc(half_ready, 1)
            dve.wait_ge(half_ready, b0 + b + 1)
            dve.scalar_tensor_tensor(c.o_feat[:, :, bass.ds(S * b, S)], src[:, :, 0, :], c.half_rows[:, 0:1],
                                     o_half[:], ALU.mult, ALU.add).then_inc(o_moved, 1)

        def body(i, first=False, last=False):
            for j in range(4):
                n, b, half = 4 * i + j, 2 * i + j // 2, j // 2
                before = not (first and j == 0)
                if before:
                    move_turned(n - 1)
                normalize(n, j % 2)
                if not (last and j == 3):
                    max_rows(n + 1, (j + 1) % 2)
                if not (last and j >= 2):
                    if j % 2 == 0:
                        move_k(b + 1, 1 - half)
                    else:
                        move_v(b + 1, 1 - half)
                if j % 2 == 0 and before:
                    move_o(b - 1)

        move_k(0, 0)
        move_v(0, 0)
        max_rows(0, 0)
        body(0, first=True)
        with dve.Fori(1, B // 2 - 1) as i:
            body(i)
        body(B // 2 - 1, last=True)
        move_turned(steps - 1)
        move_o(B - 1)

    def gpsimd(pool):
        pool.wait_ge(q_moved, 4 * (use + 1))
        pool.wait_ge(mask_ready, use + 1)

        def diagonal(b, half):
            pool.tensor_copy(pad_row[half][:], pad_bias[:, b, :]).then_inc(diag_ready, 1)
            for m in range(DC):
                pool.tensor_tensor(q_diag[half][:, m, :, :], bc(c.q_feat[:, m, bass.ds(S * b, S)], 1, 8),
                                   bc(c.head_rows[:], 2, S), ALU.mult).then_inc(diag_ready, 1)

        diagonal(0, 0)
        diagonal(1, 1)
        with pool.Fori(1, B // 2) as i:
            for half in range(2):
                b = 2 * i + half
                pool.wait_ge(scores_done, n0 + 2 * b - 2)
                diagonal(b, half)

    s.sync, s.tensor, s.scalar, s.vector, s.gpsimd = sync, tensor, scalar, vector, gpsimd
    out = out_projection(c, norm_use, out_use, c.o_feat, DC, wo, weights, [(o_moved, B * (use + 1))], bo)
    return [s, out]


def wide_attention(c, name, use, groups, weights_dram, xin, xin_ready, out, scale, positions,
                   scratch_free, first_units):
    s = Stage()
    scope = ExitStack()
    g0, r0 = first_units
    heads = 2
    unit_act = 6
    unit_dve = 4 if positions else 0
    w_tile = [c.sb(f"{name}_w{i}", [P, 3 * DC * P + 3], F32, scope) for i in range(2)]
    w = [t[:, 0:3 * DC * P].rearrange("p (a k n) -> p a k n", a=3, k=DC) for t in w_tile]
    bias = [t[:, 3 * DC * P:3 * DC * P + 3] for t in w_tile]
    w_pos = [c.sb(f"{name}_wp{i}", [P, P], F32, scope) for i in range(2)] if positions else None
    q_g = [c.sb(f"{name}_q{i}", [P, T], F32, scope) for i in range(2)]
    k_g = [c.sb(f"{name}_k{i}", [P, T], F32, scope) for i in range(2)]
    v_g = [c.sb(f"{name}_v{i}", [P, TT, P], F32, scope) for i in range(2)]
    r_g = [c.sb(f"{name}_r{i}", [P, heads, T], F32, scope) for i in range(2)] if positions else None
    x_paired = c.sb(f"{name}_xp", [P, DC, 4, 2, P], F32, scope)
    paired = c.sem("w_paired")
    probs = [c.sb(f"{name}_p{i}", [P, TT, S], F32, scope) for i in range(heads)]
    probs_t = [c.sb(f"{name}_pt{i}", [P, BANK], F32, scope) for i in range(heads)]
    neg_max = c.sb(f"{name}_nm", [P, heads, TT], F32, scope)
    row_sum = c.sb(f"{name}_rs", [P, heads, TT], F32, scope)
    scope.close()

    w_in = [c.sem("w_in0"), c.sem("w_in1")]
    act_done, dve_done = c.sem("w_act_units"), c.sem("w_dve_units")
    act_moved, dve_moved = c.sem("w_act_moved"), c.sem("w_dve_moved")
    scores_done, max_done, shifted = c.sem("w_scores_done"), c.sem("w_max_done"), c.sem("w_shifted")
    exp_done, sum_done, inv_done = c.sem("w_exp_done"), c.sem("w_sum_done"), c.sem("w_inv_done")
    probs_ready, turned = c.sem("w_probs_ready"), c.sem("w_turned")
    pt_moved = [c.sem("w_pt_moved0"), c.sem("w_pt_moved1")]
    pv_done, o_moved = c.sem("w_pv_done"), c.sem("w_o_moved")
    SCORE_BANK, UNIT_BANK, TURN_BANK, O_BANK = 0, 2, 4, 6

    def sync(sp):
        for sem, value in scratch_free:
            sp.wait_ge(sem, value)

        def load(g, slot):
            sp.dma_start(w_tile[slot][:], weights_dram[0][g]).then_inc(w_in[slot], 16)
            if positions:
                sp.dma_start(w_pos[slot][:], weights_dram[1][g]).then_inc(w_in[slot], 16)

        load(0, 0)
        load(1, 1)
        if groups > 2:
            with sp.Fori(1, groups // 2) as i:
                for slot in range(2):
                    sp.wait_ge(o_moved, 2 * (g0 + 2 * i + slot - 1))
                    load(2 * i + slot, slot)

    loads = 2 if positions else 1

    def loaded(pair):
        return c.wide_loads + 16 * loads * (pair + 1)

    base_loads = c.wide_loads

    def gpsimd(pool):
        for sem, value in xin_ready:
            pool.wait_ge(sem, value)
        for k in range(DC):
            src = xin[:, k, :].rearrange("p (q e o s) -> p o q e s", q=4, e=2, o=2)
            dst = x_paired[:, k].rearrange("p q o (e s) -> p o q e s", e=2)
            for parity in range(2):
                pool.tensor_copy(dst[:, parity], src[:, parity]).then_inc(paired, 1)

    def tensor(pe):
        for sem, value in xin_ready:
            pe.wait_ge(sem, value)

        def project(g, slot, pair, units):
            for u in units:
                if u == 0:
                    pe.wait_ge(w_in[slot], base_loads + 16 * loads * (pair + 1))
                bank = c.psum[:, UNIT_BANK + u % 2, :]
                if u < 2:
                    if positions:
                        wait_free(pe, dve_moved, unit_dve * (r0 + g) - 1 + u)
                    else:
                        wait_free(pe, act_moved, unit_act * (g0 + g) - 1 + u)
                elif u < unit_act + 2:
                    pe.wait_ge(act_moved, unit_act * (g0 + g) + u - 1)
                else:
                    pe.wait_ge(dve_moved, unit_dve * (r0 + g) + u - unit_act - 1)
                if u < 4:
                    a, n = divmod(u, 2)
                    for k in range(DC):
                        ins = pe.matmul(bank, w[slot][:, a, k, :], xin[:, k, n * BANK:(n + 1) * BANK],
                                        start=(k == 0), stop=(k == DC - 1))
                elif u < 6:
                    pe.wait_ge(paired, 4 * (use + 1))
                    for t in range(4):
                        quad, parity = divmod(4 * (u - 4) + t, 2)
                        for k in range(DC):
                            ins = pe.matmul(bank[:, t * P:(t + 1) * P], x_paired[:, k, quad, parity, :],
                                            w[slot][:, 2, k, :],
                                            start=(k == 0), stop=(k == DC - 1))
                else:
                    h, n = divmod(u - 6, 2)
                    rows = slice(h * S, (h + 1) * S)
                    ins = pe.matmul(bank, w_pos[slot][rows, :], q_g[slot][rows, n * BANK:(n + 1) * BANK],
                                    start=True, stop=True)
                ins.then_inc(act_done if u < 6 else dve_done, 1)

        def scores(g, slot):
            for h in range(heads):
                pe.wait_ge(act_moved, unit_act * (g0 + g + 1))
                if positions:
                    pe.wait_ge(dve_moved, unit_dve * (r0 + g + 1))
                wait_free(pe, shifted, heads * (g0 + g))
                bank = c.psum[:, SCORE_BANK + h, :]
                rows = slice(h * S, (h + 1) * S)
                if positions:
                    pe.matmul(bank.rearrange("p (t k) -> p t k", t=TT), c.identity_bf[:],
                              bc(positions.causal[:], 1, TT), start=True, stop=False, skip_group_check=True)
                    for t in range(TT):
                        pe.matmul(bank[:, t * S:(t + 1) * S], r_g[slot][:, h, t * P:(t + 1) * P],
                                  positions.key[:], start=False, stop=False, skip_group_check=True)
                for t in range(TT):
                    for half in range(2):
                        at = t * P + half * S
                        ins = pe.matmul(bank[half * S:(half + 1) * S, t * S:(t + 1) * S],
                                        q_g[slot][rows, at:at + S], k_g[slot][rows, at:at + S],
                                        start=not positions, stop=True, skip_group_check=bool(positions))
                ins.then_inc(scores_done, 1)

        def turn(g):
            for h in range(heads):
                pe.wait_ge(probs_ready, heads * (g0 + g) + h + 1)
                wait_free(pe, pt_moved[h], g0 + g)
                for quad in range(4):
                    ins = pe.transpose(c.psum[:, TURN_BANK + h, quad * P:(quad + 1) * P],
                                       probs[h][:, 2 * quad:2 * quad + 2, :].rearrange("p t k -> p (t k)"),
                                       c.identity[:])
                ins.then_inc(turned, 1)

        def turned_moved(g):
            for h in range(heads):
                pe.wait_ge(pt_moved[h], g0 + g + 1)
            wait_free(pe, o_moved, 2 * (g0 + g))

        def values(g, slot):
            for e in range(2):
                keys = slice(e * S, (e + 1) * S)
                for h in range(heads):
                    for quad in range(4):
                        for parity in range(2):
                            at = (2 * quad + parity) * S
                            ins = pe.matmul(c.psum[h * S:(h + 1) * S, O_BANK + e, at:at + S],
                                            v_g[slot][keys, 2 * quad + parity, h * S:(h + 1) * S],
                                            probs_t[h][keys, at:at + S], start=True, stop=True)
                ins.then_inc(pv_done, 1)

        def body(pair, last=False):
            for slot in range(2):
                g = 2 * pair + slot
                scores(g, slot)
                if not (last and slot == 1):
                    project(g + 1, 1 - slot, pair + slot, range(all_units - 1))
                turn(g)
                turned_moved(g)
                if not (last and slot == 1):
                    project(g + 1, 1 - slot, pair + slot, [all_units - 1])
                values(g, slot)

        all_units = unit_act + unit_dve
        project(0, 0, 0, range(all_units))
        if groups > 2:
            body(0)
            with pe.Fori(1, groups // 2 - 1) as i:
                body(i)
        body(groups // 2 - 1, last=True)

    def scalar(act):
        for sem, value in scratch_free:
            act.wait_ge(sem, value)

        early = unit_act if positions else unit_act - 1

        def move_units(g, slot, units):
            for u in units:
                act.wait_ge(act_done, unit_act * (g0 + g) + u + 1)
                bank, n = c.psum[:, UNIT_BANK + u % 2, :], u % 2
                if u < 4:
                    dst = (q_g, k_g)[u // 2][slot][:, n * BANK:(n + 1) * BANK]
                    act.activation(dst, bank, ACT.Identity, scale=scale,
                                   bias=bias[slot][:, u // 2:u // 2 + 1]).then_inc(act_moved, 1)
                else:
                    act.activation(v_g[slot][:, 4 * n:4 * n + 4, :], bank.rearrange("p (t d) -> p t d", t=4),
                                   ACT.Copy, scale=scale).then_inc(act_moved, 1)

        def exps(g):
            for h in range(heads):
                act.wait_ge(shifted, heads * (g0 + g) + h + 1)
                act.activation(probs[h][:], probs[h][:], ACT.Exp, scale=0.125).then_inc(exp_done, 1)

        def move_turned(g):
            for h in range(heads):
                act.wait_ge(turned, heads * (g0 + g) + h + 1)
                act.activation(probs_t[h][:], c.psum[:, TURN_BANK + h, :], ACT.Copy).then_inc(pt_moved[h], 1)

        def body(pair, last=False):
            for slot in range(2):
                g = 2 * pair + slot
                more = not (last and slot == 1)
                exps(g)
                if more:
                    move_units(g + 1, 1 - slot, range(early))
                move_turned(g)
                if more:
                    move_units(g + 1, 1 - slot, range(early, unit_act))

        move_units(0, 0, range(unit_act))
        if groups > 2:
            body(0)
            with act.Fori(1, groups // 2 - 1) as i:
                body(i)
        body(groups // 2 - 1, last=True)

    def vector(dve):
        for sem, value in scratch_free:
            dve.wait_ge(sem, value)

        def move_units(g, slot):
            for u in range(unit_dve):
                h, n = divmod(u, 2)
                dve.wait_ge(dve_done, unit_dve * (r0 + g) + u + 1)
                dve.tensor_tensor(r_g[slot][:, h, n * BANK:(n + 1) * BANK].rearrange("p (b q) -> p b q", q=S),
                                  c.psum[:, UNIT_BANK + u % 2, :].rearrange("p (b q) -> p b q", q=S),
                                  bc(positions.query[:], 1, BANK // S), ALU.mult).then_inc(dve_moved, 1)

        def softmax_head(g, h):
            src = c.psum[:, SCORE_BANK + h, :].rearrange("p (t k) -> p t k", t=TT)
            n = heads * (g0 + g) + h + 1
            dve.wait_ge(scores_done, n)
            dve.tensor_reduce(neg_max[:, h, :], src, AX.X, ALU.max, negate=True).then_inc(max_done, 1)
            dve.wait_ge(max_done, n)
            dve.tensor_tensor(probs[h][:], src, bc(neg_max[:, h, :], 2, S), ALU.add).then_inc(shifted, 1)

        def softmax_tail(g, h):
            n = heads * (g0 + g) + h + 1
            dve.wait_ge(exp_done, n)
            dve.tensor_reduce(row_sum[:, h, :], probs[h][:], AX.X, ALU.add).then_inc(sum_done, 1)
            dve.wait_ge(sum_done, n)
            dve.reciprocal(row_sum[:, h, :], row_sum[:, h, :]).then_inc(inv_done, 1)
            dve.wait_ge(inv_done, n)
            dve.tensor_tensor(probs[h][:], probs[h][:], bc(row_sum[:, h, :], 2, S), ALU.mult)\
               .then_inc(probs_ready, 1)

        def move_o(g, slot):
            for e in range(2):
                dve.wait_ge(pv_done, 2 * (g0 + g) + e + 1)
                dst = out[:, g, :].rearrange("p (q e n) -> p e q n", e=2, n=P)[:, e]
                src = c.psum[:, O_BANK + e, :].rearrange("p (q n) -> p q n", n=P)
                dve.tensor_scalar(dst, src, 1.0, bias[slot][:, 2:3], ALU.mult, ALU.add).then_inc(o_moved, 1)

        def body(pair, last=False):
            for slot in range(2):
                g = 2 * pair + slot
                softmax_head(g, 0)
                softmax_head(g, 1)
                softmax_tail(g, 0)
                softmax_tail(g, 1)
                if not (last and slot == 1):
                    move_units(g + 1, 1 - slot)
                move_o(g, slot)

        move_units(0, 0)
        if groups > 2:
            body(0)
            with dve.Fori(1, groups // 2 - 1) as i:
                body(i)
        body(groups // 2 - 1, last=True)

    c.wide_loads += 16 * loads * (groups // 2)
    s.gpsimd = gpsimd
    s.sync, s.tensor, s.scalar, s.vector = sync, tensor, scalar, vector
    return s, (o_moved, 2 * (g0 + groups))


class Positions:
    pass


def first_self_attention(c, dram, norm_use, out_use):
    groups, heads_out = 8, 8
    fan = 1024
    qkv_scale = (3.0 * D * 64 * 16) ** -0.25
    out_scale = (float(fan) * D) ** -0.25
    prep = Stage()
    weights = Loads(c, "a0_weights", 5)
    prepared = c.sem("a0_prepared")
    x_ready = c.sem("x_ready")
    scope = ExitStack()
    pos = Positions()
    wo = c.sb("a0_wo", [P, heads_out, D], F32, scope)
    bo = c.sb("a0_bo", [P, D], F32, scope)
    o8 = c.sb("a0_o", [P, groups, T], F32, scope)
    pos.query = c.sb("a0_query", [P, S], F32, scope)
    pos.key = c.sb("a0_key", [P, S], F32, scope)
    pos.causal = c.sb("a0_causal", [P, S], BF16, scope)
    causal32 = c.sb("a0_causal32", [P, S], F32, scope)

    def sync(sp):
        sp.wait_ge(x_ready, TT * norm_use)
        weights.dma(sp, pos.query[:], dram["pos_query"])
        weights.dma(sp, pos.key[:], dram["pos_key"])
        weights.dma(sp, causal32[:], dram["causal"])
        weights.dma(sp, bo[:], bc(dram["L0_attn_out_bias"], 0, P))
        weights.dma(sp, wo[:], dram["L0_attn_out_kernel"].rearrange("(k p) n -> p k n", p=P))

    def gpsimd(pool):
        weights.wait(pool)
        pool.tensor_copy(pos.causal[:], causal32[:]).then_inc(prepared, 1)
        pool.tensor_scalar(wo[:], wo[:], out_scale, None, ALU.mult).then_inc(prepared, 1)

    def vector(dve):
        weights.wait(dve)

    prep.sync, prep.gpsimd, prep.vector = sync, gpsimd, vector
    ready = [(c.sem("feat_act"), 2 * (norm_use + 1)), (c.sem("feat_dve"), 2 * (norm_use + 1)),
             (prepared, 2), (weights.sem, weights.total)]
    core, done = nested(c, scope, lambda: wide_attention(
        c, "a0", 0, groups, (dram["L0_attn_w"], dram["L0_attn_pos"]), c.xn_feat, ready, o8,
        qkv_scale, pos,
        [(x_ready, TT * norm_use)], (0, 0)))
    out = out_projection(c, norm_use, out_use, o8, groups, wo, weights, [done, (prepared, 2)], bo)
    return [prep, core, out]


def nested(c, scope, make):
    result = make()
    scope.close()
    return result


def narrow_attention(c, q_scaled, k_all, v_w, v_cols, inputs_ready, norm_use, diag_base, scratch_scope):
    s = Stage()
    pairs = 8
    xb = [c.sb(f"n_x{i}", [P, DC, 2, S], F32, scratch_scope) for i in range(2)]
    q_diag = [c.sb(f"n_qd{i}", [P, DC, 8, S], F32, scratch_scope) for i in range(2)]
    v2 = [c.sb(f"n_v{i}", [P, D], F32, scratch_scope) for i in range(2)]
    probs = [c.sb(f"n_p{i}", [P, pairs, S], F32, scratch_scope) for i in range(2)]
    probs_t = c.sb("n_pt", [P, BANK], F32, scratch_scope)
    neg_max = c.sb("n_nm", [P, 2, pairs], F32, scratch_scope)
    row_sum = c.sb("n_rs", [P, 2, pairs], F32, scratch_scope)
    o_half = c.sb("n_oh", [P, DC, S], F32, scratch_scope)
    copies, scores_done, max_done = c.sem("n_copies"), c.sem("n_scores_done"), c.sem("n_max_done")
    shifted, exp_done, sum_done = c.sem("n_shifted"), c.sem("n_exp_done"), c.sem("n_sum_done")
    inv_done, probs_ready, turned = c.sem("n_inv_done"), c.sem("n_probs_ready"), c.sem("n_turned")
    pt_moved, v_done, v_moved = c.sem("n_pt_moved"), c.sem("n_v_done"), c.sem("n_v_moved")
    pv_done, half_ready, o_moved = c.sem("n_pv_done"), c.sem("n_half_ready"), c.sem("n_o_moved")
    V_BANK, TURN_BANK, O_BANK = 4, 5, 6

    def gpsimd(pool):
        for sem, value in inputs_ready:
            pool.wait_ge(sem, value)

        def copy_in(b, half):
            pool.tensor_copy(xb[half][:], bc(c.xn_feat[:, :, bass.ds(S * b, S)], 2, 2)).then_inc(copies, 1)
            for m in range(DC):
                pool.tensor_tensor(q_diag[half][:, m, :, :], bc(q_scaled[:, m, bass.ds(S * b, S)], 1, 8),
                                   bc(c.head_rows[:], 2, S), ALU.mult).then_inc(copies, 1)

        copy_in(0, 0)
        copy_in(1, 1)
        with pool.Fori(1, B // 2) as i:
            for half in range(2):
                b = 2 * i + half
                pool.wait_ge(scores_done, b - 1)
                pool.wait_ge(v_done, b - 1)
                copy_in(b, half)

    def tensor(pe):
        for sem, value in inputs_ready:
            pe.wait_ge(sem, value)

        def scores(b, half):
            pe.wait_ge(copies, 3 * b + 3)
            wait_free(pe, shifted, b - 1)
            for i in range(pairs):
                m, j = divmod(i, 4)
                ins = pe.matmul(c.psum[:, half, i * S:(i + 1) * S],
                                q_diag[half][:, m, 2 * j:2 * j + 2, :].rearrange("p j q -> p (j q)"),
                                k_all[:, m, bass.ds(S * b, S)], start=True, stop=True)
            ins.then_inc(scores_done, 1)

        def project_v(b, half, before_last=lambda: None):
            wait_free(pe, v_moved, b)
            for k in range(DC):
                if k == DC - 1:
                    before_last()
                ins = pe.matmul(c.psum[:, V_BANK, 0:D], xb[half][:, k, :, :].rearrange("p a s -> p (a s)"),
                                v_w[:, k, :], start=(k == 0), stop=(k == DC - 1))
            ins.then_inc(v_done, 1)

        def turn(b, half):
            pe.wait_ge(probs_ready, b + 1)
            wait_free(pe, pt_moved, b)
            for u in range(pairs // 2):
                ins = pe.transpose(c.psum[:, TURN_BANK, u * P:(u + 1) * P],
                                   probs[half][:, 2 * u:2 * u + 2, :].rearrange("p t k -> p (t k)"),
                                   c.identity[:])
            ins.then_inc(turned, 1)

        def values_ready(b):
            pe.wait_ge(pt_moved, b + 1)
            pe.wait_ge(v_moved, b + 1)
            wait_free(pe, o_moved, b)

        def values(b, half):
            for i in range(pairs):
                m, j = divmod(i, 4)
                u, rows = i // 2, slice((i % 2) * S, (i % 2 + 1) * S)
                ins = pe.matmul(c.psum[32 * j:32 * j + 32, O_BANK, m * P:(m + 1) * P],
                                v2[half][rows, 32 * i:32 * i + 32], probs_t[rows, u * P:(u + 1) * P],
                                start=True, stop=True)
            ins.then_inc(pv_done, 1)

        def body(i, last=False):
            for half in range(2):
                b = 2 * i + half
                more = not (last and half == 1)
                if more:
                    scores(b + 1, 1 - half)
                turn(b, half)
                if more:
                    project_v(b + 1, 1 - half, before_last=lambda: values_ready(b))
                else:
                    values_ready(b)
                values(b, half)

        scores(0, 0)
        project_v(0, 0)
        body(0)
        with pe.Fori(1, B // 2 - 1) as i:
            body(i)
        body(B // 2 - 1, last=True)

    def scalar(act):
        for sem, value in inputs_ready:
            act.wait_ge(sem, value)

        def exps(b, half):
            act.wait_ge(shifted, b + 1)
            act.activation(probs[half][:], probs[half][:], ACT.Exp).then_inc(exp_done, 1)

        def move_v(b, half):
            act.wait_ge(v_done, b + 1)
            act.activation(v2[half][:], c.psum[:, V_BANK, 0:D], ACT.Copy).then_inc(v_moved, 1)

        def move_turned(b):
            act.wait_ge(turned, b + 1)
            act.activation(probs_t[:], c.psum[:, TURN_BANK, :], ACT.Copy).then_inc(pt_moved, 1)

        def body(i, last=False):
            for half in range(2):
                b = 2 * i + half
                move_turned(b)
                if not (last and half == 1):
                    exps(b + 1, 1 - half)
                    move_v(b + 1, 1 - half)

        exps(0, 0)
        move_v(0, 0)
        body(0)
        with act.Fori(1, B // 2 - 1) as i:
            body(i)
        body(B // 2 - 1, last=True)

    def vector(dve):
        for sem, value in inputs_ready:
            dve.wait_ge(sem, value)

        def softmax(b, half):
            src = c.psum[:, half, :].rearrange("p (t k) -> p t k", t=pairs)
            dve.wait_ge(scores_done, b + 1)
            dve.tensor_reduce(neg_max[:, half, :], src, AX.X, ALU.max, negate=True).then_inc(max_done, 1)
            dve.wait_ge(max_done, b + 1)
            dve.tensor_tensor(probs[half][:], src, bc(neg_max[:, half, :], 2, S), ALU.add).then_inc(shifted, 1)

        def normalize(b, half):
            dve.wait_ge(exp_done, b + 1)
            dve.tensor_reduce(row_sum[:, half, :], probs[half][:], AX.X, ALU.add).then_inc(sum_done, 1)
            dve.wait_ge(sum_done, b + 1)
            dve.reciprocal(row_sum[:, half, :], row_sum[:, half, :]).then_inc(inv_done, 1)
            dve.wait_ge(inv_done, b + 1)
            dve.tensor_tensor(probs[half][:], probs[half][:], bc(row_sum[:, half, :], 2, S), ALU.mult)\
               .then_inc(probs_ready, 1)

        def move_o(b):
            dve.wait_ge(pv_done, b + 1)
            src = c.psum[:, O_BANK, 0:DC * P].rearrange("p (m h q) -> p m h q", m=DC, h=2)
            for m in range(DC):
                ins = dve.tensor_scalar(o_half[:, m, :], src[:, m, 1, :], c.half_rows[:, 1:2],
                                        v_cols[:, m:m + 1], ALU.mult, ALU.add)
            ins.then_inc(half_ready, 1)
            dve.wait_ge(half_ready, b + 1)
            dve.scalar_tensor_tensor(c.o_feat[:, :, bass.ds(S * b, S)], src[:, :, 0, :], c.half_rows[:, 0:1],
                                     o_half[:], ALU.mult, ALU.add).then_inc(o_moved, 1)

        def body(i, last=False):
            for half in range(2):
                b = 2 * i + half
                if not (last and half == 1):
                    softmax(b + 1, 1 - half)
                    normalize(b + 1, 1 - half)
                move_o(b)

        softmax(0, 0)
        normalize(0, 0)
        body(0)
        with dve.Fori(1, B // 2 - 1) as i:
            body(i)
        body(B // 2 - 1, last=True)

    s.gpsimd, s.tensor, s.scalar, s.vector = gpsimd, tensor, scalar, vector
    return s, (o_moved, B)


def feature_projection(c, name, weight, xin, ready, move, move_act):
    s = Stage()
    done = c.sem(f"{name}_done")

    def tensor(pe):
        for sem, value in ready:
            pe.wait_ge(sem, value)
        for u in range(DC * NH):
            m, n = divmod(u, NH)
            for k in range(DC):
                ins = pe.matmul(c.psum[:, u, :], weight[:, k, m * P:(m + 1) * P],
                                xin[:, k, n * BANK:(n + 1) * BANK], start=(k == 0), stop=(k == DC - 1))
            ins.then_inc(done, 1)

    def scalar(act):
        for u in range(DC * NH):
            act.wait_ge(done, u + 1)
            move_act(act, u, c.psum[:, u, :])

    def vector(dve):
        for u in range(DC * NH):
            move(dve, u)

    s.tensor, s.scalar, s.vector = tensor, scalar, vector
    return s


def second_self_attention(c, dram, norm_use, out_use):
    weights = Loads(c, "a1_weights", 12)
    x_ready, prepared = c.sem("x_ready"), c.sem("a1_prepared")
    scope = ExitStack()
    names = ["Wq", "Wk", "Wv", "Wo", "gate", "ca_Wout", "mc_Wout"]
    w = {n: c.sb(f"a1_{n}", [P, DC, D], F32, scope) for n in names}
    cols = c.sb("a1_cols", [P, 6, DC], F32, scope)
    am_w = c.sb("a1_am_w", [16, D], F32, scope)
    cons = c.sb("a1_cons", [16, 1], F32, scope)
    bo = c.sb("a1_bo", [P, D], F32, scope)
    gate = c.sb("a1_gate_value", [P, DC, T], F32, scope)
    k_all = c.sb("a1_k", [P, DC, T], F32, scope)
    mixed = c.sb("a1_mixed", [P, DC, T], F32, scope)
    inner = c.sb("a1_inner", [P, DC, T], F32, scope)
    o_wide = c.sb("a1_o_wide", [P, DC, T], F32, scope)
    neg_gate = c.sb("a1_neg_gate", [P, DC], F32, scope)
    gate_bias_done = c.sem("a1_gate_bias")
    stages = []

    prep = Stage()

    def sync(sp):
        sp.wait_ge(x_ready, TT * norm_use)
        weights.dma(sp, cols[:], dram["a1_cols"])
        weights.dma(sp, am_w[:], dram["am_w"])
        weights.dma(sp, cons[:], dram["L1_attn_cons_vec"].rearrange("(n a) -> n a", a=1))
        weights.dma(sp, bo[:], bc(dram["L1_attn_bo"], 0, P))
        for n in names:
            src = "a1_gate" if n == "gate" else f"L1_attn_{n}"
            weights.dma(sp, w[n][:], dram[src].rearrange("(k p) n -> p k n", p=P))
        weights.dma(sp, neg_gate[:], dram["am_b_cols"])

    def tensor(pe):
        weights.wait(pe)
        wait_feat(c, pe, norm_use)
        for m in range(DC):
            ins = pe.matmul(c.psum[:, 7, m:m + 1], am_w[:, m * P:(m + 1) * P], cons[:],
                            start=True, stop=True)
        ins.then_inc(gate_bias_done, 1)

    def gpsimd(pool):
        weights.wait(pool)
        pool.tensor_scalar(cols[:, 4, :], cols[:, 4, :], CAUSAL_W, None, ALU.mult).then_inc(prepared, 1)
        pool.tensor_scalar(cols[:, 5, :], cols[:, 5, :], META_W, None, ALU.mult).then_inc(prepared, 1)

    def vector(dve):
        weights.wait(dve)
        dve.wait_ge(gate_bias_done, 1)
        dve.tensor_tensor(cols[:, 3, :], c.psum[:, 7, 0:DC], cols[:, 3, :], ALU.add).then_inc(prepared, 1)
        dve.wait_ge(prepared, 3)
        dve.tensor_tensor(neg_gate[:], cols[:, 3, :], neg_gate[:], ALU.add).then_inc(prepared, 1)
        dve.wait_ge(prepared, 4)
        dve.tensor_scalar(neg_gate[:], neg_gate[:], -1.0, None, ALU.mult).then_inc(prepared, 1)

    def scalar(act):
        act.wait_ge(prepared, 5)

    prep.sync, prep.tensor, prep.gpsimd, prep.vector, prep.scalar = sync, tensor, gpsimd, vector, scalar
    stages.append(prep)

    feat = [(c.sem("feat_act"), 2 * (norm_use + 1)), (c.sem("feat_dve"), 2 * (norm_use + 1)),
            (weights.sem, weights.total)]
    proj = Stage()
    p_done, p_moved = c.sem("a1_p_done"), c.sem("a1_p_moved")
    plus_one, gate_done, q_gated = c.sem("a1_plus_one"), c.sem("a1_gate_done"), c.sem("a1_q_gated")
    jobs = [("gate", gate), ("Wq", c.q_feat), ("Wk", k_all)]
    units = DC * NH

    def tensor(pe):
        for sem, value in feat:
            pe.wait_ge(sem, value)
        for a, (n, _) in enumerate(jobs):
            for u in range(units):
                m, h = divmod(u, NH)
                v = a * units + u
                if v >= 4:
                    pe.wait_ge(p_moved, v - 3)
                for k in range(DC):
                    ins = pe.matmul(c.psum[:, v % 4, :], w[n][:, k, m * P:(m + 1) * P],
                                    c.xn_feat[:, k, h * BANK:(h + 1) * BANK],
                                    start=(k == 0), stop=(k == DC - 1))
                ins.then_inc(p_done, 1)

    def scalar(act):
        for a, (n, dst) in enumerate(jobs):
            for u in range(units):
                m, h = divmod(u, NH)
                v = a * units + u
                act.wait_ge(p_done, v + 1)
                out = dst[:, m, h * BANK:(h + 1) * BANK]
                if n == "gate":
                    act.activation(out, c.psum[:, v % 4, :], ACT.Exp, scale=-1.0,
                                   bias=neg_gate[:, m:m + 1]).then_inc(p_moved, 1)
                else:
                    act.activation(out, c.psum[:, v % 4, :], ACT.Identity,
                                   bias=cols[:, a - 1, m:m + 1]).then_inc(p_moved, 1)

    def vector(dve):
        for m in range(DC):
            dve.wait_ge(p_moved, NH * (m + 1))
            dve.tensor_scalar(gate[:, m, :], gate[:, m, :], 1.0, None, ALU.add).then_inc(plus_one, 1)
            dve.wait_ge(plus_one, m + 1)
            dve.reciprocal(gate[:, m, :], gate[:, m, :]).then_inc(gate_done, 1)
        for m in range(DC):
            dve.wait_ge(gate_done, m + 1)
            dve.wait_ge(p_moved, units + NH * (m + 1))
            dve.tensor_tensor(c.q_feat[:, m, :], c.q_feat[:, m, :], gate[:, m, :], ALU.mult)\
               .then_inc(q_gated, 1)

    proj.tensor, proj.scalar, proj.vector = tensor, scalar, vector
    stages.append(proj)

    narrow_scope = ExitStack()
    core, main_done = narrow_attention(
        c, c.q_feat, k_all, w["Wv"], cols[:, 2, :], feat + [(q_gated, DC), (p_moved, 3 * units), (prepared, 5)],
        norm_use, None, narrow_scope)
    narrow_scope.close()
    stages.append(core)

    ca, ca_done = wide_attention(
        c, "ca", 1, DC, (dram["ca_w"],), c.xn_feat, feat + [main_done], o_wide, 1.0,
        None, [main_done], (8, 8))
    stages.append(ca)

    ca_moved, mixed_done = c.sem("ca_out_moved"), c.sem("mixed_done")

    def take(sem, dst, column, factor):
        def move_act(act, u, bank):
            m, n = divmod(u, NH)
            act.activation(dst[:, m, n * BANK:(n + 1) * BANK], bank, ACT.Identity, scale=factor,
                           bias=cols[:, column, m:m + 1]).then_inc(sem, 1)
        return move_act

    def mix(dst, old, added, sem, factor, done):
        def move(dve, u):
            m, n = divmod(u, NH)
            at = slice(n * BANK, (n + 1) * BANK)
            dve.wait_ge(sem, u + 1)
            dve.scalar_tensor_tensor(dst[:, m, at], old[:, m, at], 1.0 - factor, added[:, m, at],
                                     ALU.mult, ALU.add).then_inc(done, 1)
        return move

    stages.append(feature_projection(c, "ca_out", w["ca_Wout"], o_wide, [ca_done],
                                     mix(mixed, c.o_feat, inner, ca_moved, CAUSAL_W, mixed_done),
                                     take(ca_moved, inner, 4, CAUSAL_W)))
    mc, mc_done = wide_attention(
        c, "mc", 2, DC, (dram["mc_w"],), mixed, [(mixed_done, 4)], o_wide, 1.0,
        None, [(mixed_done, 4)], (10, 8))
    stages.append(mc)
    mc_moved, final_done = c.sem("mc_out_moved"), c.sem("final_done")
    stages.append(feature_projection(c, "mc_out", w["mc_Wout"], o_wide, [mc_done],
                                     mix(k_all, mixed, inner, mc_moved, META_W, final_done),
                                     take(mc_moved, inner, 5, META_W)))
    scope.close()
    stages.append(out_projection(c, norm_use, out_use, k_all, DC, w["Wo"], weights, [(final_done, 4)], bo))
    return stages


def quantized_ffn(c, dram, norm_use, stat_use, keys):
    s = Stage()
    scope = ExitStack()
    loads = Loads(c, "f_loads", 8)
    raw = [c.sb("f_raw1", [P, DC, HID], F32, scope), c.sb("f_raw2", [P, HC, D], F32, scope)]
    ternary = [c.sb("f_w1", [P, DC, HID], BF16, scope), c.sb("f_w2", [P, HC, D], BF16, scope)]
    g1, b1n = c.sb("f_g1", [P, D], F32, scope), c.sb("f_b1n", [P, D], F32, scope)
    g2, b2n = c.sb("f_g2", [P, HID], F32, scope), c.sb("f_b2n", [P, HID], F32, scope)
    bias1, bias2 = c.sb("f_bias1", [P, HID], F32, scope), c.sb("f_bias2", [P, D], F32, scope)
    asum = c.sb("f_asum", [P, 2], F32, scope)
    w_mean, w_inv = c.sb("f_wmean", [P, 2], F32, scope), c.sb("f_winv", [P, 2], F32, scope)
    top = c.sb("f_top", [P, 2, TT], F32, scope)
    q_scale, back = c.sb("f_qscale", [P, 2, TT], F32, scope), c.sb("f_back", [P, 2, TT], F32, scope)
    shift = c.sb("f_shift", [P, TT], F32, scope)
    x1 = c.sb("f_x1", [P, TT, D], F32, scope)
    x1_feat = c.sb("f_x1_feat", [P, DC, T], BF16, scope)
    hid = c.sb("f_hid", [P, TT, HID], F32, scope)
    hid_feat = [c.sb(f"f_hid_feat{i}", [P, HC, P], BF16, scope) for i in range(2)]
    keys.allocate_context(scope)
    scope.close()
    x_ready, xn_ready = c.sem("x_ready"), c.sem("xn_ready")
    rows = [RowStatistics(c, stat_use + i) for i in range(2)]
    following = c.norms.get(norm_use + 1)
    step = c.sem("f_step")
    asum_done, total_done, w_inv_ready = c.sem("f_asum_done"), c.sem("f_total_done"), c.sem("f_w_inv_ready")
    w2_step = c.sem("f_w2_step")
    q1_ready, q1_turned, q1_moved = c.sem("f_q1_ready"), c.sem("f_q1_turned"), c.sem("f_q1_moved")
    w1_ready = c.sem("f_w1_ready")
    up_done, up_moved, gelu_done = c.sem("f_up_done"), c.sem("f_up_moved"), c.sem("f_gelu_done")
    shift_ready, scaled, gained = c.sem("f_shift_ready"), c.sem("f_scaled"), c.sem("f_gained")
    q2_ready, q2_turned, q2_moved = c.sem("f_q2_ready"), c.sem("f_q2_turned"), c.sem("f_q2_moved")
    down_done, f_bias_added = c.sem("f_down_done"), c.sem("f_bias_added")
    KEYS_FIRST, KEYS_UP = 8, 4

    def sync(sp):
        keys.load_weights(sp)
        sp.wait_ge(x_ready, TT * norm_use)
        for b in range(4):
            keys.load(sp, b)
        for dst, name in ((g1, "ln1_g"), (b1n, "ln1_b")):
            loads.dma(sp, dst[:], bc(dram[f"L0_ffn_{name}"], 0, P))
        loads.dma(sp, raw[0][:], dram["w1_t"].rearrange("(k p) n -> p k n", p=P))
        loads.dma(sp, raw[1][:], dram["w2_t"].rearrange("(k p) n -> p k n", p=P))
        for dst, name in ((bias1, "b1"), (g2, "ln2_g"), (b2n, "ln2_b"), (bias2, "b2")):
            loads.dma(sp, dst[:], bc(dram[f"L0_ffn_{name}"], 0, P))
        for b in range(4, B):
            keys.load(sp, b)

    def make_ternary(eng, a, sem, base):
        eng.tensor_scalar(raw[a][:], raw[a][:], w_inv[:, a:a + 1], ROUND, ALU.mult, ALU.add).then_inc(sem, 1)
        eng.wait_ge(sem, base + 1)
        eng.tensor_scalar(raw[a][:], raw[a][:], ROUND, 1.0, ALU.subtract, ALU.min).then_inc(sem, 1)
        eng.wait_ge(sem, base + 2)
        eng.tensor_scalar(ternary[a][:], raw[a][:], -1.0, None, ALU.max).then_inc(sem, 1)

    def gpsimd(pool):
        pool.wait_ge(w_inv_ready, 1)
        make_ternary(pool, 1, w2_step, 0)
        pool.wait_ge(xn_ready, TT * (norm_use + 1))
        pool.tensor_tensor(c.x_tok[:], c.x_tok[:], bc(bias2[:], 1, TT), ALU.add).then_inc(f_bias_added, 1)
        for t in range(TT):
            pool.wait_ge(scaled, t + 1)
            pool.tensor_tensor(hid[:, t, :], hid[:, t, :], g2[:], ALU.mult).then_inc(gained, 1)

    def vector(dve):
        count = [0]

        def mark(ins):
            count[0] += 1
            ins.then_inc(step, 1)
            return count[0]

        def after(ins):
            dve.wait_ge(step, mark(ins))

        def pipelined(n, first, second):
            marks = []
            for t in range(n + 1):
                if t < n:
                    marks.append(mark(first(t)))
                if t:
                    dve.wait_ge(step, marks[t - 1])
                    last = second(t - 1)
            return last

        def scales(a, at):
            after(dve.tensor_scalar(top[:, a, at], top[:, a, at], 1e-5, None, ALU.max))
            after(dve.reciprocal(q_scale[:, a, at], top[:, a, at]))
            dve.tensor_scalar(back[:, a, at], top[:, a, at], w_mean[:, a:a + 1], 1.0 / 127.0,
                              ALU.mult, ALU.mult).then_inc(step, 1)
            count[0] += 1
            after(dve.tensor_scalar(q_scale[:, a, at], q_scale[:, a, at], 127.0, None, ALU.mult))

        dve.wait_ge(xn_ready, TT * (norm_use + 1))
        for t in range(TT):
            rows[0].tile(dve, t, [c.xn_tok[:, t, :]])
        rows[0].finish(dve)
        loads.wait(dve)
        after(pipelined(TT, lambda t: dve.scalar_tensor_tensor(
            x1[:, t, :], c.xn_tok[:, t, :], c.mean_var[:, t, 0:1], g1[:], ALU.subtract, ALU.mult),
                        lambda t: dve.scalar_tensor_tensor(
            x1[:, t, :], x1[:, t, :], c.rstd[:, t:t + 1], b1n[:], ALU.mult, ALU.add)))
        mark(dve.tensor_reduce(top[:, 0, :], x1[:], AX.X, ALU.max, apply_absolute_value=True))
        for a in range(2):
            dve.tensor_reduce(asum[:, a:a + 1], raw[a][:], AX.XY, ALU.add, apply_absolute_value=True)\
               .then_inc(asum_done, 1)
        dve.wait_ge(total_done, 1)
        after(dve.tensor_scalar(w_mean[:], c.psum[:, 7, 0:2], 1.0 / (D * HID), 1e-5, ALU.mult, ALU.max))
        dve.reciprocal(w_inv[:], w_mean[:]).then_inc(w_inv_ready, 1)
        scales(0, slice(0, TT))
        pipelined(TT, lambda t: dve.tensor_scalar(
            x1[:, t, :], x1[:, t, :], q_scale[:, 0, t:t + 1], ROUND, ALU.mult, ALU.add),
                  lambda t: dve.tensor_scalar(
            x1[:, t, :], x1[:, t, :], ROUND, 127.0, ALU.subtract, ALU.min).then_inc(q1_ready, 1))
        dve.wait_ge(w_inv_ready, 1)
        make_ternary(dve, 0, w1_ready, 0)
        for t in range(TT + 1):
            if t < TT:
                dve.wait_ge(up_done, t + 1)
                src = c.psum[:, 4 + 2 * (t % 2):6 + 2 * (t % 2), :]
                dve.scalar_tensor_tensor(hid[:, t, :].rearrange("p (a n) -> p a n", a=2), src,
                                         back[:, 0, t:t + 1], bias1[:].rearrange("p (a n) -> p a n", a=2),
                                         ALU.mult, ALU.add).then_inc(up_moved, 1)
            if t:
                dve.wait_ge(gelu_done, t)
                rows[1].tile(dve, t - 1, [hid[:, t - 1, h * BANK:(h + 1) * BANK] for h in range(2)])
        rows[1].finish(dve, 2)
        dve.scalar_tensor_tensor(shift[:], c.mean_var[:, :, 0], -1.0, c.rstd[:], ALU.mult, ALU.mult)\
           .then_inc(shift_ready, 1)

        def add_shift(t):
            dve.wait_ge(gained, t + 1)
            return dve.tensor_tensor(hid[:, t, :], hid[:, t, :], b2n[:], ALU.add)

        per = TT // 2
        for first in range(0, TT, per):
            after(pipelined(per, lambda t: add_shift(first + t), lambda t: dve.tensor_reduce(
                top[:, 1, first + t:first + t + 1], hid[:, first + t, :], AX.X, ALU.max,
                apply_absolute_value=True)))
            scales(1, slice(first, first + per))
            pipelined(per, lambda t: dve.tensor_scalar(
                hid[:, first + t, :], hid[:, first + t, :], q_scale[:, 1, first + t:first + t + 1], ROUND,
                ALU.mult, ALU.add),
                      lambda t: dve.tensor_scalar(
                hid[:, first + t, :], hid[:, first + t, :], ROUND, 127.0, ALU.subtract, ALU.min)
                      .then_inc(q2_ready, 1))
        dve.wait_ge(f_bias_added, 1)
        for t in range(TT):
            dve.wait_ge(down_done, t + 1)
            dve.scalar_tensor_tensor(c.x_tok[:, t, :], c.psum[:, 4 + t % 4, 0:D], back[:, 1, t:t + 1],
                                     c.x_tok[:, t, :], ALU.mult, ALU.add).then_inc(x_ready, 1)
            if following:
                following.follow(dve, t)

    def scalar(act):
        for b in range(KEYS_FIRST):
            keys.move(act, b)
        for k in range(TT // 2):
            act.wait_ge(q1_turned, k + 1)
            act.activation(x1_feat[:, :, 2 * P * k:2 * P * (k + 1)],
                           c.psum[:, k, :].rearrange("p (c n) -> p c n", c=DC), ACT.Copy).then_inc(q1_moved, 1)
        for t in range(TT):
            act.wait_ge(up_moved, t + 1)
            act.activation(hid[:, t, :], hid[:, t, :], ACT.Gelu).then_inc(gelu_done, 1)
            if t < KEYS_UP:
                keys.move(act, KEYS_FIRST + t)
        for b in range(KEYS_FIRST + KEYS_UP, B):
            keys.move(act, b)
        act.wait_ge(shift_ready, 1)
        for t in range(TT):
            act.activation(hid[:, t, :], hid[:, t, :], ACT.Identity, scale=c.rstd[:, t:t + 1],
                           bias=shift[:, t:t + 1]).then_inc(scaled, 1)
        for t in range(TT):
            for a in range(2):
                act.wait_ge(q2_turned, 2 * t + a + 1)
                if t >= 2:
                    act.wait_ge(down_done, t - 1)
                act.activation(hid_feat[t % 2][:, 4 * a:4 * a + 4, :],
                               c.psum[:, 2 * (t % 2) + a, :].rearrange("p (k n) -> p k n", k=4), ACT.Copy)\
                   .then_inc(q2_moved, 1)

    def tensor(pe):
        wait_feat(c, pe, norm_use)
        for b in range(KEYS_FIRST):
            keys.project(pe, b)
        pe.wait_ge(asum_done, 2)
        pe.matmul(c.psum[:, 7, 0:2], c.ones[:], asum[:], start=True, stop=True).then_inc(total_done, 1)
        pe.wait_ge(keys.moved, KEYS_FIRST)
        for t in range(TT):
            pe.wait_ge(q1_ready, t + 1)
            bank = c.psum[:, t // 2, :].rearrange("p (c n) -> p c n", c=DC)
            for m in range(DC):
                ins = pe.transpose(bank[:, m, (t % 2) * P:(t % 2 + 1) * P], x1[:, t, m * P:(m + 1) * P],
                                   c.identity[:])
            if t % 2:
                ins.then_inc(q1_turned, 1)
        pe.wait_ge(w1_ready, 3)
        for t in range(TT):
            pe.wait_ge(q1_moved, t // 2 + 1)
            if t >= 2:
                pe.wait_ge(up_moved, t - 1)
            for n in range(2):
                for k in range(DC):
                    ins = pe.matmul(c.psum[:, 4 + 2 * (t % 2) + n, :], x1_feat[:, k, t * P:(t + 1) * P],
                                    ternary[0][:, k, n * BANK:(n + 1) * BANK],
                                    start=(k == 0), stop=(k == DC - 1))
            ins.then_inc(up_done, 1)
            if t < KEYS_UP:
                pe.wait_ge(q1_moved, TT // 2)
                keys.project(pe, KEYS_FIRST + t)
        for b in range(KEYS_FIRST + KEYS_UP, B):
            keys.project(pe, b)
        pe.wait_ge(keys.moved, B)
        pe.wait_ge(up_moved, TT)

        def turn(t):
            pe.wait_ge(q2_ready, t + 1)
            if t >= 2:
                pe.wait_ge(q2_moved, 2 * (t - 1))
            for a in range(2):
                for k in range(4):
                    ins = pe.transpose(c.psum[:, 2 * (t % 2) + a, k * P:(k + 1) * P],
                                       hid[:, t, (4 * a + k) * P:(4 * a + k + 1) * P], c.identity[:])
                ins.then_inc(q2_turned, 1)

        pe.wait_ge(w2_step, 3)
        turn(0)
        for t in range(TT):
            if t + 1 < TT:
                turn(t + 1)
            pe.wait_ge(q2_moved, 2 * (t + 1))
            if t >= 4:
                pe.wait_ge(x_ready, TT * norm_use + t - 3)
            for k in range(HC):
                ins = pe.matmul(c.psum[:, 4 + t % 4, 0:D], hid_feat[t % 2][:, k, :], ternary[1][:, k, :],
                                start=(k == 0), stop=(k == HC - 1))
            ins.then_inc(down_done, 1)

    s.sync, s.gpsimd, s.vector, s.scalar, s.tensor = sync, gpsimd, vector, scalar, tensor
    return [s]


def expert_ffn(c, dram, norm_use):
    s = Stage()
    scope = ExitStack()
    sh_in, wr_in = c.sem("m_sh_in"), c.sem("m_wr_in")
    e_in = [c.sem("m_e_in0"), c.sem("m_e_in1")]
    F = P
    up_sh = c.sb("m_up_sh", [P, DC, F], F32, scope)
    down_sh = c.sb("m_down_sh", [P, D], F32, scope)
    up = [c.sb(f"m_up{i}", [P, DC, F], F32, scope) for i in range(2)]
    down = [c.sb(f"m_down{i}", [P, D], F32, scope) for i in range(2)]
    wr = c.sb("m_wr", [P, DC, EXPERTS], F32, scope)
    logits = c.sb("m_logits", [P, TT, EXPERTS], F32, scope)
    best = c.sb("m_best", [P, TT, 8], F32, scope)
    chance = c.sb("m_chance", [P, TT], F32, scope)
    prob = c.sb("m_prob", [P, TT, EXPERTS], F32, scope)
    act_h = [c.sb(f"m_h{i}", [P, T], F32, scope) for i in range(2)]
    scope.close()
    x_ready = c.sem("x_ready")
    step = c.sem("m_step")
    logits_done, gap_ready, gap_exp = c.sem("m_logits_done"), c.sem("m_gap_ready"), c.sem("m_gap_exp")
    up_done, relu_done, h_ready = c.sem("m_up_done"), c.sem("m_relu_done"), c.sem("m_h_ready")
    down_done, added = c.sem("m_down_done"), c.sem("m_added")
    prob_ready = c.sem("m_prob_ready")
    UP_BANK, DOWN_BANK = 0, 4

    def sync(sp):
        sp.wait_ge(x_ready, TT * norm_use)
        sp.dma_start(wr[:], dram["L1_ffn_Wr"].rearrange("(k p) n -> p k n", p=P)).then_inc(wr_in, 16)
        sp.dma_start(up_sh[:], dram["L1_ffn_Ws1"].rearrange("(k p) n -> p k n", p=P)).then_inc(sh_in, 16)
        sp.dma_start(down_sh[:], dram["L1_ffn_Ws2"]).then_inc(sh_in, 16)

        def load(e, slot):
            sp.dma_start(up[slot][:], dram["L1_ffn_W1"][e].rearrange("(k p) n -> p k n", p=P)).then_inc(e_in[slot], 16)
            sp.dma_start(down[slot][:], dram["L1_ffn_W2"][e]).then_inc(e_in[slot], 16)

        load(0, 0)
        load(1, 1)
        with sp.Fori(1, EXPERTS // 2) as i:
            for slot in range(2):
                sp.wait_ge(down_done, TT * (2 * i + slot))
                load(2 * i + slot, slot)

    def tensor(pe):
        wait_feat(c, pe, norm_use)
        pe.wait_ge(wr_in, 16)
        pe.wait_ge(sh_in, 32)
        for t in range(TT):
            for k in range(DC):
                ins = pe.matmul(c.psum[:, 7, t * EXPERTS:(t + 1) * EXPERTS], c.xn_feat[:, k, t * P:(t + 1) * P],
                                wr[:, k, :], start=(k == 0), stop=(k == DC - 1))
        ins.then_inc(logits_done, 1)

        def hidden(wi, h, weight):
            wait_free(pe, h_ready, NH * (wi - 1))
            for n in range(NH):
                for k in range(DC):
                    ins = pe.matmul(c.psum[:, UP_BANK + 2 * h + n, :], weight[:, k, :],
                                    c.xn_feat[:, k, n * BANK:(n + 1) * BANK], start=(k == 0), stop=(k == DC - 1))
                ins.then_inc(up_done, 1)

        def outputs(wi, h, weight):
            for t in range(TT):
                pe.wait_ge(h_ready, NH * wi + t // 4 + 1)
                if isinstance(wi, int) and wi == 0 and t == 3:
                    pe.wait_ge(prob_ready, 1)
                elif isinstance(wi, int) and wi == EXPERTS and t >= 4:
                    pe.wait_ge(x_ready, TT * norm_use + t - 3)
                else:
                    wait_free(pe, added, TT * wi + t - 3)
                ins = pe.matmul(c.psum[:, DOWN_BANK + t % 4, 0:D], act_h[h][:, t * P:(t + 1) * P], weight[:],
                                start=True, stop=True)
                ins.then_inc(down_done, 1)

        def expert(e, slot, pair, last):
            if not last:
                pe.wait_ge(e_in[1 - slot], 32 * (pair + slot + 1))
                hidden(e + 2, slot, up[1 - slot])
            outputs(e + 1, 1 - slot, down[slot])

        hidden(0, 0, up_sh)
        pe.wait_ge(e_in[0], 32)
        hidden(1, 1, up[0])
        outputs(0, 0, down_sh)
        with pe.Fori(0, EXPERTS // 2 - 1) as i:
            for slot in range(2):
                expert(2 * i + slot, slot, i, False)
        for slot in range(2):
            expert(EXPERTS - 2 + slot, slot, EXPERTS // 2 - 1, slot == 1)

    def scalar(act):
        act.wait_ge(gap_ready, 1)
        act.activation(chance[:], chance[:], ACT.Exp).then_inc(gap_exp, 1)

        def relu(wi, h):
            for n in range(NH):
                act.wait_ge(up_done, NH * wi + n + 1)
                if not isinstance(wi, int) or wi >= 2:
                    act.wait_ge(down_done, TT * (wi - 1))
                act.activation(act_h[h][:, n * BANK:(n + 1) * BANK], c.psum[:, UP_BANK + 2 * h + n, :],
                               ACT.Relu).then_inc(relu_done, 1)
                act.wait_ge(relu_done, NH * wi + n + 1)
                act.activation(act_h[h][:, n * BANK:(n + 1) * BANK], act_h[h][:, n * BANK:(n + 1) * BANK],
                               ACT.Square).then_inc(h_ready, 1)

        relu(0, 0)
        relu(1, 1)
        with act.Fori(1, EXPERTS // 2) as i:
            for slot in range(2):
                relu(2 * i + slot, slot)
        relu(EXPERTS, 0)

    def vector(dve):
        count = [0]

        def after(ins):
            count[0] += 1
            ins.then_inc(step, 1)
            dve.wait_ge(step, count[0])

        dve.wait_ge(logits_done, 1)
        after(dve.tensor_copy(logits[:], c.psum[:, 7, 0:TT * EXPERTS].rearrange("p (t e) -> p t e", t=TT)))
        for t in range(TT):
            ins = dve.max(best[:, t, :], logits[:, t, :])
        after(ins)
        dve.tensor_tensor(chance[:], best[:, :, 1], best[:, :, 0], ALU.subtract).then_inc(gap_ready, 1)
        dve.wait_ge(gap_exp, 1)
        after(dve.tensor_scalar(chance[:], chance[:], 1.0, None, ALU.add))
        after(dve.reciprocal(chance[:], chance[:]))
        after(dve.tensor_scalar(chance[:], chance[:], 1.0, None, ALU.is_ge))
        after(dve.tensor_tensor(prob[:], logits[:], bc(best[:, :, 0], 2, EXPERTS), ALU.is_equal))
        dve.tensor_tensor(prob[:], prob[:], bc(chance[:], 2, EXPERTS), ALU.mult).then_inc(prob_ready, 1)
        dve.wait_ge(prob_ready, 1)

        def add(wi, weight, last=False):
            for t in range(TT):
                dve.wait_ge(down_done, TT * wi + t + 1)
                if not isinstance(wi, int) or wi:
                    dve.wait_ge(added, TT * (wi - 1) + t + 1)
                ins = dve.scalar_tensor_tensor(c.x_tok[:, t, :], c.psum[:, DOWN_BANK + t % 4, 0:D], weight(t),
                                               c.x_tok[:, t, :], ALU.mult, ALU.add)
                ins.then_inc(x_ready if last else added, 1)

        add(0, lambda t: c.ones[:, 0:1])
        with dve.Fori(1, EXPERTS) as wi:
            add(wi, lambda t: prob[:, t, bass.ds(wi - 1, 1)])
        add(EXPERTS, lambda t: prob[:, t, EXPERTS - 1:EXPERTS], last=True)

    s.sync, s.tensor, s.scalar, s.vector = sync, tensor, scalar, vector
    return [s]


def store_stage(c, dram, uses):
    s = Stage()
    x_ready, stored = c.sem("x_ready"), c.sem("stored")

    def sync(sp):
        for t in range(0, TT, 2):
            sp.wait_ge(x_ready, TT * uses + t + 2)
            sp.dma_start(dram["out"].rearrange("(t p) d -> p t d", p=P)[:, t:t + 2, :], c.x_tok[:, t:t + 2, :])\
              .then_inc(stored, 16)
        sp.wait_ge(stored, 16 * (TT // 2))

    s.sync = sync
    return s


def perceiver(nc, dram, upto=6):
    ctx = ExitStack()
    with ctx:
        c = Shared(nc, ctx)
        c.wide_loads = 0
        c.cross_weights = {layer: allocate_cross_weights(c, layer) for layer in ("L0", "L1")}
        c.norms = {i: Norm(c, i, i if i < 3 else i + 2, 0 if i == 3 else 4) for i in range(upto)}
        keys = []

        def feed_forward():
            keys.append(ContextKeys(c, dram))
            return quantized_ffn(c, dram, 2, 3, keys[0])

        parts = [
            lambda: cross_attention(c, dram, 0, 0, 0, "L0", False),
            lambda: first_self_attention(c, dram, 1, 1),
            feed_forward,
            lambda: cross_attention(c, dram, 1, 3, 2, "L1", True, keys[0]),
            lambda: second_self_attention(c, dram, 4, 3),
            lambda: expert_ffn(c, dram, 5),
        ]
        stages = [load_stage(c, dram)]
        for i, part in enumerate(parts[:upto]):
            stages += [c.norms[i].stage(), *part()]
        stages.append(store_stage(c, dram, upto - 1))
        block = ctx.enter_context(nc.Block())

        @block.sync
        def _(sp):
            for s in stages:
                s.sync(sp)

        @block.gpsimd
        def _(pool):
            for s in stages:
                s.gpsimd(pool)

        @block.tensor
        def _(pe):
            for s in stages:
                s.tensor(pe)

        @block.scalar
        def _(act):
            for s in stages:
                s.scalar(act)

        @block.vector
        def _(dve):
            for s in stages:
                s.vector(dve)


UPTO = 6


def kernel(**inputs):
    import numpy as np
    import concourse.bacc as bacc
    from concourse.bass_utils import run_bass_kernel_spmd as run

    a = {name: np.asarray(v) for name, v in inputs.items()}
    lay = {"x": a["x"].reshape(T, D)}

    def columns(v):
        return v.reshape(-1, P).T

    lay["ctx"] = a["ctx_1024"].reshape(B, NKV, DC, P).transpose(0, 3, 2, 1)
    lay["L0_mask"] = a["mask_BxS2_bf1"]
    lay["L1_mask"] = a["mask_BxS2_bk0"]
    for n in ("Wq", "Wk", "Wv", "Wo"):
        lay[f"L0_xattn_{n}"] = a[f"L0_xattn_{n}"].T
        lay[f"L1_xattn_{n}"] = a[f"L1_xattn_{n}"]
        lay[f"L1_attn_{n}"] = a[f"L1_attn_{n}"]
    lay["L0_xattn_bo"], lay["L1_xattn_bo"] = a["L0_xattn_bo"], a["L1_xattn_bo"]
    lay["L1_xattn_cols"] = np.stack([columns(a[f"L1_xattn_{n}"]) for n in ("bq", "bk", "bv")], axis=1)
    def grouped(w, biases):
        groups = w.shape[2]
        tiles = w.reshape(DC, P, 3, groups, P).transpose(3, 1, 2, 0, 4).reshape(groups, P, 3 * DC * P)
        cols = np.stack([v.reshape(groups, P) for v in biases], axis=2)
        return np.concatenate([tiles, cols], axis=2)

    no_bias = np.zeros(HID, np.float32)
    lay["L0_attn_w"] = grouped(a["L0_attn_qkv"].reshape(D, 3, 8, P),
                               [a["L0_attn_q_bias"].reshape(-1), no_bias, no_bias])
    pos = a["L0_attn_positional"].transpose(1, 2, 0)
    swapped = pos.reshape(16, 64, 32, 2)[..., ::-1].reshape(16, 64, 64)
    lay["L0_attn_pos"] = np.concatenate([pos, swapped], axis=2).reshape(8, P, P)
    lay["L0_attn_out_kernel"], lay["L0_attn_out_bias"] = a["L0_attn_out_kernel"], a["L0_attn_out_bias"]
    lay["w1_t"], lay["w2_t"] = a["L0_ffn_w1"].T, a["L0_ffn_w2"].T
    for n in ("ln1_g", "ln1_b", "ln2_g", "ln2_b", "b1", "b2"):
        lay[f"L0_ffn_{n}"] = a[f"L0_ffn_{n}"]
    lay["a1_gate"] = np.repeat(a["L1_attn_cg_W"], 16, axis=1)
    lay["am_w"] = np.repeat(a["L1_attn_am_W"], 16, axis=1)
    lay["am_b_cols"] = columns(np.repeat(a["L1_attn_am_b"], 16))
    lay["a1_cols"] = np.stack([columns(v) for v in (
        a["L1_attn_bq"], a["L1_attn_bk"], a["L1_attn_bv"], np.repeat(a["L1_attn_cg_b"], 16),
        a["L1_attn_ca_bout"], a["L1_attn_mc_bout"])], axis=1)
    lay["L1_attn_cons_vec"], lay["L1_attn_bo"] = a["L1_attn_cons_vec"], a["L1_attn_bo"]
    for n in ("ca", "mc"):
        lay[f"L1_attn_{n}_Wout"] = a[f"L1_attn_{n}_Wout"]
        lay[f"{n}_w"] = grouped(a[f"L1_attn_{n}_Win"].reshape(D, 3, DC, P), a[f"L1_attn_{n}_bin"].reshape(3, D))
    for n in ("Ws1", "Ws2", "W1", "W2", "Wr"):
        lay[f"L1_ffn_{n}"] = a[f"L1_ffn_{n}"]

    lay["identity"] = np.eye(P, dtype=np.float32)
    row = np.arange(P)
    lay["head_rows"] = np.where(row[:, None] // 16 == np.arange(8)[None], 0.25, 0).astype(np.float32)
    lay["half_rows"] = np.where(row[:, None] // 16 % 2 == np.arange(2)[None], 1, 0).astype(np.float32)
    place = np.arange(S)
    lay["causal"] = np.where(place[None, :] > (row % S)[:, None], -1.0e9, 0).astype(np.float32)
    freq = np.arange(S)
    angle = np.outer(2500.0 ** (-(freq // 2 * 2) / 64), place.astype(np.float64))
    sin, cos, even = np.sin(angle), np.cos(angle), (freq % 2 == 0)[:, None]
    key = np.where(even, sin, cos)
    query = np.concatenate([np.where(even, -cos, cos), sin]) * np.sqrt(2.0) / 8
    lay["pos_key"] = np.concatenate([key, key]).astype(np.float32)
    lay["pos_query"] = query.astype(np.float32)

    nc = bacc.Bacc("TRN2", target_bir_lowering=False, num_devices=1)
    arrays, dram = {}, {}
    for name, v in lay.items():
        v = np.ascontiguousarray(v)
        arrays[f"in_{name}"] = v
        dram[name] = nc.dram_tensor(f"in_{name}", v.shape, mybir.dt.from_np(v.dtype), kind="ExternalInput").ap()
    dram["out"] = nc.dram_tensor("out", (T, D), F32, kind="ExternalOutput").ap()
    perceiver(nc, dram, UPTO)
    r = run(nc, [arrays], core_ids=[0])
    return r.results[0]["out"].reshape(B, S, D)
```

```python
from contextlib import ExitStack

import concourse.bass as bass
from concourse import mybir

F32 = mybir.dt.float32
F32R = mybir.dt.float32r
BF16 = mybir.dt.bfloat16
U8 = mybir.dt.uint8
I32 = mybir.dt.int32
ALU = mybir.AluOpType
ACT = mybir.ActivationFunctionType
AX = mybir.AxisListType

P = 128
B, S, D = 16, 64, 256
T = B * S
TT = T // P
DC = D // P
NKV = 256
KT = NKV // P
BANK = 512
NH = T // BANK
HID = 1024
HC = HID // P
EXPERTS = 8
EPS = 1e-5
RSQRT_GUESS = float(0x5f3759df)
ROUND = 12582912.0
MASKED = -3.0e38
CAUSAL_W = 0.7
META_W = (0.9 - 0.8) / 0.2 * 0.3


def bc(ap, axis, n):
    shape = list(ap.shape)
    return ap.unsqueeze(axis).broadcast_to(shape[:axis] + [n] + shape[axis:])


def wait_free(eng, sem, value):
    if not (isinstance(value, int) and value <= 0):
        eng.wait_ge(sem, value)


def split_products(pe, out, left, right, start, stop):
    ins = pe.matmul(out, left[0], right[0], start=start, stop=False)
    ins = pe.matmul(out, left[0], right[1], start=False, stop=False)
    return pe.matmul(out, left[1], right[0], start=False, stop=stop)


class Shared:

    def __init__(self, nc, ctx):
        self.nc, self.ctx = nc, ctx
        self.sems = {}
        sb = self.sb
        self.x_tok = sb("x_tok", [P, TT, D])
        self.xn_tok = sb("xn_tok", [P, TT, D])
        self.xn_feat = sb("xn_feat", [P, DC, T])
        self.q_feat = sb("q_feat", [P, DC, T])
        self.o_feat = sb("o_feat", [P, DC, T])
        self.stats = sb("stats", [P, TT, 2, 6])
        self.mean_var = sb("mean_var", [P, TT, 2])
        self.var_eps = sb("var_eps", [P, TT])
        self.rstd = sb("rstd", [P, TT])
        self.newton = sb("newton", [P, TT])
        self.identity = sb("identity", [P, P])
        self.identity_bf = sb("identity_bf", [P, P], BF16)
        self.ones = sb("ones", [P, P])
        self.ones_bf = sb("ones_bf", [1, P], BF16)
        self.head_rows = sb("head_rows", [P, 8])
        self.half_rows = sb("half_rows", [P, 2])
        self.psum = ctx.enter_context(nc.psum_tensor("psum", [P, 8, BANK], F32))

    def sb(self, name, shape, dt=F32, scope=None):
        return (scope or self.ctx).enter_context(self.nc.sbuf_tensor(name, shape, dt))

    def sem(self, name):
        if name not in self.sems:
            self.sems[name] = self.ctx.enter_context(self.nc.semaphore(name))
        return self.sems[name]


class Stage:

    def tensor(self, pe):
        pass

    def scalar(self, act):
        pass

    def vector(self, dve):
        pass

    def gpsimd(self, pool):
        pass

    def sync(self, sp):
        pass


def load_stage(c, dram):
    s = Stage()
    x_in = [c.sem("x_in0"), c.sem("x_in1")]
    const_in, ident_bf = c.sem("const_in"), c.sem("ident_bf")

    def sync(sp):
        for half in range(2):
            at = slice(TT // 2 * half, TT // 2 * (half + 1))
            sp.dma_start(c.x_tok[:, at, :], dram["x"].rearrange("(t p) d -> p t d", p=P)[:, at, :])\
              .then_inc(x_in[half], 16)
        sp.dma_start(c.identity[:], dram["identity"]).then_inc(const_in, 16)
        sp.dma_start(c.head_rows[:], dram["head_rows"]).then_inc(const_in, 16)
        sp.dma_start(c.half_rows[:], dram["half_rows"]).then_inc(const_in, 16)

    def gpsimd(pool):
        pool.memset(c.ones_bf[:], 1.0).then_inc(ident_bf, 1)
        pool.memset(c.ones[:], 1.0).then_inc(ident_bf, 1)
        pool.wait_ge(const_in, 48)
        pool.tensor_copy(c.identity_bf[:], c.identity[:]).then_inc(ident_bf, 1)
        pool.wait_ge(ident_bf, 3)

    def tensor(pe):
        pe.wait_ge(const_in, 48)
        pe.wait_ge(ident_bf, 3)

    def vector(dve):
        dve.wait_ge(const_in, 48)
        for t in range(TT):
            if t % (TT // 2) == 0:
                dve.wait_ge(x_in[2 * t // TT], 16)
            c.norms[0].follow(dve, t)

    s.sync, s.gpsimd, s.tensor, s.vector = sync, gpsimd, tensor, vector
    return s


class RowStatistics:
    STEPS = 11

    def __init__(self, c, use):
        self.c, self.use = c, use
        self.stats_done, self.aggr_done = c.sem("stats_done"), c.sem("aggr_done")
        self.chain = c.sem("rstd_chain")

    def tile(self, dve, t, pieces):
        for h, piece in enumerate(pieces):
            ins = dve.bn_stats(self.c.stats[:, t, h, :], piece)
        ins.then_inc(self.stats_done, 1)

    def finish(self, dve, pieces=1):
        c, use = self.c, self.use
        dve.wait_ge(self.stats_done, TT * (use + 1))
        for t in range(TT):
            ins = dve.bn_aggr(c.mean_var[:, t, :], c.stats[:, t, 0:pieces, :])
        ins.then_inc(self.aggr_done, 1)
        dve.wait_ge(self.aggr_done, use + 1)
        v, y, t = c.var_eps[:], c.rstd[:], c.newton[:]
        count = [self.STEPS * use]

        def after(ins):
            count[0] += 1
            ins.then_inc(self.chain, 1)
            dve.wait_ge(self.chain, count[0])

        after(dve.tensor_scalar(v, c.mean_var[:, :, 1], EPS, None, ALU.add))
        after(dve.tensor_scalar(y.bitcast(I32), v.bitcast(I32), -0.5, RSQRT_GUESS, ALU.mult, ALU.add))
        for _ in range(3):
            after(dve.tensor_tensor(t, y, y, ALU.mult))
            after(dve.scalar_tensor_tensor(t, t, -0.5, v, ALU.mult, ALU.mult))
            after(dve.scalar_tensor_tensor(y, t, 1.5, y, ALU.add, ALU.mult))


class Norm:

    def __init__(self, c, use, stat_use, turn_bank=4):
        self.c, self.use, self.turn_bank = c, use, turn_bank
        self.split = None
        self.rows = RowStatistics(c, stat_use)

    def want_split(self, high, low):
        self.split = high, low
        self.high_act, self.high_dve = self.c.sem(f"high_act{self.use}"), self.c.sem(f"high_dve{self.use}")
        self.split_ready = self.c.sem(f"split_ready{self.use}")

    def follow(self, dve, t):
        if t:
            self._tile(dve, t - 1)
        if t == TT - 1:
            self._tile(dve, t)
            self._normalize(dve)

    def _tile(self, dve, t):
        if self.use:
            dve.wait_ge(self.c.sem("x_ready"), TT * (self.use - 1) + t + 1)
        self.rows.tile(dve, t, [self.c.x_tok[:, t, :]])

    def _normalize(self, dve):
        c = self.c
        self.rows.finish(dve)
        for t in range(TT):
            dve.tensor_scalar(c.xn_tok[:, t, :], c.x_tok[:, t, :], c.mean_var[:, t, 0:1],
                              c.rstd[:, t:t + 1], ALU.subtract, ALU.mult).then_inc(c.sem("xn_ready"), 1)

    def stage(self):
        c, use = self.c, self.use
        s = Stage()
        xn_ready, turned = c.sem("xn_ready"), c.sem("norm_turned")
        feat_act, feat_dve = c.sem("feat_act"), c.sem("feat_dve")
        tiles = TT // 2

        def feat(k):
            return c.xn_feat[:, :, 2 * P * k:2 * P * (k + 1)]

        def bank(k):
            return c.psum[:, self.turn_bank + k, :].rearrange("p (c n) -> p c n", c=DC)

        def part(which, k):
            return self.split[which][:, :, 2 * P * k:2 * P * (k + 1)]

        def vector(dve):
            if self.split:
                for k in range(tiles):
                    dve.wait_ge(turned, tiles * use + k + 1)
                    if k % 2:
                        dve.tensor_copy(part(0, k), bank(k)).then_inc(self.high_dve, 1)
                    dve.wait_ge((self.high_act, self.high_dve)[k % 2], k // 2 + 1)
                    dve.tensor_tensor(part(1, k), bank(k), part(0, k).bitcast(F32), ALU.subtract)\
                       .then_inc(self.split_ready, 1)
            for k in range(1, tiles, 2):
                dve.wait_ge(turned, tiles * use + k + 1)
                dve.tensor_copy(feat(k), bank(k)).then_inc(feat_dve, 1)

        def scalar(act):
            if self.split:
                for k in range(0, tiles, 2):
                    act.wait_ge(turned, tiles * use + k + 1)
                    act.activation(part(0, k), bank(k), ACT.Copy).then_inc(self.high_act, 1)
            for k in range(0, tiles, 2):
                act.wait_ge(turned, tiles * use + k + 1)
                if self.split:
                    act.wait_ge(self.split_ready, k + 1)
                act.activation(feat(k), bank(k), ACT.Copy).then_inc(feat_act, 1)

        def tensor(pe):
            for k in range(tiles):
                for h in range(2):
                    pe.wait_ge(xn_ready, TT * use + 2 * k + h + 1)
                    for m in range(DC):
                        ins = pe.transpose(bank(k)[:, m, h * P:(h + 1) * P],
                                           c.xn_tok[:, 2 * k + h, m * P:(m + 1) * P], c.identity[:])
                ins.then_inc(turned, 1)

        s.vector, s.scalar, s.tensor = vector, scalar, tensor
        return s


def feat_ready(c, use, half=1):
    return [(c.sem(n), 2 * use + 1 + half) for n in ("feat_act", "feat_dve")]


def wait_feat(c, eng, use, half=1):
    for sem, value in feat_ready(c, use, half):
        eng.wait_ge(sem, value)


def out_projection(c, use, out_use, feat, chunks, weight, weights, feat_ready, bias, early=()):
    s = Stage()
    x_ready, xn_ready, out_done = c.sem("x_ready"), c.sem("xn_ready"), c.sem("out_done")
    bias_added = c.sem("bias_added")
    following = c.norms.get(use + 1)
    ring = 4

    def gpsimd(pool):
        weights.wait(pool)
        pool.wait_ge(xn_ready, TT * (use + 1))
        pool.tensor_tensor(c.x_tok[:], c.x_tok[:], bc(bias[:], 1, TT), ALU.add).then_inc(bias_added, 1)

    def tensor(pe):
        weights.wait(pe)
        for sem, value in feat_ready:
            pe.wait_ge(sem, value)
        for t in range(TT):
            if t >= ring:
                pe.wait_ge(x_ready, TT * use + t - ring + 1)
            for k in range(chunks - 1 if t in early else 0, chunks):
                ins = pe.matmul(c.psum[:, t % ring, 0:D], feat[:, k, t * P:(t + 1) * P],
                                weight[:, k, :], start=(k == 0), stop=(k == chunks - 1))
            ins.then_inc(out_done, 1)

    def vector(dve):
        dve.wait_ge(bias_added, out_use + 1)
        for t in range(TT):
            dve.wait_ge(out_done, TT * out_use + t + 1)
            dve.tensor_tensor(c.x_tok[:, t, :], c.psum[:, t % ring, 0:D], c.x_tok[:, t, :],
                              ALU.add).then_inc(x_ready, 1)
            if following:
                following.follow(dve, t)

    s.gpsimd, s.tensor, s.vector = gpsimd, tensor, vector
    return s


def early_products(c, pe, feat, chunks, weight, tiles):
    for t in tiles:
        for k in range(chunks - 1):
            pe.matmul(c.psum[:, t, 0:D], feat[:, k, t * P:(t + 1) * P], weight[:, k, :],
                      start=(k == 0), stop=False)


class Loads:

    def __init__(self, c, name, count):
        self.sem, self.total = c.sem(name), 16 * count

    def dma(self, sp, out, in_):
        sp.dma_start(out, in_).then_inc(self.sem, 16)

    def wait(self, eng):
        eng.wait_ge(self.sem, self.total)


def allocate_cross_weights(c, layer):
    wq, wk, wv, wo = (c.sb(f"{layer}x_{n}", [P, DC, D]) for n in ("wq", "wk", "wv", "wo"))
    bo = c.sb(f"{layer}x_bo", [P, D])
    cols = c.sb(f"{layer}x_cols", [P, 3, DC])
    return wq, wk, wv, wo, bo, cols


def load_cross_weights(c, dram, sp, layer, weights):
    wq, wk, wv, wo, bo, cols = c.cross_weights[layer]
    for a, name in ((wk, "Wk"), (wq, "Wq"), (wv, "Wv"), (wo, "Wo")):
        weights.dma(sp, a[:], dram[f"{layer}_xattn_{name}"].rearrange("(k p) n -> p k n", p=P))
    weights.dma(sp, bo[:], bc(dram[f"{layer}_xattn_bo"], 0, P))
    if layer == "L1":
        weights.dma(sp, cols[:], dram["L1_xattn_cols"])


class ContextAhead:
    RING = 4
    JOBS = 3 * B // 2

    def __init__(self, c, dram):
        self.c, self.dram = c, dram
        self.scope = ExitStack()
        self.k_feat = c.sb("ahead_k", [P, B, DC, NKV], F32, self.scope)
        self.v_first = c.sb("ahead_v", [P, B, D], F32, self.scope)
        self.weights = Loads(c, "L1x_weights", 6)
        self.ctx_in = [c.sem(f"ahead_ctx_in{j}") for j in range(self.RING)]
        self.done, self.moved = c.sem("ahead_done"), c.sem("ahead_moved")

    def allocate_context(self, scope):
        self.ctx_t = [self.c.sb(f"ahead_ctx{j}", [P, DC, NKV], F32, scope) for j in range(self.RING)]

    def load_weights(self, sp):
        load_cross_weights(self.c, self.dram, sp, "L1", self.weights)

    def load(self, sp, b):
        if b >= self.RING:
            sp.wait_ge(self.done, 3 * ((b - self.RING) // 2 + 1))
        sp.dma_start(self.ctx_t[b % self.RING][:], self.dram["ctx"][b]).then_inc(self.ctx_in[b % self.RING], 16)

    def project(self, pe, jobs):
        wk, wv = self.c.cross_weights["L1"][1:3]
        for job in jobs:
            pair, kind = divmod(job, 3)
            bank = self.c.psum[:, job % self.RING, :]
            if job == 0:
                self.weights.wait(pe)
            if kind < 2:
                b = 2 * pair + kind
                pe.wait_ge(self.ctx_in[b % self.RING], 16 * (b // self.RING + 1))
            if job >= self.RING:
                pe.wait_ge(self.moved, job - self.RING + 1)
            for m in range(2):
                for k in range(DC):
                    if kind < 2:
                        left, right = wk[:, k, m * P:(m + 1) * P], self.ctx_t[b % self.RING][:, k, :]
                    else:
                        left, right = self.ctx_t[(2 * pair + m) % self.RING][:, k, 0:P], wv[:, k, :]
                    ins = pe.matmul(bank[:, m * NKV:(m + 1) * NKV], left, right,
                                    start=(k == 0), stop=(k == DC - 1))
            ins.then_inc(self.done, 1)

    def move(self, act, jobs):
        cols = self.c.cross_weights["L1"][5]
        for job in jobs:
            pair, kind = divmod(job, 3)
            bank = self.c.psum[:, job % self.RING, :].rearrange("p (m n) -> p m n", m=2)
            if job == 0:
                self.weights.wait(act)
            act.wait_ge(self.done, job + 1)
            if kind < 2:
                for m in range(DC):
                    ins = act.activation(self.k_feat[:, 2 * pair + kind, m, :], bank[:, m, :],
                                         ACT.Identity, bias=cols[:, 1, m:m + 1])
            else:
                ins = act.activation(self.v_first[:, 2 * pair:2 * pair + 2, :], bank, ACT.Copy)
            ins.then_inc(self.moved, 1)


def cross_attention(c, dram, use, norm_use, out_use, layer, biased, ahead=None):
    s = Stage()
    scope = ExitStack()
    steps = DC * B
    pairs = 4
    wq, wk, wv, wo, bo, cols = c.cross_weights[layer]
    mask = c.sb(f"{layer}x_mask", [1, B, NKV], U8, scope)
    pad_bias = c.sb(f"{layer}x_pad_bias", [1, B, NKV], BF16, scope)
    ctx_t = [c.sb(f"{layer}ctx{i}", [P, DC, NKV], F32, scope) for i in range(2)]
    k_feat = None if ahead else [c.sb(f"{layer}k{i}", [P, DC, NKV], F32, scope) for i in range(2)]
    v_tok = [c.sb(f"{layer}v{i}", [P, KT, D], F32, scope) for i in range(2)]
    q_diag = [c.sb(f"{layer}qd{i}", [P, DC, 8, S], F32, scope) for i in range(2)]
    probs = [c.sb(f"{layer}p{i}", [P, pairs, NKV], F32, scope) for i in range(2)]
    pad_row = [c.sb(f"{layer}pr{i}", [1, NKV], BF16, scope) for i in range(2)]
    probs_t = c.sb(f"{layer}pt", [P, KT, BANK], F32, scope)
    neg_max = c.sb(f"{layer}nm", [P, 2, pairs], F32, scope)
    row_sum = c.sb(f"{layer}rs", [P, 2, pairs], F32, scope)
    row_inv = c.sb(f"{layer}ri", [P, 2, pairs], F32, scope)
    o_half = c.sb(f"{layer}oh", [P, DC, S], F32, scope)
    w_parts = [[c.sb(f"{layer}x_{n}{i}", [P, DC, D], F32R, scope) for n in ("high", "low")]
               for i in range(1 if ahead else 2)]
    ctx_parts = [[c.sb(f"{layer}ctx_{n}{i}", [P, DC, NKV], F32R, scope) for n in ("high", "low")]
                 for i in range(2)]
    scope.close()
    split_weights = [wv] if ahead else [wk, wv]
    v_tiles = range(1, KT) if ahead else range(KT)
    if ahead:
        ahead.scope.close()

    weights = ahead.weights if ahead else Loads(c, f"{layer}x_weights", 5)
    mask_is_pad = layer == "L1"
    mask_in, mask_ready = c.sem(f"{layer}x_mask_in"), c.sem("x_mask_ready")
    ctx_in = [c.sem("ctx_in0"), c.sem("ctx_in1")]
    q_done, q_moved = c.sem("xq_done"), c.sem("xq_moved")
    kv_done, kv_moved = c.sem("x_kv_done"), c.sem("x_kv_moved")
    diag_ready, scores_done, max_done = c.sem("x_diag_ready"), c.sem("x_scores_done"), c.sem("x_max_done")
    exp_done, inv_ready, probs_ready = c.sem("x_exp_done"), c.sem("x_inv_ready"), c.sem("x_probs_ready")
    turned, pt_act, pt_dve = c.sem("x_turned"), c.sem("x_pt_act"), c.sem("x_pt_dve")
    pv_done, half_ready, o_moved = c.sem("x_pv_done"), c.sem("x_half_ready"), c.sem("x_o_moved")
    x_ready = c.sem("x_ready")
    n0, b0 = steps * use, B * use
    kv0, per = 2 * b0, 1 if ahead else 2
    v_copied = c.sem("x_v_copied")
    high_done, w_split, ctx_split = c.sem("x_high_done"), c.sem("x_w_split"), c.sem("x_ctx_split")
    high0, w0 = use * (B + 2), use * 2
    KV_BANK, O_BANK, TURN_BANK = 4, 5, 6

    def sync(sp):
        if not ahead:
            load_cross_weights(c, dram, sp, layer, weights)
        if use:
            sp.wait_ge(x_ready, TT * norm_use)
        sp.dma_start(mask[:], dram[f"{layer}_mask"].unsqueeze(0)).then_inc(mask_in, 16)

        def load(b, half):
            sp.dma_start(ctx_t[half][:], dram["ctx"][b]).then_inc(ctx_in[half], 16)

        load(0, 0)
        load(1, 1)
        with sp.Fori(1, B // 2) as i:
            for half in range(2):
                sp.wait_ge(ctx_split, b0 + 2 * i + half - 1)
                load(2 * i + half, half)

    def tensor(pe):
        weights.wait(pe)
        for n in range(NH):
            wait_feat(c, pe, norm_use, n)
            for m in range(DC):
                for k in range(DC):
                    ins = pe.matmul(c.psum[:, KV_BANK + 2 * m + n, :], wq[:, k, m * P:(m + 1) * P],
                                    c.xn_feat[:, k, n * BANK:(n + 1) * BANK],
                                    start=(k == 0), stop=(k == DC - 1))
                ins.then_inc(q_done, 1)
        pe.wait_ge(q_moved, 4 * (use + 1))

        if ahead:
            pe.wait_ge(ahead.moved, ahead.JOBS)

        pe.wait_ge(w_split, w0 + len(split_weights))

        def project_k(b, half):
            pe.wait_ge(ctx_split, b0 + b + 1)
            if ahead:
                return
            wait_free(pe, kv_moved, kv0 + per * b)
            for m in range(DC):
                for k in range(DC):
                    ins = split_products(pe, c.psum[:, KV_BANK, m * NKV:(m + 1) * NKV],
                                         [w[:, k, m * P:(m + 1) * P] for w in w_parts[0]],
                                         [x[:, k, :] for x in ctx_parts[half]],
                                         start=(k == 0), stop=(k == DC - 1))
            ins.then_inc(kv_done, 1)

        def project_v(b, half):
            wait_free(pe, kv_moved, kv0 + per * (b + 1) - 1)
            for t in v_tiles:
                for k in range(DC):
                    ins = split_products(pe, c.psum[:, KV_BANK, t * D:(t + 1) * D],
                                         [x[:, k, t * P:(t + 1) * P] for x in ctx_parts[half]],
                                         [w[:, k, :] for w in w_parts[-1]],
                                         start=(k == 0), stop=(k == DC - 1))
            ins.then_inc(kv_done, 1)

        def scores(n, b, half, chunk):
            slot = 2 * chunk
            if chunk == 0:
                if not ahead:
                    pe.wait_ge(kv_moved, kv0 + per * b + 1)
                pe.wait_ge(diag_ready, 3 * b0 + 3 * b + 3)
            wait_free(pe, exp_done, n0 + n - 1)
            for i in range(pairs):
                bank = c.psum[:, slot + i // 2, :]
                if i % 2 == 0:
                    pe.matmul(bank.rearrange("p (a k) -> p a k", a=2), c.ones_bf[:],
                              bc(pad_row[half][:], 1, 2), start=True, stop=False,
                              skip_group_check=True)
                ins = pe.matmul(bank[:, (i % 2) * NKV:(i % 2 + 1) * NKV],
                                q_diag[half][:, chunk, 2 * i:2 * i + 2, :].rearrange("p j q -> p (j q)"),
                                ahead.k_feat[:, b, chunk, :] if ahead else k_feat[half][:, chunk, :], start=False, stop=True, skip_group_check=True)
                if i % 2:
                    ins.then_inc(scores_done, 1)

        def turn(n, slot):
            pe.wait_ge(probs_ready, n0 + n + 1)
            for t in range(KT):
                wait_free(pe, (pt_act, pt_dve)[t], n0 + n)
                for i in range(pairs):
                    ins = pe.transpose(c.psum[:, TURN_BANK + t, i * P:(i + 1) * P],
                                       probs[slot][:, i, t * P:(t + 1) * P], c.identity[:])
                ins.then_inc(turned, 1)

        def values(n, b, half, chunk):
            pe.wait_ge(pt_act, n0 + n + 1)
            pe.wait_ge(pt_dve, n0 + n + 1)
            if chunk == 0:
                pe.wait_ge(kv_moved, kv0 + per * (b + 1))
                if ahead:
                    pe.wait_ge(v_copied, b + 1)
                wait_free(pe, o_moved, b0 + b)
            for i in range(pairs):
                for t in range(KT):
                    ins = pe.matmul(c.psum[32 * i:32 * i + 32, O_BANK, chunk * P:(chunk + 1) * P],
                                    v_tok[half][:, t, chunk * P + 32 * i:chunk * P + 32 * i + 32],
                                    probs_t[:, t, i * P:(i + 1) * P], start=(t == 0), stop=(t == KT - 1))
            ins.then_inc(pv_done, 1)

        def body(i, first=False, last=False):
            for j in range(4):
                n, b, half, chunk = 4 * i + j, 2 * i + j // 2, j // 2, j % 2
                before = not (first and j == 0)
                if before:
                    turn(n - 1, (j - 1) % 2)
                if not (last and j == 3):
                    scores(n + 1, 2 * i + (j + 1) // 2, (j + 1) // 2 % 2, (j + 1) % 2)
                if not (last and j >= 2):
                    if chunk == 0:
                        project_k(b + 1, 1 - half)
                    else:
                        project_v(b + 1, 1 - half)
                if before:
                    values(n - 1, 2 * i + (j - 1) // 2, (j - 1) // 2 % 2, (j - 1) % 2)

        project_k(0, 0)
        project_v(0, 0)
        scores(0, 0, 0, 0)
        body(0, first=True)
        with pe.Fori(1, B // 2 - 1) as i:
            body(i)
        body(B // 2 - 1, last=True)
        turn(steps - 1, 1)
        values(steps - 1, B - 1, 1, 1)

    def scalar(act):
        weights.wait(act)
        for n in range(NH):
            for m in range(DC):
                act.wait_ge(q_done, 4 * use + 2 * n + m + 1)
                out, src = c.q_feat[:, m, n * BANK:(n + 1) * BANK], c.psum[:, KV_BANK + 2 * m + n, :]
                if biased:
                    act.activation(out, src, ACT.Identity, bias=cols[:, 0, m:m + 1]).then_inc(q_moved, 1)
                else:
                    act.activation(out, src, ACT.Copy).then_inc(q_moved, 1)

        def exps(n, slot):
            if not isinstance(n, int) or n >= 2:
                act.wait_ge(turned, 2 * (n0 + n - 1))
            for i in range(pairs):
                if i % 2 == 0:
                    act.wait_ge(max_done, 2 * (n0 + n) + i // 2 + 1)
                ins = act.activation(probs[slot][:, i, :], c.psum[:, 2 * slot + i // 2, (i % 2) * NKV:(i % 2 + 1) * NKV],
                                     ACT.Exp, bias=neg_max[:, slot, i:i + 1],
                                     accum_out=row_sum[:, slot, i:i + 1])
            ins.then_inc(exp_done, 1)

        def move_turned(n):
            act.wait_ge(turned, 2 * (n0 + n) + 1)
            act.activation(probs_t[:, 0, :], c.psum[:, TURN_BANK, :], ACT.Copy).then_inc(pt_act, 1)

        def body(i, first=False):
            for j in range(4):
                exps(4 * i + j, j % 2)
                if not (first and j == 0):
                    move_turned(4 * i + j - 1)

        body(0, first=True)
        with act.Fori(1, B // 2) as i:
            body(i)
        move_turned(steps - 1)

    def vector(dve):
        dve.wait_ge(mask_in, 16)
        if mask_is_pad:
            dve.tensor_scalar(pad_bias[:], mask[:], MASKED, None, ALU.mult).then_inc(mask_ready, 1)
        else:
            dve.tensor_scalar(pad_bias[:], mask[:], 1.0, -MASKED, ALU.subtract, ALU.mult).then_inc(mask_ready, 1)
        weights.wait(dve)

        def max_rows(n, slot):
            for a in range(2):
                dve.wait_ge(scores_done, 2 * (n0 + n) + a + 1)
                dve.tensor_reduce(neg_max[:, slot, 2 * a:2 * a + 2],
                                  c.psum[:, 2 * slot + a, :].rearrange("p (h k) -> p h k", h=2),
                                  AX.X, ALU.max, negate=True).then_inc(max_done, 1)

        def move_k(b, half):
            if ahead:
                return
            dve.wait_ge(kv_done, kv0 + per * b + 1)
            dve.tensor_copy(k_feat[half][:], c.psum[:, KV_BANK, :].rearrange("p (m k) -> p m k", m=DC))\
               .then_inc(kv_moved, 1)

        def move_v(b, half):
            dve.wait_ge(kv_done, kv0 + per * (b + 1))
            at = slice(v_tiles[0], KT)
            dve.tensor_copy(v_tok[half][:, at, :], c.psum[:, KV_BANK, :].rearrange("p (t d) -> p t d", t=KT)[:, at, :])\
               .then_inc(kv_moved, 1)

        def move_turned(n):
            dve.wait_ge(turned, 2 * (n0 + n) + 2)
            dve.tensor_copy(probs_t[:, 1, :], c.psum[:, TURN_BANK + 1, :]).then_inc(pt_dve, 1)

        def normalize(n, slot):
            dve.wait_ge(exp_done, n0 + n + 1)
            dve.reciprocal(row_inv[:, slot, :], row_sum[:, slot, :]).then_inc(inv_ready, 1)
            dve.wait_ge(inv_ready, n0 + n + 1)
            for i in range(pairs):
                ins = dve.tensor_scalar(probs[slot][:, i, :], probs[slot][:, i, :], row_inv[:, slot, i:i + 1],
                                        None, ALU.mult)
            ins.then_inc(probs_ready, 1)

        def move_o(b):
            dve.wait_ge(pv_done, n0 + 2 * b + 2)
            src = c.psum[:, O_BANK, 0:DC * P].rearrange("p (m h q) -> p m h q", m=DC, h=2)
            for m in range(DC):
                bias = (cols[:, 2, m:m + 1], ALU.add) if biased else (None, ALU.bypass)
                ins = dve.tensor_scalar(o_half[:, m, :], src[:, m, 1, :], c.half_rows[:, 1:2], bias[0],
                                        ALU.mult, bias[1])
            ins.then_inc(half_ready, 1)
            dve.wait_ge(half_ready, b0 + b + 1)
            dve.scalar_tensor_tensor(c.o_feat[:, :, bass.ds(S * b, S)], src[:, :, 0, :], c.half_rows[:, 0:1],
                                     o_half[:], ALU.mult, ALU.add).then_inc(o_moved, 1)

        def body(i, first=False, last=False):
            for j in range(4):
                n, b, half = 4 * i + j, 2 * i + j // 2, j // 2
                before = not (first and j == 0)
                if before:
                    move_turned(n - 1)
                normalize(n, j % 2)
                if not (last and j == 3):
                    max_rows(n + 1, (j + 1) % 2)
                if not (last and j >= 2):
                    if j % 2 == 0:
                        move_k(b + 1, 1 - half)
                    else:
                        move_v(b + 1, 1 - half)
                if j % 2 == 0 and before:
                    move_o(b - 1)

        move_k(0, 0)
        move_v(0, 0)
        max_rows(0, 0)
        body(0, first=True)
        with dve.Fori(1, B // 2 - 1) as i:
            body(i)
        body(B // 2 - 1, last=True)
        move_turned(steps - 1)
        move_o(B - 1)

    def gpsimd(pool):
        def split(raw, parts, high_before, done):
            raw, high, low = (a[:].rearrange("p k (a n) -> p (k a) n", n=P) for a in (raw, *parts))
            pool.tensor_tensor(high, raw, bc(c.ones[:], 1, 2 * DC), ALU.mult).then_inc(high_done, 1)
            pool.wait_ge(high_done, high_before + 1)
            pool.tensor_tensor(low, raw, high.bitcast(F32), ALU.subtract).then_inc(done, 1)

        def split_context(b, half, pair):
            pool.wait_ge(ctx_in[half], 16 * (B // 2 * use + pair + 1))
            if not isinstance(b, int) or b >= 2:
                pool.wait_ge(kv_done, kv0 + per * (b - 1))
            split(ctx_t[half], ctx_parts[half], high0 + len(split_weights) + b, ctx_split)

        weights.wait(pool)
        if use:
            pool.wait_ge(x_ready, TT * norm_use)
        for a, w in enumerate(split_weights):
            split(w, w_parts[a], high0 + a, w_split)
        split_context(0, 0, 0)
        pool.wait_ge(q_moved, 4 * (use + 1))
        pool.wait_ge(mask_ready, use + 1)

        def diagonal(b, half):
            pool.tensor_copy(pad_row[half][:], pad_bias[:, b, :]).then_inc(diag_ready, 1)
            for m in range(DC):
                pool.tensor_tensor(q_diag[half][:, m, :, :], bc(c.q_feat[:, m, bass.ds(S * b, S)], 1, 8),
                                   bc(c.head_rows[:], 2, S), ALU.mult).then_inc(diag_ready, 1)

        def copy_v(b, half):
            pool.tensor_copy(v_tok[half][:, 0, :], ahead.v_first[:, b, :]).then_inc(v_copied, 1)

        def body(i, last=False):
            for half in range(2):
                b = 2 * i + half
                if not (last and half == 1):
                    split_context(b + 1, 1 - half, i + half)
                    pool.wait_ge(scores_done, 2 * (n0 + 2 * b))
                    diagonal(b + 1, 1 - half)
                if ahead:
                    pool.wait_ge(pv_done, n0 + 2 * b - 2)
                    copy_v(b, half)

        for b in range(2):
            diagonal(b, b)
            if ahead:
                copy_v(b, b)
        split_context(1, 1, 0)
        split_context(2, 0, 1)
        pool.wait_ge(scores_done, 2 * (n0 + 2))
        diagonal(2, 0)
        with pool.Fori(1, B // 2 - 1) as i:
            body(i)
        body(B // 2 - 1, last=True)

    s.sync, s.tensor, s.scalar, s.vector, s.gpsimd = sync, tensor, scalar, vector, gpsimd
    out = out_projection(c, norm_use, out_use, c.o_feat, DC, wo, weights, [(o_moved, B * (use + 1))], bo)
    return [s, out]


def wide_weight_tiles(c, name, scope):
    return [c.sb(f"{name}_w{i}", [P, 3 * DC * P + 3], F32, scope) for i in range(2)]


def wide_attention(c, name, use, groups, weights_dram, xin, xin_ready, out, scale, positions,
                   scratch_free, first_units, w_tile=None, xin_ready_first=None, banks_free=(), middle=None,
                   before_last_turn=None):
    s = Stage()
    scope = ExitStack()
    g0, r0 = first_units
    heads = 2
    unit_act = 6
    unit_dve = 4 if positions else 0
    own_tiles = w_tile is None
    if own_tiles:
        w_tile = wide_weight_tiles(c, name, scope)
    v_bias = [c.sb(f"{name}_vb{i}", [P, 1], F32, scope) for i in range(2)]
    w = [t[:, 0:3 * DC * P].rearrange("p (a k n) -> p a k n", a=3, k=DC) for t in w_tile]
    bias = [t[:, 3 * DC * P:3 * DC * P + 3] for t in w_tile]
    w_pos = [c.sb(f"{name}_wp{i}", [P, P], F32, scope) for i in range(2)] if positions else None
    q_g = [c.sb(f"{name}_q{i}", [P, T], F32, scope) for i in range(2)]
    k_g = [c.sb(f"{name}_k{i}", [P, T], F32, scope) for i in range(2)]
    v_g = [c.sb(f"{name}_v{i}", [P, TT, P], F32, scope) for i in range(2)]
    r_g = [c.sb(f"{name}_r{i}", [P, heads, T], F32, scope) for i in range(2)] if positions else None
    x_paired = c.sb(f"{name}_xp", [P, DC, 4, 2, P], F32, scope)
    paired = c.sem("w_paired")
    probs = [c.sb(f"{name}_p{i}", [P, TT, S], F32, scope) for i in range(heads)]
    probs_t = [c.sb(f"{name}_pt{i}", [P, BANK], F32, scope) for i in range(heads)]
    neg_max = c.sb(f"{name}_nm", [P, heads, TT], F32, scope)
    row_sum = c.sb(f"{name}_rs", [P, heads, TT], F32, scope)
    scope.close()

    w_in = [c.sem(f"{name}_w_in0"), c.sem(f"{name}_w_in1")]
    act_done, dve_done = c.sem("w_act_units"), c.sem("w_dve_units")
    act_moved, dve_moved = c.sem("w_act_moved"), c.sem("w_dve_moved")
    scores_done, max_done, shifted = c.sem("w_scores_done"), c.sem("w_max_done"), c.sem("w_shifted")
    exp_done, sum_done, inv_done = c.sem("w_exp_done"), c.sem("w_sum_done"), c.sem("w_inv_done")
    probs_ready, turned = c.sem("w_probs_ready"), c.sem("w_turned")
    pt_moved = [c.sem("w_pt_moved0"), c.sem("w_pt_moved1")]
    pv_done, o_moved = c.sem("w_pv_done"), c.sem("w_o_moved")
    v_bias_copied = c.sem("w_v_bias_copied")
    SCORE_BANK, UNIT_BANK, TURN_BANK, O_BANK = 0, 2, 4, 6

    def sync(sp):
        if own_tiles:
            for sem, value in scratch_free:
                sp.wait_ge(sem, value)

        def load(g, slot):
            sp.dma_start(w_tile[slot][:], weights_dram[0][g]).then_inc(w_in[slot], 16)
            if positions:
                sp.dma_start(w_pos[slot][:], weights_dram[1][g]).then_inc(w_in[slot], 16)

        load(0, 0)
        load(1, 1)
        if groups > 2:
            with sp.Fori(1, groups // 2) as i:
                for slot in range(2):
                    sp.wait_ge(dve_moved, unit_dve * (r0 + 2 * i + slot - 1))
                    load(2 * i + slot, slot)

    loads = 2 if positions else 1

    def gpsimd(pool):
        for sem, value in xin_ready:
            pool.wait_ge(sem, value)
        for k in range(DC):
            src = xin[:, k, :].rearrange("p (q e o s) -> p o q e s", q=4, e=2, o=2)
            dst = x_paired[:, k].rearrange("p q o (e s) -> p o q e s", e=2)
            for parity in range(2):
                pool.tensor_copy(dst[:, parity], src[:, parity]).then_inc(paired, 1)

    def tensor(pe, first):
        if first:
            for sem, value in [*(xin_ready_first or xin_ready), *banks_free]:
                pe.wait_ge(sem, value)

        def project(g, slot, pair, units):
            for u in units:
                if u == 0:
                    pe.wait_ge(w_in[slot], 16 * loads * (pair + 1))
                bank = c.psum[:, UNIT_BANK + u % 2, :]
                if u < 2:
                    if positions:
                        wait_free(pe, dve_moved, unit_dve * (r0 + g) - 1 + u)
                    else:
                        wait_free(pe, act_moved, unit_act * (g0 + g) - 1 + u)
                elif u < unit_act + 2:
                    pe.wait_ge(act_moved, unit_act * (g0 + g) + u - 1)
                else:
                    pe.wait_ge(dve_moved, unit_dve * (r0 + g) + u - unit_act - 1)
                if isinstance(g, int) and g == 0 and u == 1 and xin_ready_first:
                    for sem, value in xin_ready:
                        pe.wait_ge(sem, value)
                if u < 4:
                    a, n = divmod(u, 2)
                    for k in range(DC):
                        ins = pe.matmul(bank, w[slot][:, a, k, :], xin[:, k, n * BANK:(n + 1) * BANK],
                                        start=(k == 0), stop=(k == DC - 1))
                elif u < 6:
                    pe.wait_ge(paired, 4 * (use + 1))
                    for t in range(4):
                        quad, parity = divmod(4 * (u - 4) + t, 2)
                        for k in range(DC):
                            ins = pe.matmul(bank[:, t * P:(t + 1) * P], x_paired[:, k, quad, parity, :],
                                            w[slot][:, 2, k, :],
                                            start=(k == 0), stop=(k == DC - 1))
                else:
                    h, n = divmod(u - 6, 2)
                    rows = slice(h * S, (h + 1) * S)
                    ins = pe.matmul(bank, w_pos[slot][rows, :], q_g[slot][rows, n * BANK:(n + 1) * BANK],
                                    start=True, stop=True)
                ins.then_inc(act_done if u < 6 else dve_done, 1)

        def scores(g, slot, between_heads=lambda: None):
            for h in range(heads):
                if h:
                    between_heads()
                pe.wait_ge(act_moved, unit_act * (g0 + g + 1))
                if positions:
                    pe.wait_ge(dve_moved, unit_dve * (r0 + g + 1))
                wait_free(pe, shifted, heads * (g0 + g))
                bank = c.psum[:, SCORE_BANK + h, :]
                rows = slice(h * S, (h + 1) * S)
                if positions:
                    pe.matmul(bank.rearrange("p (t k) -> p t k", t=TT), c.identity_bf[:],
                              bc(positions.causal[:], 1, TT), start=True, stop=False, skip_group_check=True)
                    for t in range(TT):
                        pe.matmul(bank[:, t * S:(t + 1) * S], r_g[slot][:, h, t * P:(t + 1) * P],
                                  positions.key[:], start=False, stop=False, skip_group_check=True)
                for t in range(TT):
                    for half in range(2):
                        at = t * P + half * S
                        ins = pe.matmul(bank[half * S:(half + 1) * S, t * S:(t + 1) * S],
                                        q_g[slot][rows, at:at + S], k_g[slot][rows, at:at + S],
                                        start=not positions, stop=True, skip_group_check=bool(positions))
                ins.then_inc(scores_done, 1)

        def turn(g):
            for h in range(heads):
                pe.wait_ge(probs_ready, heads * (g0 + g) + h + 1)
                wait_free(pe, pt_moved[h], g0 + g)
                for quad in range(4):
                    ins = pe.transpose(c.psum[:, TURN_BANK + h, quad * P:(quad + 1) * P],
                                       probs[h][:, 2 * quad:2 * quad + 2, :].rearrange("p t k -> p (t k)"),
                                       c.identity[:])
                ins.then_inc(turned, 1)

        def turned_moved(g):
            for h in range(heads):
                pe.wait_ge(pt_moved[h], g0 + g + 1)
            wait_free(pe, o_moved, 2 * (g0 + g))

        def values(g, slot):
            for e in range(2):
                keys = slice(e * S, (e + 1) * S)
                for h in range(heads):
                    for quad in range(4):
                        for parity in range(2):
                            at = (2 * quad + parity) * S
                            ins = pe.matmul(c.psum[h * S:(h + 1) * S, O_BANK + e, at:at + S],
                                            v_g[slot][keys, 2 * quad + parity, h * S:(h + 1) * S],
                                            probs_t[h][keys, at:at + S], start=True, stop=True)
                ins.then_inc(pv_done, 1)

        def body(pair, last=False):
            for slot in range(2):
                g = 2 * pair + slot
                if last and slot == 1:
                    if before_last_turn:
                        before_last_turn(pe)
                    turn(g)
                    turned_moved(g)
                else:
                    project(g + 1, 1 - slot, pair + slot, range(all_units))
                    turn(g)
                    scores(g + 1, 1 - slot, between_heads=lambda: turned_moved(g))
                values(g, slot)

        all_units = unit_act + unit_dve
        if first:
            project(0, 0, 0, range(4))
            if middle:
                middle(pe)
            project(0, 0, 0, range(4, all_units))
            return
        scores(0, 0)
        if groups > 2:
            body(0)
            with pe.Fori(1, groups // 2 - 1) as i:
                body(i)
        body(groups // 2 - 1, last=True)

    def scalar(act, first):
        if first:
            for sem, value in scratch_free:
                act.wait_ge(sem, value)

        def move_units(g, slot):
            for u in range(unit_act):
                act.wait_ge(act_done, unit_act * (g0 + g) + u + 1)
                bank, n = c.psum[:, UNIT_BANK + u % 2, :], u % 2
                if u < 4:
                    dst = (q_g, k_g)[u // 2][slot][:, n * BANK:(n + 1) * BANK]
                    act.activation(dst, bank, ACT.Identity, scale=scale,
                                   bias=bias[slot][:, u // 2:u // 2 + 1]).then_inc(act_moved, 1)
                else:
                    act.activation(v_g[slot][:, 4 * n:4 * n + 4, :], bank.rearrange("p (t d) -> p t d", t=4),
                                   ACT.Copy, scale=scale).then_inc(act_moved, 1)

        def exps(g):
            for h in range(heads):
                act.wait_ge(shifted, heads * (g0 + g) + h + 1)
                act.activation(probs[h][:], probs[h][:], ACT.Exp, scale=0.125).then_inc(exp_done, 1)

        def move_turned(g):
            for h in range(heads):
                act.wait_ge(turned, heads * (g0 + g) + h + 1)
                act.activation(probs_t[h][:], c.psum[:, TURN_BANK + h, :], ACT.Copy).then_inc(pt_moved[h], 1)

        def body(pair, last=False):
            for slot in range(2):
                g = 2 * pair + slot
                more = not (last and slot == 1)
                if more:
                    move_units(g + 1, 1 - slot)
                move_turned(g)
                if more:
                    exps(g + 1)

        if first:
            move_units(0, 0)
            return
        exps(0)
        if groups > 2:
            body(0)
            with act.Fori(1, groups // 2 - 1) as i:
                body(i)
        body(groups // 2 - 1, last=True)

    def vector(dve, first):
        if first:
            for sem, value in scratch_free:
                dve.wait_ge(sem, value)

        def move_units(g, slot):
            dve.wait_ge(act_done, unit_act * (g0 + g) + 1)
            dve.tensor_copy(v_bias[slot][:], bias[slot][:, 2:3]).then_inc(v_bias_copied, 1)
            for u in range(unit_dve):
                h, n = divmod(u, 2)
                dve.wait_ge(dve_done, unit_dve * (r0 + g) + u + 1)
                dve.tensor_tensor(r_g[slot][:, h, n * BANK:(n + 1) * BANK].rearrange("p (b q) -> p b q", q=S),
                                  c.psum[:, UNIT_BANK + u % 2, :].rearrange("p (b q) -> p b q", q=S),
                                  bc(positions.query[:], 1, BANK // S), ALU.mult).then_inc(dve_moved, 1)

        def softmax_head(g, h):
            src = c.psum[:, SCORE_BANK + h, :].rearrange("p (t k) -> p t k", t=TT)
            n = heads * (g0 + g) + h + 1
            dve.wait_ge(scores_done, n)
            dve.tensor_reduce(neg_max[:, h, :], src, AX.X, ALU.max, negate=True).then_inc(max_done, 1)
            dve.wait_ge(max_done, n)
            dve.tensor_tensor(probs[h][:], src, bc(neg_max[:, h, :], 2, S), ALU.add).then_inc(shifted, 1)

        def softmax_tail(g, h):
            n = heads * (g0 + g) + h + 1
            dve.wait_ge(exp_done, n)
            dve.tensor_reduce(row_sum[:, h, :], probs[h][:], AX.X, ALU.add).then_inc(sum_done, 1)
            dve.wait_ge(sum_done, n)
            dve.reciprocal(row_sum[:, h, :], row_sum[:, h, :]).then_inc(inv_done, 1)
            dve.wait_ge(inv_done, n)
            dve.tensor_tensor(probs[h][:], probs[h][:], bc(row_sum[:, h, :], 2, S), ALU.mult)\
               .then_inc(probs_ready, 1)

        def move_o(g, slot):
            dve.wait_ge(v_bias_copied, g0 + g + 1)
            for e in range(2):
                dve.wait_ge(pv_done, 2 * (g0 + g) + e + 1)
                dst = out[:, g, :].rearrange("p (q e n) -> p e q n", e=2, n=P)[:, e]
                src = c.psum[:, O_BANK + e, :].rearrange("p (q n) -> p q n", n=P)
                dve.tensor_scalar(dst, src, 1.0, v_bias[slot][:], ALU.mult, ALU.add).then_inc(o_moved, 1)

        def body(pair, last=False):
            for slot in range(2):
                g = 2 * pair + slot
                softmax_tail(g, 0)
                softmax_tail(g, 1)
                if not (last and slot == 1):
                    move_units(g + 1, 1 - slot)
                    softmax_head(g + 1, 0)
                    softmax_head(g + 1, 1)
                move_o(g, slot)

        if first:
            move_units(0, 0)
            return
        softmax_head(0, 0)
        softmax_head(0, 1)
        if groups > 2:
            body(0)
            with dve.Fori(1, groups // 2 - 1) as i:
                body(i)
        body(groups // 2 - 1, last=True)

    s.first = Stage()
    s.first.sync, s.first.gpsimd = sync, gpsimd
    s.first.tensor, s.tensor = (lambda pe: tensor(pe, True)), (lambda pe: tensor(pe, False))
    s.first.scalar, s.scalar = (lambda act: scalar(act, True)), (lambda act: scalar(act, False))
    s.first.vector, s.vector = (lambda dve: vector(dve, True)), (lambda dve: vector(dve, False))
    return s, (o_moved, 2 * (g0 + groups))


class Positions:
    pass


def first_self_attention(c, dram, norm_use, out_use):
    groups, heads_out = 8, 8
    fan = 1024
    qkv_scale = (3.0 * D * 64 * 16) ** -0.25
    out_scale = (float(fan) * D) ** -0.25
    prep = Stage()
    weights = Loads(c, "a0_weights", 5)
    prepared = c.sem("a0_prepared")
    x_ready = c.sem("x_ready")
    scope = ExitStack()
    pos = Positions()
    wo = c.sb("a0_wo", [P, heads_out, D], F32, scope)
    bo = c.sb("a0_bo", [P, D], F32, scope)
    o8 = c.sb("a0_o", [P, groups, T], F32, scope)
    pos.query = c.sb("a0_query", [P, S], F32, scope)
    pos.key = c.sb("a0_key", [P, S], F32, scope)
    pos.causal = c.sb("a0_causal", [P, S], BF16, scope)
    causal32 = c.sb("a0_causal32", [P, S], F32, scope)

    def sync(sp):
        sp.wait_ge(x_ready, TT * norm_use)
        weights.dma(sp, pos.query[:], dram["pos_query"])
        weights.dma(sp, pos.key[:], dram["pos_key"])
        weights.dma(sp, causal32[:], dram["causal"])
        weights.dma(sp, bo[:], bc(dram["L0_attn_out_bias"], 0, P))
        weights.dma(sp, wo[:], dram["L0_attn_out_kernel"].rearrange("(k p) n -> p k n", p=P))

    def gpsimd(pool):
        weights.wait(pool)
        pool.tensor_copy(pos.causal[:], causal32[:]).then_inc(prepared, 1)

    def vector(dve):
        weights.wait(dve)

    prep.sync, prep.gpsimd, prep.vector = sync, gpsimd, vector
    ready = [(c.sem("feat_act"), 2 * (norm_use + 1)), (c.sem("feat_dve"), 2 * (norm_use + 1)),
             (prepared, 1), (weights.sem, weights.total)]
    early = (2, 3)

    def before_last_turn(pe):
        pe.wait_ge(prepared, 2)
        pe.wait_ge(c.sem("w_o_moved"), 2 * (groups - 1))
        early_products(c, pe, o8, groups, wo, early)

    core, done = nested(c, scope, lambda: wide_attention(
        c, "a0", 0, groups, (dram["L0_attn_w"], dram["L0_attn_pos"]), c.xn_feat, ready, o8,
        qkv_scale, pos,
        [(x_ready, TT * norm_use)], (0, 0), xin_ready_first=feat_ready(c, norm_use, 0),
        before_last_turn=before_last_turn))
    scaling = Stage()

    def gpsimd(pool):
        pool.tensor_scalar(wo[:], wo[:], out_scale, None, ALU.mult).then_inc(prepared, 1)

    scaling.gpsimd = gpsimd
    out = out_projection(c, norm_use, out_use, o8, groups, wo, weights, [done, (prepared, 2)], bo, early)
    return [prep, core.first, core, scaling, out]


def nested(c, scope, make):
    result = make()
    scope.close()
    return result


def narrow_attention(c, q_scaled, k_all, v_w, v_cols, inputs_ready, norm_use, diag_base, scratch_scope):
    s = Stage()
    pairs = 8
    xb = [c.sb(f"n_x{i}", [P, DC, 2, S], F32, scratch_scope) for i in range(2)]
    q_diag = [c.sb(f"n_qd{i}", [P, DC, 8, S], F32, scratch_scope) for i in range(2)]
    v2 = [c.sb(f"n_v{i}", [P, D], F32, scratch_scope) for i in range(2)]
    probs = [c.sb(f"n_p{i}", [P, pairs, S], F32, scratch_scope) for i in range(2)]
    probs_t = c.sb("n_pt", [P, BANK], F32, scratch_scope)
    neg_max = c.sb("n_nm", [P, 2, pairs], F32, scratch_scope)
    row_sum = c.sb("n_rs", [P, 2, pairs], F32, scratch_scope)
    o_half = c.sb("n_oh", [P, DC, S], F32, scratch_scope)
    diag_ready, x_twice = c.sem("n_diag_ready"), c.sem("n_x_twice")
    scores_done, max_done = c.sem("n_scores_done"), c.sem("n_max_done")
    shifted, exp_done, sum_done = c.sem("n_shifted"), c.sem("n_exp_done"), c.sem("n_sum_done")
    inv_done, probs_ready, turned = c.sem("n_inv_done"), c.sem("n_probs_ready"), c.sem("n_turned")
    pt_moved, v_done, v_moved = c.sem("n_pt_moved"), c.sem("n_v_done"), c.sem("n_v_moved")
    pv_done, half_ready, o_moved = c.sem("n_pv_done"), c.sem("n_half_ready"), c.sem("n_o_moved")
    V_BANK, TURN_BANK, O_BANK = 4, 5, 6

    def gpsimd(pool):
        for sem, value in inputs_ready:
            pool.wait_ge(sem, value)

        def diagonal(b, half):
            for m in range(DC):
                pool.tensor_tensor(q_diag[half][:, m, :, :], bc(q_scaled[:, m, bass.ds(S * b, S)], 1, 8),
                                   bc(c.head_rows[:], 2, S), ALU.mult).then_inc(diag_ready, 1)

        def twice(b, half):
            pool.tensor_copy(xb[half][:], bc(c.xn_feat[:, :, bass.ds(S * b, S)], 2, 2)).then_inc(x_twice, 1)

        def body(i, last=False):
            for half in range(2):
                b = 2 * i + half
                if not (last and half == 1):
                    pool.wait_ge(scores_done, b)
                    diagonal(b + 1, 1 - half)
                pool.wait_ge(v_done, b - 1)
                twice(b, half)

        for b in range(2):
            diagonal(b, b)
            twice(b, b)
        pool.wait_ge(scores_done, 1)
        diagonal(2, 0)
        with pool.Fori(1, B // 2 - 1) as i:
            body(i)
        body(B // 2 - 1, last=True)

    def tensor(pe, start):
        def scores(b, half):
            pe.wait_ge(diag_ready, DC * (b + 1))
            wait_free(pe, shifted, b - 1)
            for i in range(pairs):
                m, j = divmod(i, 4)
                ins = pe.matmul(c.psum[:, half, i * S:(i + 1) * S],
                                q_diag[half][:, m, 2 * j:2 * j + 2, :].rearrange("p j q -> p (j q)"),
                                k_all[:, m, bass.ds(S * b, S)], start=True, stop=True)
            ins.then_inc(scores_done, 1)

        def project_v(b, half, before_last=lambda: None):
            pe.wait_ge(x_twice, b + 1)
            wait_free(pe, v_moved, b)
            for k in range(DC):
                if k == DC - 1:
                    before_last()
                ins = pe.matmul(c.psum[:, V_BANK, 0:D], xb[half][:, k, :, :].rearrange("p a s -> p (a s)"),
                                v_w[:, k, :], start=(k == 0), stop=(k == DC - 1))
            ins.then_inc(v_done, 1)

        def turn(b, half):
            pe.wait_ge(probs_ready, b + 1)
            wait_free(pe, pt_moved, b)
            for u in range(pairs // 2):
                ins = pe.transpose(c.psum[:, TURN_BANK, u * P:(u + 1) * P],
                                   probs[half][:, 2 * u:2 * u + 2, :].rearrange("p t k -> p (t k)"),
                                   c.identity[:])
            ins.then_inc(turned, 1)

        def values_ready(b):
            pe.wait_ge(pt_moved, b + 1)
            pe.wait_ge(v_moved, b + 1)
            wait_free(pe, o_moved, b)

        def values(b, half):
            for i in range(pairs):
                m, j = divmod(i, 4)
                u, rows = i // 2, slice((i % 2) * S, (i % 2 + 1) * S)
                ins = pe.matmul(c.psum[32 * j:32 * j + 32, O_BANK, m * P:(m + 1) * P],
                                v2[half][rows, 32 * i:32 * i + 32], probs_t[rows, u * P:(u + 1) * P],
                                start=True, stop=True)
            ins.then_inc(pv_done, 1)

        def body(i, first=False, last=False):
            for half in range(2):
                b = 2 * i + half
                before = not (first and half == 0)
                if before:
                    turn(b - 1, 1 - half)
                if not (last and half == 1):
                    scores(b + 1, 1 - half)
                if before:
                    project_v(b, half, before_last=lambda: values_ready(b - 1))
                    values(b - 1, 1 - half)
                else:
                    project_v(b, half)

        if start:
            for sem, value in inputs_ready:
                pe.wait_ge(sem, value)
            scores(0, 0)
            return
        body(0, first=True)
        with pe.Fori(1, B // 2 - 1) as i:
            body(i)
        body(B // 2 - 1, last=True)
        turn(B - 1, 1)
        values_ready(B - 1)
        values(B - 1, 1)

    def scalar(act):
        for sem, value in inputs_ready:
            act.wait_ge(sem, value)

        def exps(b, half):
            act.wait_ge(shifted, b + 1)
            act.activation(probs[half][:], probs[half][:], ACT.Exp).then_inc(exp_done, 1)

        def move_v(b, half):
            act.wait_ge(v_done, b + 1)
            act.activation(v2[half][:], c.psum[:, V_BANK, 0:D], ACT.Copy).then_inc(v_moved, 1)

        def move_turned(b):
            act.wait_ge(turned, b + 1)
            act.activation(probs_t[:], c.psum[:, TURN_BANK, :], ACT.Copy).then_inc(pt_moved, 1)

        def other_head(b):
            act.wait_ge(pv_done, b + 1)
            wait_free(act, o_moved, b)
            src = c.psum[:, O_BANK, 0:DC * P].rearrange("p (m h q) -> p m h q", m=DC, h=2)
            for m in range(DC):
                ins = act.activation(o_half[:, m, :], src[:, m, 1, :], ACT.Identity,
                                     scale=c.half_rows[:, 1:2], bias=v_cols[:, m:m + 1])
            ins.then_inc(half_ready, 1)

        def body(i, first=False):
            for half in range(2):
                b = 2 * i + half
                exps(b, half)
                if not first:
                    other_head(b - 2)
                if not (first and half == 0):
                    move_turned(b - 1)
                move_v(b, half)

        body(0, first=True)
        with act.Fori(1, B // 2) as i:
            body(i)
        other_head(B - 2)
        move_turned(B - 1)
        other_head(B - 1)

    def vector(dve):
        for sem, value in inputs_ready:
            dve.wait_ge(sem, value)

        def softmax(b, half):
            src = c.psum[:, half, :].rearrange("p (t k) -> p t k", t=pairs)
            dve.wait_ge(scores_done, b + 1)
            dve.tensor_reduce(neg_max[:, half, :], src, AX.X, ALU.max, negate=True).then_inc(max_done, 1)
            dve.wait_ge(max_done, b + 1)
            dve.tensor_tensor(probs[half][:], src, bc(neg_max[:, half, :], 2, S), ALU.add).then_inc(shifted, 1)

        def normalize(b, half):
            dve.wait_ge(exp_done, b + 1)
            dve.tensor_reduce(row_sum[:, half, :], probs[half][:], AX.X, ALU.add).then_inc(sum_done, 1)
            dve.wait_ge(sum_done, b + 1)
            dve.reciprocal(row_sum[:, half, :], row_sum[:, half, :]).then_inc(inv_done, 1)
            dve.wait_ge(inv_done, b + 1)
            dve.tensor_tensor(probs[half][:], probs[half][:], bc(row_sum[:, half, :], 2, S), ALU.mult)\
               .then_inc(probs_ready, 1)

        def move_o(b):
            src = c.psum[:, O_BANK, 0:DC * P].rearrange("p (m h q) -> p m h q", m=DC, h=2)
            dve.wait_ge(half_ready, b + 1)
            dve.scalar_tensor_tensor(c.o_feat[:, :, bass.ds(S * b, S)], src[:, :, 0, :], c.half_rows[:, 0:1],
                                     o_half[:], ALU.mult, ALU.add).then_inc(o_moved, 1)

        def body(i, first=False, last=False):
            for half in range(2):
                b = 2 * i + half
                normalize(b, half)
                if not first:
                    move_o(b - 2)
                if not (last and half == 1):
                    softmax(b + 1, 1 - half)

        softmax(0, 0)
        body(0, first=True)
        with dve.Fori(1, B // 2 - 1) as i:
            body(i)
        body(B // 2 - 1, last=True)
        move_o(B - 2)
        move_o(B - 1)

    s.start = lambda pe: tensor(pe, True)
    s.gpsimd, s.tensor, s.scalar, s.vector = gpsimd, (lambda pe: tensor(pe, False)), scalar, vector
    return s, (o_moved, B)


def feature_projection(c, name, weight, xin, ready, move, move_act):
    s = Stage()
    done = c.sem(f"{name}_done")

    def tensor(pe):
        for sem, value in ready:
            pe.wait_ge(sem, value)
        for u in range(DC * NH):
            m, n = divmod(u, NH)
            for k in range(DC):
                ins = pe.matmul(c.psum[:, u, :], weight[:, k, m * P:(m + 1) * P],
                                xin[:, k, n * BANK:(n + 1) * BANK], start=(k == 0), stop=(k == DC - 1))
            ins.then_inc(done, 1)

    def scalar(act):
        for u in range(DC * NH):
            act.wait_ge(done, u + 1)
            move_act(act, u, c.psum[:, u, :])

    def vector(dve):
        for u in range(DC * NH):
            move(dve, u)

    s.tensor, s.scalar, s.vector = tensor, scalar, vector
    return s


def second_self_attention(c, dram, norm_use, out_use):
    weights = Loads(c, "a1_weights", 12)
    x_ready, prepared = c.sem("x_ready"), c.sem("a1_prepared")
    scope = ExitStack()
    names = ["Wq", "Wk", "Wv", "Wo", "gate", "ca_Wout", "mc_Wout"]
    w = {n: c.sb(f"a1_{n}", [P, DC, D], F32, scope) for n in names}
    cols = c.sb("a1_cols", [P, 6, DC], F32, scope)
    am_w = c.sb("a1_am_w", [16, D], F32, scope)
    cons = c.sb("a1_cons", [16, 1], F32, scope)
    bo = c.sb("a1_bo", [P, D], F32, scope)
    gate = c.sb("a1_gate_value", [P, DC, T], F32, scope)
    k_all = c.sb("a1_k", [P, DC, T], F32, scope)
    mixed = c.sb("a1_mixed", [P, DC, T], F32, scope)
    inner = c.sb("a1_inner", [P, DC, T], F32, scope)
    o_wide = c.sb("a1_o_wide", [P, DC, T], F32, scope)
    neg_gate = c.sb("a1_neg_gate", [P, DC], F32, scope)
    wide_tiles = {n: wide_weight_tiles(c, n, scope) for n in ("ca", "mc")}
    gate_bias_done = c.sem("a1_gate_bias")
    stages = []

    prep = Stage()

    def sync(sp):
        sp.wait_ge(x_ready, TT * norm_use)
        weights.dma(sp, cols[:], dram["a1_cols"])
        weights.dma(sp, am_w[:], dram["am_w"])
        weights.dma(sp, cons[:], dram["L1_attn_cons_vec"].rearrange("(n a) -> n a", a=1))
        weights.dma(sp, bo[:], bc(dram["L1_attn_bo"], 0, P))
        for n in names:
            src = "a1_gate" if n == "gate" else f"L1_attn_{n}"
            weights.dma(sp, w[n][:], dram[src].rearrange("(k p) n -> p k n", p=P))
        weights.dma(sp, neg_gate[:], dram["am_b_cols"])

    def tensor(pe):
        weights.wait(pe)
        for m in range(DC):
            ins = pe.matmul(c.psum[:, 3, m:m + 1], am_w[:, m * P:(m + 1) * P], cons[:],
                            start=True, stop=True)
        ins.then_inc(gate_bias_done, 1)

    def gpsimd(pool):
        weights.wait(pool)
        pool.tensor_scalar(cols[:, 4, :], cols[:, 4, :], CAUSAL_W, None, ALU.mult).then_inc(prepared, 1)
        pool.tensor_scalar(cols[:, 5, :], cols[:, 5, :], META_W, None, ALU.mult).then_inc(prepared, 1)

    def vector(dve):
        weights.wait(dve)
        dve.wait_ge(gate_bias_done, 1)
        dve.tensor_tensor(cols[:, 3, :], c.psum[:, 3, 0:DC], cols[:, 3, :], ALU.add).then_inc(prepared, 1)
        dve.wait_ge(prepared, 3)
        dve.tensor_tensor(neg_gate[:], cols[:, 3, :], neg_gate[:], ALU.add).then_inc(prepared, 1)
        dve.wait_ge(prepared, 4)
        dve.tensor_scalar(neg_gate[:], neg_gate[:], -1.0, None, ALU.mult).then_inc(prepared, 1)

    def scalar(act):
        act.wait_ge(prepared, 5)

    prep.sync, prep.tensor, prep.gpsimd, prep.vector, prep.scalar = sync, tensor, gpsimd, vector, scalar
    stages.append(prep)

    feat = [(c.sem("feat_act"), 2 * (norm_use + 1)), (c.sem("feat_dve"), 2 * (norm_use + 1)),
            (weights.sem, weights.total)]
    proj = Stage()
    p_done, p_moved = c.sem("a1_p_done"), c.sem("a1_p_moved")
    plus_one, gate_done, q_gated = c.sem("a1_plus_one"), c.sem("a1_gate_done"), c.sem("a1_q_gated")
    jobs = [("gate", gate), ("Wq", c.q_feat), ("Wk", k_all)]
    units = DC * NH

    def tensor(pe):
        for a, (n, _) in enumerate(jobs):
            for u in range(units):
                m, h = divmod(u, NH)
                v = a * units + u
                if v < NH:
                    wait_feat(c, pe, norm_use, h)
                if v >= 3:
                    pe.wait_ge(p_moved, v - 2)
                for k in range(DC):
                    ins = pe.matmul(c.psum[:, v % 3, :], w[n][:, k, m * P:(m + 1) * P],
                                    c.xn_feat[:, k, h * BANK:(h + 1) * BANK],
                                    start=(k == 0), stop=(k == DC - 1))
                ins.then_inc(p_done, 1)

    def scalar(act):
        for a, (n, dst) in enumerate(jobs):
            for u in range(units):
                m, h = divmod(u, NH)
                v = a * units + u
                act.wait_ge(p_done, v + 1)
                out = dst[:, m, h * BANK:(h + 1) * BANK]
                if n == "gate":
                    act.activation(out, c.psum[:, v % 3, :], ACT.Exp, scale=-1.0,
                                   bias=neg_gate[:, m:m + 1]).then_inc(p_moved, 1)
                else:
                    act.activation(out, c.psum[:, v % 3, :], ACT.Identity,
                                   bias=cols[:, a - 1, m:m + 1]).then_inc(p_moved, 1)

    def vector(dve):
        for m in range(DC):
            dve.wait_ge(p_moved, NH * (m + 1))
            dve.tensor_scalar(gate[:, m, :], gate[:, m, :], 1.0, None, ALU.add).then_inc(plus_one, 1)
            dve.wait_ge(plus_one, m + 1)
            dve.reciprocal(gate[:, m, :], gate[:, m, :]).then_inc(gate_done, 1)
        for m in range(DC):
            dve.wait_ge(gate_done, m + 1)
            dve.wait_ge(p_moved, units + NH * (m + 1))
            dve.tensor_tensor(c.q_feat[:, m, :], c.q_feat[:, m, :], gate[:, m, :], ALU.mult)\
               .then_inc(q_gated, 1)

    proj.tensor, proj.scalar, proj.vector = tensor, scalar, vector
    stages.append(proj)

    narrow_scope = ExitStack()
    core, main_done = narrow_attention(
        c, c.q_feat, k_all, w["Wv"], cols[:, 2, :], feat + [(q_gated, DC), (p_moved, 3 * units), (prepared, 5)],
        norm_use, None, narrow_scope)
    ca, ca_done = wide_attention(
        c, "ca", 1, DC, (dram["ca_w"],), c.xn_feat, feat, o_wide, 1.0,
        None, [(x_ready, TT * norm_use)], (8, 8), wide_tiles["ca"], banks_free=[(p_moved, 3 * units)],
        middle=core.start)
    narrow_scope.close()
    stages += [ca.first, core, ca]

    ca_moved, mixed_done = c.sem("ca_out_moved"), c.sem("mixed_done")

    def take(sem, dst, column, factor):
        def move_act(act, u, bank):
            m, n = divmod(u, NH)
            act.activation(dst[:, m, n * BANK:(n + 1) * BANK], bank, ACT.Identity, scale=factor,
                           bias=cols[:, column, m:m + 1]).then_inc(sem, 1)
        return move_act

    def mix(dst, old, added, sem, factor, done):
        def move(dve, u):
            m, n = divmod(u, NH)
            at = slice(n * BANK, (n + 1) * BANK)
            dve.wait_ge(sem, u + 1)
            dve.scalar_tensor_tensor(dst[:, m, at], old[:, m, at], 1.0 - factor, added[:, m, at],
                                     ALU.mult, ALU.add).then_inc(done, 1)
        return move

    stages.append(feature_projection(c, "ca_out", w["ca_Wout"], o_wide, [ca_done],
                                     mix(mixed, c.o_feat, inner, ca_moved, CAUSAL_W, mixed_done),
                                     take(ca_moved, inner, 4, CAUSAL_W)))
    mc, mc_done = wide_attention(
        c, "mc", 2, DC, (dram["mc_w"],), mixed, [(mixed_done, 4)], o_wide, 1.0,
        None, [(mixed_done, 4)], (10, 8), wide_tiles["mc"])
    stages += [mc.first, mc]
    mc_moved, final_done = c.sem("mc_out_moved"), c.sem("final_done")
    stages.append(feature_projection(c, "mc_out", w["mc_Wout"], o_wide, [mc_done],
                                     mix(k_all, mixed, inner, mc_moved, META_W, final_done),
                                     take(mc_moved, inner, 5, META_W)))
    scope.close()
    stages.append(out_projection(c, norm_use, out_use, k_all, DC, w["Wo"], weights, [(final_done, 4)], bo))
    return stages


def quantized_ffn(c, dram, norm_use, stat_use, ahead):
    s = Stage()
    scope = ExitStack()
    loads = Loads(c, "f_loads", 8)
    ternary = [c.sb("f_w1", [P, DC, HID], BF16, scope), c.sb("f_w2", [P, HC, D], BF16, scope)]
    g1, b1n = c.sb("f_g1", [P, D], F32, scope), c.sb("f_b1n", [P, D], F32, scope)
    g2, b2n = c.sb("f_g2", [P, HID], F32, scope), c.sb("f_b2n", [P, HID], F32, scope)
    bias1, bias2 = c.sb("f_bias1", [P, HID], F32, scope), c.sb("f_bias2", [P, D], F32, scope)
    asum = c.sb("f_asum", [P, 2], F32, scope)
    w_mean, w_inv = c.sb("f_wmean", [P, 2], F32, scope), c.sb("f_winv", [P, 2], F32, scope)
    top = c.sb("f_top", [P, 2, TT], F32, scope)
    q_scale, back = c.sb("f_qscale", [P, 2, TT], F32, scope), c.sb("f_back", [P, 2, TT], F32, scope)
    shift = c.sb("f_shift", [P, TT], F32, scope)
    x1 = c.sb("f_x1", [P, TT, D], F32, scope)
    x1_feat = c.sb("f_x1_feat", [P, DC, T], BF16, scope)
    hid = c.sb("f_hid", [P, TT, HID], F32, scope)
    raw = [hid[:, 4:6, :], hid[:, 6:8, :].rearrange("p a (k n) -> p (a k) n", n=D)]
    hid_feat = [c.sb(f"f_hid_feat{i}", [P, HC, P], BF16, scope) for i in range(2)]
    ahead.allocate_context(scope)
    scope.close()
    x_ready, xn_ready = c.sem("x_ready"), c.sem("xn_ready")
    rows = [RowStatistics(c, stat_use + i) for i in range(2)]
    following = c.norms.get(norm_use + 1)
    step = c.sem("f_step")
    asum_done, total_done, w_inv_ready = c.sem("f_asum_done"), c.sem("f_total_done"), c.sem("f_w_inv_ready")
    w2_step = c.sem("f_w2_step")
    q1_ready, q1_turned, q1_moved = c.sem("f_q1_ready"), c.sem("f_q1_turned"), c.sem("f_q1_moved")
    w1_ready = c.sem("f_w1_ready")
    up_done, up_moved, gelu_done = c.sem("f_up_done"), c.sem("f_up_moved"), c.sem("f_gelu_done")
    shift_ready, scaled, gained = c.sem("f_shift_ready"), c.sem("f_scaled"), c.sem("f_gained")
    q2_ready, q2_turned, q2_moved = c.sem("f_q2_ready"), c.sem("f_q2_turned"), c.sem("f_q2_moved")
    down_done, f_bias_added = c.sem("f_down_done"), c.sem("f_bias_added")
    FIRST, BETWEEN, AFTER = range(0, 8), range(8, 12), range(12, ahead.JOBS)

    def sync(sp):
        ahead.load_weights(sp)
        sp.wait_ge(x_ready, TT * norm_use)
        for b in range(4):
            ahead.load(sp, b)
        for dst, name in ((g1, "ln1_g"), (b1n, "ln1_b")):
            loads.dma(sp, dst[:], bc(dram[f"L0_ffn_{name}"], 0, P))
        loads.dma(sp, raw[0], dram["w1_t"].rearrange("(k p) n -> p k n", p=P))
        loads.dma(sp, raw[1], dram["w2_t"].rearrange("(k p) n -> p k n", p=P))
        for dst, name in ((bias1, "b1"), (g2, "ln2_g"), (b2n, "ln2_b"), (bias2, "b2")):
            loads.dma(sp, dst[:], bc(dram[f"L0_ffn_{name}"], 0, P))
        for b in range(4, B):
            ahead.load(sp, b)

    def make_ternary(eng, a, sem, base):
        eng.tensor_scalar(raw[a], raw[a], w_inv[:, a:a + 1], ROUND, ALU.mult, ALU.add).then_inc(sem, 1)
        eng.wait_ge(sem, base + 1)
        eng.tensor_scalar(raw[a], raw[a], ROUND, 1.0, ALU.subtract, ALU.min).then_inc(sem, 1)
        eng.wait_ge(sem, base + 2)
        eng.tensor_scalar(ternary[a][:], raw[a], -1.0, None, ALU.max).then_inc(sem, 1)

    def gpsimd(pool):
        pool.wait_ge(w_inv_ready, 1)
        make_ternary(pool, 1, w2_step, 0)
        pool.wait_ge(xn_ready, TT * (norm_use + 1))
        pool.tensor_tensor(c.x_tok[:], c.x_tok[:], bc(bias2[:], 1, TT), ALU.add).then_inc(f_bias_added, 1)
        for t in range(1, TT):
            pool.wait_ge(scaled, t + 1)
            pool.tensor_tensor(hid[:, t, :], hid[:, t, :], g2[:], ALU.mult).then_inc(gained, 1)

    def vector(dve):
        count = [0]

        def mark(ins):
            count[0] += 1
            ins.then_inc(step, 1)
            return count[0]

        def after(ins):
            dve.wait_ge(step, mark(ins))

        def pipelined(n, first, second):
            marks = []
            for t in range(n + 1):
                if t < n:
                    marks.append(mark(first(t)))
                if t:
                    dve.wait_ge(step, marks[t - 1])
                    last = second(t - 1)
            return last

        def scales(a, at):
            after(dve.tensor_scalar(top[:, a, at], top[:, a, at], 1e-5, None, ALU.max))
            after(dve.reciprocal(q_scale[:, a, at], top[:, a, at]))
            dve.tensor_scalar(back[:, a, at], top[:, a, at], w_mean[:, a:a + 1], 1.0 / 127.0,
                              ALU.mult, ALU.mult).then_inc(step, 1)
            count[0] += 1
            after(dve.tensor_scalar(q_scale[:, a, at], q_scale[:, a, at], 127.0, None, ALU.mult))

        dve.wait_ge(xn_ready, TT * (norm_use + 1))
        for t in range(TT):
            rows[0].tile(dve, t, [c.xn_tok[:, t, :]])
        rows[0].finish(dve)
        loads.wait(dve)
        after(pipelined(TT, lambda t: dve.scalar_tensor_tensor(
            x1[:, t, :], c.xn_tok[:, t, :], c.mean_var[:, t, 0:1], g1[:], ALU.subtract, ALU.mult),
                        lambda t: dve.scalar_tensor_tensor(
            x1[:, t, :], x1[:, t, :], c.rstd[:, t:t + 1], b1n[:], ALU.mult, ALU.add)))
        mark(dve.tensor_reduce(top[:, 0, :], x1[:], AX.X, ALU.max, apply_absolute_value=True))
        dve.wait_ge(total_done, 1)
        after(dve.tensor_scalar(w_mean[:], c.psum[:, 7, 0:2], 1.0 / (D * HID), 1e-5, ALU.mult, ALU.max))
        dve.reciprocal(w_inv[:], w_mean[:]).then_inc(w_inv_ready, 1)
        scales(0, slice(0, TT))
        pipelined(TT, lambda t: dve.tensor_scalar(
            x1[:, t, :], x1[:, t, :], q_scale[:, 0, t:t + 1], ROUND, ALU.mult, ALU.add),
                  lambda t: dve.tensor_scalar(
            x1[:, t, :], x1[:, t, :], ROUND, 127.0, ALU.subtract, ALU.min).then_inc(q1_ready, 1))
        dve.wait_ge(w_inv_ready, 1)
        make_ternary(dve, 0, w1_ready, 0)
        for t in range(TT + 1):
            if t < TT:
                dve.wait_ge(up_done, t + 1)
                if t == 6:
                    dve.wait_ge(w2_step, 3)
                src = c.psum[:, 4 + 2 * (t % 2):6 + 2 * (t % 2), :]
                dve.scalar_tensor_tensor(hid[:, t, :].rearrange("p (a n) -> p a n", a=2), src,
                                         back[:, 0, t:t + 1], bias1[:].rearrange("p (a n) -> p a n", a=2),
                                         ALU.mult, ALU.add).then_inc(up_moved, 1)
            if t:
                dve.wait_ge(gelu_done, t)
                rows[1].tile(dve, t - 1, [hid[:, t - 1, h * BANK:(h + 1) * BANK] for h in range(2)])
        rows[1].finish(dve, 2)
        dve.scalar_tensor_tensor(shift[:], c.mean_var[:, :, 0], -1.0, c.rstd[:], ALU.mult, ALU.mult)\
           .then_inc(shift_ready, 1)

        def add_shift(t):
            if t:
                dve.wait_ge(gained, t)
            else:
                dve.wait_ge(scaled, 1)
                after(dve.tensor_tensor(hid[:, 0, :], hid[:, 0, :], g2[:], ALU.mult))
            return dve.tensor_tensor(hid[:, t, :], hid[:, t, :], b2n[:], ALU.add)

        per = TT // 2
        for first in range(0, TT, per):
            after(pipelined(per, lambda t: add_shift(first + t), lambda t: dve.tensor_reduce(
                top[:, 1, first + t:first + t + 1], hid[:, first + t, :], AX.X, ALU.max,
                apply_absolute_value=True)))
            scales(1, slice(first, first + per))
            pipelined(per, lambda t: dve.tensor_scalar(
                hid[:, first + t, :], hid[:, first + t, :], q_scale[:, 1, first + t:first + t + 1], ROUND,
                ALU.mult, ALU.add),
                      lambda t: dve.tensor_scalar(
                hid[:, first + t, :], hid[:, first + t, :], ROUND, 127.0, ALU.subtract, ALU.min)
                      .then_inc(q2_ready, 1))
        dve.wait_ge(f_bias_added, 1)
        for t in range(TT):
            dve.wait_ge(down_done, t + 1)
            dve.scalar_tensor_tensor(c.x_tok[:, t, :], c.psum[:, 4 + t % 4, 0:D], back[:, 1, t:t + 1],
                                     c.x_tok[:, t, :], ALU.mult, ALU.add).then_inc(x_ready, 1)
            if following:
                following.follow(dve, t)

    def scalar(act):
        for job in FIRST:
            if job == 4:
                loads.wait(act)
                for a in range(2):
                    act.activation(ternary[a][:], raw[a], ACT.Abs, accum_out=asum[:, a:a + 1])\
                       .then_inc(asum_done, 1)
            ahead.move(act, [job])
        for k in range(TT // 2):
            act.wait_ge(q1_turned, k + 1)
            act.activation(x1_feat[:, :, 2 * P * k:2 * P * (k + 1)],
                           c.psum[:, k, :].rearrange("p (c n) -> p c n", c=DC), ACT.Copy).then_inc(q1_moved, 1)
        for t in range(TT):
            act.wait_ge(up_moved, t + 1)
            act.activation(hid[:, t, :], hid[:, t, :], ACT.Gelu).then_inc(gelu_done, 1)
            ahead.move(act, BETWEEN[t:t + 1])
        before = len(AFTER) - TT
        ahead.move(act, AFTER[:before])
        act.wait_ge(shift_ready, 1)
        for t in range(TT):
            act.activation(hid[:, t, :], hid[:, t, :], ACT.Identity, scale=c.rstd[:, t:t + 1],
                           bias=shift[:, t:t + 1]).then_inc(scaled, 1)
            ahead.move(act, [AFTER[before + t]])
        for t in range(TT):
            for a in range(2):
                act.wait_ge(q2_turned, 2 * t + a + 1)
                if t >= 2:
                    act.wait_ge(down_done, t - 1)
                act.activation(hid_feat[t % 2][:, 4 * a:4 * a + 4, :],
                               c.psum[:, 2 * (t % 2) + a, :].rearrange("p (k n) -> p k n", k=4), ACT.Copy)\
                   .then_inc(q2_moved, 1)

    def tensor(pe):
        wait_feat(c, pe, norm_use)
        ahead.project(pe, FIRST)
        pe.wait_ge(asum_done, 2)
        pe.matmul(c.psum[:, 7, 0:2], c.ones[:], asum[:], start=True, stop=True).then_inc(total_done, 1)
        pe.wait_ge(ahead.moved, len(FIRST))
        for t in range(TT):
            pe.wait_ge(q1_ready, t + 1)
            bank = c.psum[:, t // 2, :].rearrange("p (c n) -> p c n", c=DC)
            for m in range(DC):
                ins = pe.transpose(bank[:, m, (t % 2) * P:(t % 2 + 1) * P], x1[:, t, m * P:(m + 1) * P],
                                   c.identity[:])
            if t % 2:
                ins.then_inc(q1_turned, 1)
        pe.wait_ge(w1_ready, 3)
        for t in range(TT):
            pe.wait_ge(q1_moved, t // 2 + 1)
            if t >= 2:
                pe.wait_ge(up_moved, t - 1)
            for n in range(2):
                for k in range(DC):
                    ins = pe.matmul(c.psum[:, 4 + 2 * (t % 2) + n, :], x1_feat[:, k, t * P:(t + 1) * P],
                                    ternary[0][:, k, n * BANK:(n + 1) * BANK],
                                    start=(k == 0), stop=(k == DC - 1))
            ins.then_inc(up_done, 1)
            if t == 0:
                pe.wait_ge(q1_moved, TT // 2)
            ahead.project(pe, BETWEEN[t:t + 1])
        ahead.project(pe, AFTER)
        pe.wait_ge(ahead.moved, ahead.JOBS)
        pe.wait_ge(up_moved, TT)

        def turn(t):
            pe.wait_ge(q2_ready, t + 1)
            if t >= 2:
                pe.wait_ge(q2_moved, 2 * (t - 1))
            for a in range(2):
                for k in range(4):
                    ins = pe.transpose(c.psum[:, 2 * (t % 2) + a, k * P:(k + 1) * P],
                                       hid[:, t, (4 * a + k) * P:(4 * a + k + 1) * P], c.identity[:])
                ins.then_inc(q2_turned, 1)

        pe.wait_ge(w2_step, 3)
        turn(0)
        for t in range(TT):
            if t + 1 < TT:
                turn(t + 1)
            pe.wait_ge(q2_moved, 2 * (t + 1))
            if t >= 4:
                pe.wait_ge(x_ready, TT * norm_use + t - 3)
            for k in range(HC):
                ins = pe.matmul(c.psum[:, 4 + t % 4, 0:D], hid_feat[t % 2][:, k, :], ternary[1][:, k, :],
                                start=(k == 0), stop=(k == HC - 1))
            ins.then_inc(down_done, 1)

    s.sync, s.gpsimd, s.vector, s.scalar, s.tensor = sync, gpsimd, vector, scalar, tensor
    return [s]


def expert_ffn(c, dram, norm_use):
    s = Stage()
    scope = ExitStack()
    sh_in, wr_in = c.sem("m_sh_in"), c.sem("m_wr_in")
    up_in = [c.sem("m_up_in0"), c.sem("m_up_in1")]
    down_in = [c.sem("m_down_in0"), c.sem("m_down_in1")]
    F = P

    def weights(name, shape):
        return (c.sb(f"{name}_raw", shape, F32, scope), c.sb(f"{name}_high", shape, F32R, scope),
                c.sb(f"{name}_low", shape, F32R, scope))

    up_sh, down_sh = weights("m_up_sh", [P, DC, F]), weights("m_down_sh", [P, D])
    up = [weights(f"m_up{i}", [P, DC, F]) for i in range(2)]
    down = [weights(f"m_down{i}", [P, D]) for i in range(2)]
    wr = c.sb("m_wr", [P, DC, EXPERTS], F32, scope)
    logits = c.sb("m_logits", [P, TT, EXPERTS], F32, scope)
    best = c.sb("m_best", [P, TT, 8], F32, scope)
    chance = c.sb("m_chance", [P, TT], F32, scope)
    prob = c.sb("m_prob", [P, TT, EXPERTS], F32, scope)
    x_parts = [c.sb(f"m_x_{n}", [P, DC, T], F32R, scope) for n in ("high", "low")]
    act_h = [c.sb(f"m_h{i}", [P, T], F32, scope) for i in range(2)]
    h_parts = [[c.sb(f"m_h_{n}{i}", [P, T], F32R, scope) for n in ("high", "low")] for i in range(2)]
    scope.close()
    norm = c.norms[norm_use]
    norm.want_split(*x_parts)
    x_ready = c.sem("x_ready")
    step = c.sem("m_step")
    logits_done, gap_ready, gap_exp = c.sem("m_logits_done"), c.sem("m_gap_ready"), c.sem("m_gap_exp")
    high_done, sh_split = c.sem("m_high_done"), c.sem("m_sh_split")
    up_split, down_split = c.sem("m_up_split"), c.sem("m_down_split")
    up_done, relu_done, squared, h_ready = c.sem("m_up_done"), c.sem("m_relu_done"), c.sem("m_squared"), c.sem("m_h_ready")
    down_done, added = c.sem("m_down_done"), c.sem("m_added")
    prob_ready = c.sem("m_prob_ready")
    UP_BANK, DOWN_BANK = 0, 4

    def sync(sp):
        sp.wait_ge(x_ready, TT * norm_use)
        sp.dma_start(up_sh[0][:], dram["L1_ffn_Ws1"].rearrange("(k p) n -> p k n", p=P)).then_inc(sh_in, 16)
        sp.dma_start(down_sh[0][:], dram["L1_ffn_Ws2"]).then_inc(sh_in, 16)
        sp.dma_start(wr[:], dram["L1_ffn_Wr"].rearrange("(k p) n -> p k n", p=P)).then_inc(wr_in, 16)

        def load_up(e, slot):
            sp.dma_start(up[slot][0][:], dram["L1_ffn_W1"][e].rearrange("(k p) n -> p k n", p=P))\
              .then_inc(up_in[slot], 16)

        def load_down(e, slot):
            sp.dma_start(down[slot][0][:], dram["L1_ffn_W2"][e]).then_inc(down_in[slot], 16)

        for slot in range(2):
            load_up(slot, slot)
            load_down(slot, slot)
        with sp.Fori(1, EXPERTS // 2) as i:
            for slot in range(2):
                sp.wait_ge(up_split, 2 * i + slot - 1)
                load_up(2 * i + slot, slot)
                sp.wait_ge(down_split, 2 * i + slot - 1)
                load_down(2 * i + slot, slot)

    def gpsimd(pool):
        def split(w, done, base):
            raw, high, low = (buf[:] if len(buf[:].shape) == 3 else buf[:].rearrange("p (k n) -> p k n", n=P)
                              for buf in w)
            pool.tensor_tensor(high, raw, bc(c.ones[:], 1, 2), ALU.mult).then_inc(high_done, 1)
            pool.wait_ge(high_done, base + 1)
            pool.tensor_tensor(low, raw, high.bitcast(F32), ALU.subtract).then_inc(done, 1)

        def split_up(e, slot, pair, base):
            pool.wait_ge(up_in[slot], 16 * (pair + 1))
            if not isinstance(e, int) or e >= 2:
                pool.wait_ge(up_done, NH * e)
            split(up[slot], up_split, base)

        def split_down(e, slot, pair, base):
            pool.wait_ge(down_in[slot], 16 * (pair + 1))
            if not isinstance(e, int) or e >= 2:
                pool.wait_ge(down_done, TT * e)
            split(down[slot], down_split, base)

        def body(i, last=False):
            base = 4 * i + 3
            split_up(2 * i + 1, 1, i, base)
            split_down(2 * i, 0, i, base + 1)
            if not last:
                split_up(2 * i + 2, 0, i + 1, base + 2)
            split_down(2 * i + 1, 1, i, base + (2 if last else 3))

        pool.wait_ge(sh_in, 32)
        split(up_sh, sh_split, 0)
        split_up(0, 0, 0, 1)
        split(down_sh, sh_split, 2)
        body(0)
        with pool.Fori(1, EXPERTS // 2 - 1) as i:
            body(i)
        body(EXPERTS // 2 - 1, last=True)

    def tensor(pe):
        def hidden(wi, h, weight, first=False):
            wait_free(pe, h_ready, NH * (wi - 1))
            for n in range(NH):
                if first:
                    pe.wait_ge(norm.split_ready, 2 * (n + 1))
                for k in range(DC):
                    ins = split_products(pe, c.psum[:, UP_BANK + 2 * h + n, :],
                                         [weight[a][:, k, :] for a in (1, 2)],
                                         [x[:, k, n * BANK:(n + 1) * BANK] for x in x_parts],
                                         start=(k == 0), stop=(k == DC - 1))
                ins.then_inc(up_done, 1)

        def outputs(wi, h, weight):
            for t in range(TT):
                pe.wait_ge(h_ready, NH * wi + t // 4 + 1)
                if isinstance(wi, int) and wi == 0 and t == 3:
                    pe.wait_ge(prob_ready, 1)
                elif isinstance(wi, int) and wi == EXPERTS and t >= 4:
                    pe.wait_ge(x_ready, TT * norm_use + t - 3)
                else:
                    wait_free(pe, added, TT * wi + t - 3)
                ins = split_products(pe, c.psum[:, DOWN_BANK + t % 4, 0:D],
                                     [part[:, t * P:(t + 1) * P] for part in h_parts[h]],
                                     [weight[a][:] for a in (1, 2)], start=True, stop=True)
                ins.then_inc(down_done, 1)

        def expert(e, slot, last):
            if not last:
                pe.wait_ge(up_split, e + 2)
                hidden(e + 2, slot, up[1 - slot])
            pe.wait_ge(down_split, e + 1)
            outputs(e + 1, 1 - slot, down[slot])

        pe.wait_ge(sh_split, 1)
        hidden(0, 0, up_sh, first=True)
        wait_feat(c, pe, norm_use)
        pe.wait_ge(wr_in, 16)
        for t in range(TT):
            for k in range(DC):
                ins = pe.matmul(c.psum[:, 7, t * EXPERTS:(t + 1) * EXPERTS], c.xn_feat[:, k, t * P:(t + 1) * P],
                                wr[:, k, :], start=(k == 0), stop=(k == DC - 1))
        ins.then_inc(logits_done, 1)
        pe.wait_ge(up_split, 1)
        hidden(1, 1, up[0])
        pe.wait_ge(sh_split, 2)
        outputs(0, 0, down_sh)
        with pe.Fori(0, EXPERTS // 2 - 1) as i:
            for slot in range(2):
                expert(2 * i + slot, slot, False)
        for slot in range(2):
            expert(EXPERTS - 2 + slot, slot, slot == 1)

    def scalar(act):
        def relu(wi, h):
            for n in range(NH):
                at = slice(n * BANK, (n + 1) * BANK)
                act.wait_ge(up_done, NH * wi + n + 1)
                if not isinstance(wi, int) or wi >= 2:
                    act.wait_ge(down_done, TT * (wi - 1))
                act.activation(act_h[h][:, at], c.psum[:, UP_BANK + 2 * h + n, :], ACT.Relu)\
                   .then_inc(relu_done, 1)
                act.wait_ge(relu_done, NH * wi + n + 1)
                act.activation(h_parts[h][0][:, at], act_h[h][:, at], ACT.Square)
                act.activation(act_h[h][:, at], act_h[h][:, at], ACT.Square).then_inc(squared, 1)

        relu(0, 0)
        act.wait_ge(gap_ready, 1)
        act.activation(chance[:], chance[:], ACT.Exp).then_inc(gap_exp, 1)
        relu(1, 1)
        with act.Fori(1, EXPERTS // 2) as i:
            for slot in range(2):
                relu(2 * i + slot, slot)
        relu(EXPERTS, 0)

    def vector(dve):
        count = [0]

        def after(ins):
            count[0] += 1
            ins.then_inc(step, 1)
            dve.wait_ge(step, count[0])

        def low_part(wi, h, halves=range(NH)):
            for n in halves:
                at = slice(n * BANK, (n + 1) * BANK)
                dve.wait_ge(squared, NH * wi + n + 1)
                dve.tensor_tensor(h_parts[h][1][:, at], act_h[h][:, at], h_parts[h][0][:, at].bitcast(F32),
                                  ALU.subtract).then_inc(h_ready, 1)

        low_part(0, 0)
        dve.wait_ge(logits_done, 1)
        after(dve.tensor_copy(logits[:], c.psum[:, 7, 0:TT * EXPERTS].rearrange("p (t e) -> p t e", t=TT)))
        for t in range(TT):
            ins = dve.max(best[:, t, :], logits[:, t, :])
        after(ins)
        dve.tensor_tensor(chance[:], best[:, :, 1], best[:, :, 0], ALU.subtract).then_inc(gap_ready, 1)
        dve.wait_ge(gap_exp, 1)
        after(dve.tensor_scalar(chance[:], chance[:], 1.0, None, ALU.add))
        after(dve.reciprocal(chance[:], chance[:]))
        after(dve.tensor_scalar(chance[:], chance[:], 1.0, None, ALU.is_ge))
        after(dve.tensor_tensor(prob[:], logits[:], bc(best[:, :, 0], 2, EXPERTS), ALU.is_equal))
        dve.tensor_tensor(prob[:], prob[:], bc(chance[:], 2, EXPERTS), ALU.mult).then_inc(prob_ready, 1)
        dve.wait_ge(prob_ready, 1)

        def add(wi, weight, last=False, tiles=range(TT)):
            for t in tiles:
                dve.wait_ge(down_done, TT * wi + t + 1)
                if not isinstance(wi, int) or wi:
                    dve.wait_ge(added, TT * (wi - 1) + t + 1)
                ins = dve.scalar_tensor_tensor(c.x_tok[:, t, :], c.psum[:, DOWN_BANK + t % 4, 0:D], weight(t),
                                               c.x_tok[:, t, :], ALU.mult, ALU.add)
                ins.then_inc(x_ready if last else added, 1)

        def add_and_split(wi, weight, h):
            add(wi, weight, tiles=range(0, 2))
            low_part(wi + 1, h, [0])
            add(wi, weight, tiles=range(2, 6))
            low_part(wi + 1, h, [1])
            add(wi, weight, tiles=range(6, TT))

        def chosen(wi):
            return lambda t: prob[:, t, bass.ds(wi - 1, 1)]

        add_and_split(0, lambda t: c.ones[:, 0:1], 1)
        with dve.Fori(0, EXPERTS // 2 - 1) as i:
            add_and_split(2 * i + 1, chosen(2 * i + 1), 0)
            add_and_split(2 * i + 2, chosen(2 * i + 2), 1)
        add_and_split(EXPERTS - 1, lambda t: prob[:, t, EXPERTS - 2:EXPERTS - 1], 0)
        add(EXPERTS, lambda t: prob[:, t, EXPERTS - 1:EXPERTS], last=True)

    s.sync, s.gpsimd, s.tensor, s.scalar, s.vector = sync, gpsimd, tensor, scalar, vector
    return [s]


def store_stage(c, dram, uses):
    s = Stage()
    x_ready, stored = c.sem("x_ready"), c.sem("stored")

    def sync(sp):
        for t in range(0, TT, 2):
            sp.wait_ge(x_ready, TT * uses + t + 2)
            sp.dma_start(dram["out"].rearrange("(t p) d -> p t d", p=P)[:, t:t + 2, :], c.x_tok[:, t:t + 2, :])\
              .then_inc(stored, 16)
        sp.wait_ge(stored, 16 * (TT // 2))

    s.sync = sync
    return s


def perceiver(nc, dram, upto=6):
    ctx = ExitStack()
    with ctx:
        c = Shared(nc, ctx)
        c.cross_weights = {layer: allocate_cross_weights(c, layer) for layer in ("L0", "L1")}
        c.norms = {i: Norm(c, i, i if i < 3 else i + 2, 0 if i in (0, 3) else 4) for i in range(upto)}
        ahead = []

        def feed_forward():
            ahead.append(ContextAhead(c, dram))
            return quantized_ffn(c, dram, 2, 3, ahead[0])

        parts = [
            lambda: cross_attention(c, dram, 0, 0, 0, "L0", False),
            lambda: first_self_attention(c, dram, 1, 1),
            feed_forward,
            lambda: cross_attention(c, dram, 1, 3, 2, "L1", True, ahead[0]),
            lambda: second_self_attention(c, dram, 4, 3),
            lambda: expert_ffn(c, dram, 5),
        ]
        stages = [load_stage(c, dram)]
        for i, part in enumerate(parts[:upto]):
            stages += [c.norms[i].stage(), *part()]
        stages.append(store_stage(c, dram, upto - 1))
        block = ctx.enter_context(nc.Block())

        @block.sync
        def _(sp):
            for s in stages:
                s.sync(sp)

        @block.gpsimd
        def _(pool):
            for s in stages:
                s.gpsimd(pool)

        @block.tensor
        def _(pe):
            for s in stages:
                s.tensor(pe)

        @block.scalar
        def _(act):
            for s in stages:
                s.scalar(act)

        @block.vector
        def _(dve):
            for s in stages:
                s.vector(dve)


UPTO = 6


def kernel(**inputs):
    import numpy as np
    import concourse.bacc as bacc
    from concourse.bass_utils import run_bass_kernel_spmd as run

    a = {name: np.asarray(v) for name, v in inputs.items()}
    lay = {"x": a["x"].reshape(T, D)}

    def columns(v):
        return v.reshape(-1, P).T

    lay["ctx"] = a["ctx_1024"].reshape(B, NKV, DC, P).transpose(0, 3, 2, 1)
    lay["L0_mask"] = a["mask_BxS2_bf1"]
    lay["L1_mask"] = a["mask_BxS2_bk0"]
    for n in ("Wq", "Wk", "Wv", "Wo"):
        lay[f"L0_xattn_{n}"] = a[f"L0_xattn_{n}"].T
        lay[f"L1_xattn_{n}"] = a[f"L1_xattn_{n}"]
        lay[f"L1_attn_{n}"] = a[f"L1_attn_{n}"]
    lay["L0_xattn_bo"], lay["L1_xattn_bo"] = a["L0_xattn_bo"], a["L1_xattn_bo"]
    lay["L1_xattn_cols"] = np.stack([columns(a[f"L1_xattn_{n}"]) for n in ("bq", "bk", "bv")], axis=1)
    def grouped(w, biases):
        groups = w.shape[2]
        tiles = w.reshape(DC, P, 3, groups, P).transpose(3, 1, 2, 0, 4).reshape(groups, P, 3 * DC * P)
        cols = np.stack([v.reshape(groups, P) for v in biases], axis=2)
        return np.concatenate([tiles, cols], axis=2)

    no_bias = np.zeros(HID, np.float32)
    lay["L0_attn_w"] = grouped(a["L0_attn_qkv"].reshape(D, 3, 8, P),
                               [a["L0_attn_q_bias"].reshape(-1), no_bias, no_bias])
    pos = a["L0_attn_positional"].transpose(1, 2, 0)
    swapped = pos.reshape(16, 64, 32, 2)[..., ::-1].reshape(16, 64, 64)
    lay["L0_attn_pos"] = np.concatenate([pos, swapped], axis=2).reshape(8, P, P)
    lay["L0_attn_out_kernel"], lay["L0_attn_out_bias"] = a["L0_attn_out_kernel"], a["L0_attn_out_bias"]
    lay["w1_t"], lay["w2_t"] = a["L0_ffn_w1"].T, a["L0_ffn_w2"].T
    for n in ("ln1_g", "ln1_b", "ln2_g", "ln2_b", "b1", "b2"):
        lay[f"L0_ffn_{n}"] = a[f"L0_ffn_{n}"]
    lay["a1_gate"] = np.repeat(a["L1_attn_cg_W"], 16, axis=1)
    lay["am_w"] = np.repeat(a["L1_attn_am_W"], 16, axis=1)
    lay["am_b_cols"] = columns(np.repeat(a["L1_attn_am_b"], 16))
    lay["a1_cols"] = np.stack([columns(v) for v in (
        a["L1_attn_bq"], a["L1_attn_bk"], a["L1_attn_bv"], np.repeat(a["L1_attn_cg_b"], 16),
        a["L1_attn_ca_bout"], a["L1_attn_mc_bout"])], axis=1)
    lay["L1_attn_cons_vec"], lay["L1_attn_bo"] = a["L1_attn_cons_vec"], a["L1_attn_bo"]
    for n in ("ca", "mc"):
        lay[f"L1_attn_{n}_Wout"] = a[f"L1_attn_{n}_Wout"]
        lay[f"{n}_w"] = grouped(a[f"L1_attn_{n}_Win"].reshape(D, 3, DC, P), a[f"L1_attn_{n}_bin"].reshape(3, D))
    for n in ("Ws1", "Ws2", "W1", "W2", "Wr"):
        lay[f"L1_ffn_{n}"] = a[f"L1_ffn_{n}"]

    lay["identity"] = np.eye(P, dtype=np.float32)
    row = np.arange(P)
    lay["head_rows"] = np.where(row[:, None] // 16 == np.arange(8)[None], 0.25, 0).astype(np.float32)
    lay["half_rows"] = np.where(row[:, None] // 16 % 2 == np.arange(2)[None], 1, 0).astype(np.float32)
    place = np.arange(S)
    lay["causal"] = np.where(place[None, :] > (row % S)[:, None], -1.0e9, 0).astype(np.float32)
    freq = np.arange(S)
    angle = np.outer(2500.0 ** (-(freq // 2 * 2) / 64), place.astype(np.float64))
    sin, cos, even = np.sin(angle), np.cos(angle), (freq % 2 == 0)[:, None]
    key = np.where(even, sin, cos)
    query = np.concatenate([np.where(even, -cos, cos), sin]) * np.sqrt(2.0) / 8
    lay["pos_key"] = np.concatenate([key, key]).astype(np.float32)
    lay["pos_query"] = query.astype(np.float32)

    nc = bacc.Bacc("TRN2", target_bir_lowering=False, num_devices=1)
    arrays, dram = {}, {}
    for name, v in lay.items():
        v = np.ascontiguousarray(v)
        arrays[f"in_{name}"] = v
        dram[name] = nc.dram_tensor(f"in_{name}", v.shape, mybir.dt.from_np(v.dtype), kind="ExternalInput").ap()
    dram["out"] = nc.dram_tensor("out", (T, D), F32, kind="ExternalOutput").ap()
    perceiver(nc, dram, UPTO)
    r = run(nc, [arrays], core_ids=[0])
    return r.results[0]["out"].reshape(B, S, D)
```
